# Optimizing a Trainium2 kernel written in Bass

```python
import numpy as np
import jax
import jax.numpy as jnp

def _softmax(x, axis=-1):
    return jax.nn.softmax(x, axis=axis)

def _gelu(x):
    return jax.nn.gelu(x, approximate=True)

def _silu(x):
    return jax.nn.silu(x)

def _sigmoid(x):
    return jax.nn.sigmoid(x)

def _layernorm(x, axis=-1, eps=1e-05):
    m = jnp.mean(x, axis=axis, keepdims=True)
    v = jnp.var(x, axis=axis, keepdims=True)
    return (x - m) / jnp.sqrt(v + eps)

def _scatter_add(tgt, idx, src, axis=0):
    return tgt.at[idx].add(src)

def _segment_sum(src, seg, n):
    return jax.ops.segment_sum(src, seg, n)
kernel_name = 'mk_seq_preln_d2_jaxref_r4_ee9c2b'

def setup_inputs(seed: int=0):
    np.random.seed(seed)
    _w = jnp.asarray

    def _L0_attn_setup():
        import jax, jax.numpy as jnp
        import numpy as np
        import math
        N_HEAD = 16
        ATTN_THRESHOLD = -0.1
        EPS = 1e-06
        key = jax.random.key(seed)
        ks = jax.random.split(key, 5)
        B, T, C = (2, 512, 512)
        s = 1.0 / math.sqrt(C)
        return {'x': jax.random.normal(ks[0], (B, T, C), dtype=jnp.float32), 'Wq': jax.random.normal(ks[1], (C, C), dtype=jnp.float32) * s, 'Wk': jax.random.normal(ks[2], (C, C), dtype=jnp.float32) * s, 'Wv': jax.random.normal(ks[3], (C, C), dtype=jnp.float32) * s, 'Wo': jax.random.normal(ks[4], (C, C), dtype=jnp.float32) * s}
    _L0_attn_in = _L0_attn_setup()

    def _L0_ffn_setup():
        import jax, jax.numpy as jnp
        import numpy as np
        N_EXPERTS = 8
        TOP_K = 2
        C = 512
        H = 256
        HS = 512
        B, T = (1, 128)
        SCALE = 0.02
        key = jax.random.key(seed)
        ks = jax.random.split(key, 10)
        x = jax.random.normal(ks[0], (B, T, C), dtype=jnp.float32)
        gate_w = jax.random.normal(ks[1], (N_EXPERTS, C), dtype=jnp.float32) * SCALE
        w_gate = jax.random.normal(ks[2], (N_EXPERTS, H, C), dtype=jnp.float32) * SCALE
        w_up = jax.random.normal(ks[3], (N_EXPERTS, H, C), dtype=jnp.float32) * SCALE
        w_down = jax.random.normal(ks[4], (N_EXPERTS, C, H), dtype=jnp.float32) * SCALE
        sh_gate = jax.random.normal(ks[5], (HS, C), dtype=jnp.float32) * SCALE
        sh_up = jax.random.normal(ks[6], (HS, C), dtype=jnp.float32) * SCALE
        sh_down = jax.random.normal(ks[7], (C, HS), dtype=jnp.float32) * SCALE
        se_gate_w = jax.random.normal(ks[8], (1, C), dtype=jnp.float32) * SCALE
        return {'x': x, 'gate_w': gate_w, 'w_gate': w_gate, 'w_up': w_up, 'w_down': w_down, 'sh_gate': sh_gate, 'sh_up': sh_up, 'sh_down': sh_down, 'se_gate_w': se_gate_w}
    _L0_ffn_in = _L0_ffn_setup()

    def _L1_attn_setup():
        import jax, jax.numpy as jnp
        import numpy as np
        L, N, E, H = (512, 2, 512, 16)
        DH = E // H
        SCALE = DH ** (-0.5)
        key = jax.random.key(seed)
        k1, k2, k3 = jax.random.split(key, 3)
        x = jax.random.normal(k1, (L, N, E), dtype=jnp.float32)
        weight_qkv = jax.random.normal(k2, (3 * E, E), dtype=jnp.float32) * 0.02
        weight_out = jax.random.normal(k3, (E, E), dtype=jnp.float32) * 0.02
        return {'x': x, 'weight_qkv': weight_qkv, 'weight_out': weight_out}
    _L1_attn_in = _L1_attn_setup()

    def _L1_ffn_setup():
        import jax, jax.numpy as jnp
        import numpy as np
        E, K, H, F = (64, 6, 512, 192)
        G, KG = (8, 4)
        SHARED_F = 192
        SCALE = 2.5
        T = 2 * 256
        CAP = 2 * (T * K // E)

        def _grouped_topk(logits, bias):
            scores = jax.nn.sigmoid(logits.astype(jnp.float32))
            scores_b = scores + bias[None, :]
            gs = scores_b.reshape(-1, G, E // G)
            group_scores = jnp.sum(jax.lax.top_k(gs, 2)[0], axis=-1)
            gidx = jax.lax.top_k(group_scores, KG)[1]
            rows = jnp.arange(group_scores.shape[0])[:, None]
            group_mask = jnp.zeros_like(group_scores).at[rows, gidx].set(1.0)
            score_mask = jnp.repeat(group_mask, E // G, axis=-1) > 0
            tmp = jnp.where(score_mask, scores_b, -jnp.inf)
            topk_ids = jax.lax.top_k(tmp, K)[1]
            topk_w = jnp.take_along_axis(scores, topk_ids, axis=-1)
            topk_w = topk_w / jnp.sum(topk_w, axis=-1, keepdims=True)
            return (topk_w * SCALE, topk_ids)

        def _routed_moe(x, topk_w, topk_ids, w_gate, w_up, w_down):
            Tn = x.shape[0]
            flat_e = topk_ids.reshape(-1)
            order = jnp.argsort(flat_e)
            se = flat_e[order]
            pos = jnp.arange(Tn * K) - jnp.searchsorted(se, se, side='left')
            tok = order // K
            valid = pos < CAP
            slot = jnp.where(valid, pos, CAP)
            buf = jnp.zeros((E, CAP + 1, H), x.dtype).at[se, slot].set(x[tok])[:, :CAP]
            h = jax.nn.silu(jnp.einsum('ech,ehf->ecf', buf, w_gate)) * jnp.einsum('ech,ehf->ecf', buf, w_up)
            out = jnp.einsum('ecf,efh->ech', h, w_down)
            gathered = out[se, jnp.minimum(pos, CAP - 1)] * valid.astype(x.dtype)[:, None]
            w = topk_w.reshape(-1)[order].astype(x.dtype)[:, None]
            return jax.ops.segment_sum(gathered * w, tok, num_segments=Tn)
        key = jax.random.key(seed)
        ks = jax.random.split(key, 9)
        s = 0.02
        return dict(hidden_states=jax.random.normal(ks[0], (2, 256, H), jnp.float32), gate_w=jax.random.normal(ks[1], (H, E), jnp.float32) * s, bias=jax.random.normal(ks[2], (E,), jnp.float32) * s, w_gate=jax.random.normal(ks[3], (E, H, F), jnp.float32) * s, w_up=jax.random.normal(ks[4], (E, H, F), jnp.float32) * s, w_down=jax.random.normal(ks[5], (E, F, H), jnp.float32) * s, ws_gate=jax.random.normal(ks[6], (H, SHARED_F), jnp.float32) * s, ws_up=jax.random.normal(ks[7], (H, SHARED_F), jnp.float32) * s, ws_down=jax.random.normal(ks[8], (SHARED_F, H), jnp.float32) * s)
    _L1_ffn_in = _L1_ffn_setup()
    _d = {'L0_attn_x': _L0_attn_in['x'], 'L0_attn_Wq': _L0_attn_in['Wq'], 'L0_attn_Wk': _L0_attn_in['Wk'], 'L0_attn_Wv': _L0_attn_in['Wv'], 'L0_attn_Wo': _L0_attn_in['Wo'], 'L0_ffn_gate_w': _L0_ffn_in['gate_w'], 'L0_ffn_w_gate': _L0_ffn_in['w_gate'], 'L0_ffn_w_up': _L0_ffn_in['w_up'], 'L0_ffn_w_down': _L0_ffn_in['w_down'], 'L0_ffn_sh_gate': _L0_ffn_in['sh_gate'], 'L0_ffn_sh_up': _L0_ffn_in['sh_up'], 'L0_ffn_sh_down': _L0_ffn_in['sh_down'], 'L0_ffn_se_gate_w': _L0_ffn_in['se_gate_w'], 'L1_attn_weight_qkv': _L1_attn_in['weight_qkv'], 'L1_attn_weight_out': _L1_attn_in['weight_out'], 'L1_ffn_gate_w': _L1_ffn_in['gate_w'], 'L1_ffn_bias': _L1_ffn_in['bias'], 'L1_ffn_w_gate': _L1_ffn_in['w_gate'], 'L1_ffn_w_up': _L1_ffn_in['w_up'], 'L1_ffn_w_down': _L1_ffn_in['w_down'], 'L1_ffn_ws_gate': _L1_ffn_in['ws_gate'], 'L1_ffn_ws_up': _L1_ffn_in['ws_up'], 'L1_ffn_ws_down': _L1_ffn_in['ws_down']}
    _x0 = _d['L0_attn_x']
    _d['L0_attn_x'] = jax.random.normal(jax.random.fold_in(jax.random.key(seed), 1), (8, 512, 512), dtype=_x0.dtype)
    del _x0
    return _d

def reference(L0_attn_x, L0_attn_Wq, L0_attn_Wk, L0_attn_Wv, L0_attn_Wo, L0_ffn_gate_w, L0_ffn_w_gate, L0_ffn_w_up, L0_ffn_w_down, L0_ffn_sh_gate, L0_ffn_sh_up, L0_ffn_sh_down, L0_ffn_se_gate_w, L1_attn_weight_qkv, L1_attn_weight_out, L1_ffn_gate_w, L1_ffn_bias, L1_ffn_w_gate, L1_ffn_w_up, L1_ffn_w_down, L1_ffn_ws_gate, L1_ffn_ws_up, L1_ffn_ws_down):

    def _L0_attn_ref(x, Wq, Wk, Wv, Wo):
        import jax, jax.numpy as jnp
        import numpy as np
        import math
        N_HEAD = 16
        ATTN_THRESHOLD = -0.1
        EPS = 1e-06
        B, T, C = x.shape
        H = N_HEAD
        hd = C // H
        scale = 1.0 / math.sqrt(hd)

        def proj(W):
            return jnp.einsum('btc,oc->bto', x, W).reshape(B, T, H, hd).swapaxes(1, 2)
        q, k, v = (proj(Wq), proj(Wk), proj(Wv))
        scores = jnp.einsum('bhqd,bhkd->bhqk', q, k) * scale
        causal = jnp.tril(jnp.ones((T, T), dtype=bool))
        w = jnp.where(causal, jax.nn.relu(scores - ATTN_THRESHOLD), 0.0)
        w = w / (jnp.sum(w, axis=-1, keepdims=True) + EPS)
        out = jnp.einsum('bhqk,bhkd->bhqd', w, v)
        out = out.swapaxes(1, 2).reshape(B, T, C)
        return jnp.einsum('btc,oc->bto', out, Wo)

    def _L0_ffn_ref(x, gate_w, w_gate, w_up, w_down, sh_gate, sh_up, sh_down, se_gate_w):
        import jax, jax.numpy as jnp
        import numpy as np
        N_EXPERTS = 8
        TOP_K = 2
        C = 512
        H = 256
        HS = 512
        B, T = (1, 128)
        SCALE = 0.02
        Bb, Tt, Cc = x.shape
        xf = x.reshape(-1, Cc)
        scores = xf @ gate_w.T
        ew, ei = jax.lax.top_k(scores, TOP_K)
        ew = jax.nn.softmax(ew, axis=-1)
        x1 = jax.nn.silu(jnp.einsum('td,ehd->teh', xf, w_gate))
        x3 = jnp.einsum('td,ehd->teh', xf, w_up)
        expert_out = jnp.einsum('teh,edh->ted', x1 * x3, w_down)
        onehot = jax.nn.one_hot(ei, N_EXPERTS, dtype=ew.dtype)
        comb = jnp.einsum('ta,tae->te', ew, onehot)
        routed = jnp.einsum('te,ted->td', comb, expert_out)
        shared = jax.nn.silu(xf @ sh_gate.T) * (xf @ sh_up.T) @ sh_down.T
        sgate = jax.nn.sigmoid(xf @ se_gate_w.T)
        return (routed + sgate * shared).reshape(Bb, Tt, Cc)

    def _L1_attn_ref(x, weight_qkv, weight_out):
        import jax, jax.numpy as jnp
        import numpy as np
        L, N, E, H = (512, 2, 512, 16)
        DH = E // H
        SCALE = DH ** (-0.5)
        l, n, e = x.shape
        h, dh = (H, DH)
        qkv = jnp.einsum('lne,fe->lnf', x, weight_qkv)
        q, k, v = jnp.split(qkv, 3, axis=-1)
        q = q.reshape(l, n, h, dh) * jnp.asarray(SCALE, x.dtype)
        k = k.reshape(l, n, h, dh)
        v = v.reshape(l, n, h, dh)
        attn = jnp.einsum('lnhd,mnhd->nhlm', q, k)
        causal = jnp.tril(jnp.ones((l, l), dtype=bool))
        attn = jnp.where(causal, attn, jnp.asarray(-jnp.inf, attn.dtype))
        attn = jax.nn.softmax(attn, axis=-1)
        out = jnp.einsum('nhlm,mnhd->lnhd', attn, v).reshape(l, n, e)
        return jnp.einsum('lne,fe->lnf', out, weight_out)

    def _L1_ffn_ref(hidden_states, gate_w, bias, w_gate, w_up, w_down, ws_gate, ws_up, ws_down):
        import jax, jax.numpy as jnp
        import numpy as np
        E, K, H, F = (64, 6, 512, 192)
        G, KG = (8, 4)
        SHARED_F = 192
        SCALE = 2.5
        T = 2 * 256
        CAP = 2 * (T * K // E)

        def _grouped_topk(logits, bias):
            scores = jax.nn.sigmoid(logits.astype(jnp.float32))
            scores_b = scores + bias[None, :]
            gs = scores_b.reshape(-1, G, E // G)
            group_scores = jnp.sum(jax.lax.top_k(gs, 2)[0], axis=-1)
            gidx = jax.lax.top_k(group_scores, KG)[1]
            rows = jnp.arange(group_scores.shape[0])[:, None]
            group_mask = jnp.zeros_like(group_scores).at[rows, gidx].set(1.0)
            score_mask = jnp.repeat(group_mask, E // G, axis=-1) > 0
            tmp = jnp.where(score_mask, scores_b, -jnp.inf)
            topk_ids = jax.lax.top_k(tmp, K)[1]
            topk_w = jnp.take_along_axis(scores, topk_ids, axis=-1)
            topk_w = topk_w / jnp.sum(topk_w, axis=-1, keepdims=True)
            return (topk_w * SCALE, topk_ids)

        def _routed_moe(x, topk_w, topk_ids, w_gate, w_up, w_down):
            Tn = x.shape[0]
            flat_e = topk_ids.reshape(-1)
            order = jnp.argsort(flat_e)
            se = flat_e[order]
            pos = jnp.arange(Tn * K) - jnp.searchsorted(se, se, side='left')
            tok = order // K
            valid = pos < CAP
            slot = jnp.where(valid, pos, CAP)
            buf = jnp.zeros((E, CAP + 1, H), x.dtype).at[se, slot].set(x[tok])[:, :CAP]
            h = jax.nn.silu(jnp.einsum('ech,ehf->ecf', buf, w_gate)) * jnp.einsum('ech,ehf->ecf', buf, w_up)
            out = jnp.einsum('ecf,efh->ech', h, w_down)
            gathered = out[se, jnp.minimum(pos, CAP - 1)] * valid.astype(x.dtype)[:, None]
            w = topk_w.reshape(-1)[order].astype(x.dtype)[:, None]
            return jax.ops.segment_sum(gathered * w, tok, num_segments=Tn)
        orig_shape = hidden_states.shape
        x = hidden_states.reshape(-1, H)
        router_logits = x @ gate_w
        topk_w, topk_ids = _grouped_topk(router_logits, bias)
        y = _routed_moe(x, topk_w, topk_ids, w_gate, w_up, w_down)
        shared = jax.nn.silu(x @ ws_gate) * (x @ ws_up) @ ws_down
        return (y + shared).reshape(orig_shape)
    x = L0_attn_x
    x = x + _L0_attn_ref(_layernorm(x, axis=-1), L0_attn_Wq, L0_attn_Wk, L0_attn_Wv, L0_attn_Wo)
    x = x + _L0_ffn_ref(_layernorm(x, axis=-1), L0_ffn_gate_w, L0_ffn_w_gate, L0_ffn_w_up, L0_ffn_w_down, L0_ffn_sh_gate, L0_ffn_sh_up, L0_ffn_sh_down, L0_ffn_se_gate_w)
    x = x + _L1_attn_ref(_layernorm(x, axis=-1), L1_attn_weight_qkv, L1_attn_weight_out)
    x = x + _L1_ffn_ref(_layernorm(x, axis=-1), L1_ffn_gate_w, L1_ffn_bias, L1_ffn_w_gate, L1_ffn_w_up, L1_ffn_w_down, L1_ffn_ws_gate, L1_ffn_ws_up, L1_ffn_ws_down)
    return x

_drawn_inputs = setup_inputs


def setup_inputs(seed=0):
    import zlib

    import numpy as np

    out = dict(_drawn_inputs(seed))
    spreads = {}
    factors = {'L0_ffn_se_gate_w': 8.0,
     'L1_ffn_gate_w': 3.914,
     'L1_ffn_bias': 6.621,
     'L1_ffn_w_gate': 3.815,
     'L1_ffn_w_up': 3.727,
     'L1_ffn_w_down': 3.742}
    for name, (base, spread) in spreads.items():
        noise = np.random.default_rng([zlib.crc32(name.encode()), seed]).standard_normal(out[name].shape)
        drawn = base * np.exp(spread * noise) if base else spread * noise
        out[name] = jnp.asarray(drawn.astype(out[name].dtype))
    for name, factor in factors.items():
        out[name] = (out[name] * factor).astype(out[name].dtype)
    return out
```

```python
from contextlib import ExitStack

import concourse.bass as bass
from concourse import mybir

F32 = mybir.dt.float32
I32 = mybir.dt.int32
U32 = mybir.dt.uint32
ALU = mybir.AluOpType
ACT = mybir.ActivationFunctionType
AX = mybir.AxisListType

P = 128
C = 512
CC = C // P
TOKENS = 4096
TILES = TOKENS // P
LN_EPS = 1e-5

BATCHES = 8
SEQ = TOKENS // BATCHES
ST = SEQ // P
HEADS = 16
HD = C // HEADS
QUADS = HEADS // 4
ATTN_SCALE = float(HD) ** -0.5
ATTN_SHIFT = 0.1
ATTN_EPS = 1e-6


class Steps:

    def __init__(self, eng, sem, base=0):
        self.eng, self.sem, self.base, self.n = eng, sem, base, 0

    def mark(self, instruction):
        instruction.then_inc(self.sem, 1)
        self.n += 1

    def wait(self):
        self.eng.wait_ge(self.sem, self.base + self.n)


def constants(nc, ctx, ident, ones):
    set_up = ctx.enter_context(nc.semaphore("constants_set"))
    with nc.Block() as block:
        @block.gpsimd
        def _(pool):
            nc.gpsimd.memset(ident[:], 0.0).then_inc(set_up, 1)
            nc.gpsimd.memset(ones[:], 1.0).then_inc(set_up, 1)
            pool.wait_ge(set_up, 2)
            nc.gpsimd.affine_select(out=ident[:], in_=ident[:], compare_op=ALU.not_equal, fill=1.0, base=0,
                                    pattern=[[-1, P]], channel_multiplier=1)
            nc.gpsimd.affine_select(out=ones[:, P:2 * P], in_=ones[:, P:2 * P], compare_op=ALU.is_ge, fill=0.0,
                                    base=-1, pattern=[[1, P]], channel_multiplier=-1)


def layernorm_tiles(dve, steps, x_tile, stats, mean_var, n, carrier, one):
    for i in range(n):
        ins = dve.bn_stats(stats[:, i, :], x_tile(i))
    steps.mark(ins)
    steps.wait()
    dve.tensor_copy(carrier, one)
    for i in range(n):
        ins = dve.bn_aggr(mean_var[:, i, :], stats[:, i, :])
    return ins


def first_attention(nc, x_dram, wq, wk, wv, wo, X, ident, ones):
    with ExitStack() as ctx:
        sb = lambda name, shape: ctx.enter_context(nc.sbuf_tensor(name, shape, F32))
        sem = lambda name: ctx.enter_context(nc.semaphore(name))
        ps = lambda name, shape: ctx.enter_context(nc.psum_tensor(name, shape, F32))

        w_q, w_k, w_v, w_o = (sb(f"a_w{n}", [P, CC, C]) for n in "qkvo")
        stats = sb("a_stats", [P, ST, 6])
        mean_var = sb("a_mean_var", [P, ST, 2])
        std = sb("a_std", [P, ST])
        rstd = sb("a_rstd", [P, ST])
        eps = sb("a_eps", [P, 1])
        shift = sb("a_shift", [P, 1])
        carrier = sb("a_carrier", [P, 4])
        dve_carrier = sb("a_dve_carrier", [P, 1])
        xn = sb("a_xn", [P, ST, C])
        xnT = sb("a_xnT", [P, CC, SEQ])
        qT = sb("a_qT", [P, QUADS, SEQ])
        kT = sb("a_kT", [P, HEADS, SEQ])
        v = sb("a_v", [P, ST, C])
        w = sb("a_w", [P, 2, 4, SEQ])
        attnT = sb("a_attnT", [P, QUADS, SEQ])
        sums = sb("a_sums", [P, SEQ])

        pj = ps("a_pj", [P, 2, SEQ])
        sc = ps("a_sc", [P, 2, SEQ])
        num = ps("a_num", [P, 2, SEQ])
        den = ps("a_den", [P, 2, SEQ])

        x_loaded = sem("a_x_loaded")
        w_loaded = sem("a_w_loaded")
        zeroed = sem("a_zeroed")
        var_ready = sem("a_var_ready")
        std_ready = sem("a_std_ready")
        xn_ready = sem("a_xn_ready")
        pj_full = sem("a_pj_full")
        pj_taken = [sem("a_pj_taken0"), sem("a_pj_taken1")]
        sc_full = sem("a_sc_full")
        sc_taken = [sem("a_sc_taken0"), sem("a_sc_taken1")]
        w_masked = sem("a_w_masked")
        pv_done = sem("a_pv_done")
        attn_ready = sem("a_attn_ready")
        dve_steps = sem("a_dve_steps")

        T_PER = 20
        N_SC = QUADS * ST * 4
        N_STEP = QUADS * ST

        block = ctx.enter_context(nc.Block())

        @block.sync
        def _(sp):
            for b in range(BATCHES):
                if b >= 1:
                    sp.wait_ge(x_loaded, 16 * b)
                sp.dma_start(X[:, ST * b:ST * (b + 1), :],
                             x_dram.rearrange("(t p) c -> p t c", p=P)[:, ST * b:ST * (b + 1), :]).then_inc(x_loaded, 16)
                if b == 0:
                    for dst, src in ((w_q, wq), (w_k, wk), (w_v, wv), (w_o, wo)):
                        sp.dma_start(dst[:], src.rearrange("(c p) o -> p c o", p=P)).then_inc(w_loaded, 16)

        @block.gpsimd
        def _(pool):
            nc.gpsimd.memset(eps[:], LN_EPS).then_inc(zeroed, 1)
            nc.gpsimd.memset(shift[:], ATTN_SHIFT).then_inc(zeroed, 1)
            nc.gpsimd.memset(kT[:], 0.0).then_inc(zeroed, 1)

            def batch(b):
                for s in range(N_STEP):
                    half = (s * 4) // 2
                    kc = s % ST
                    pool.wait_ge(sc_taken[0], b * (N_SC // 2) + half + 2)
                    pool.wait_ge(sc_taken[1], b * (N_SC // 2) + half + 2)
                    nc.gpsimd.tensor_tensor(carrier[:, s % 4:s % 4 + 1], eps[:], eps[:], ALU.add)
                    diag = w[:, s % 2, :, P * kc:P * (kc + 1)]
                    nc.gpsimd.affine_select(out=diag, in_=diag, compare_op=ALU.is_ge, fill=0.0, base=0,
                                            pattern=[[0, 4], [1, P]], channel_multiplier=-1).then_inc(w_masked, 1)

            batch(0)
            with pool.Fori(1, BATCHES) as b:
                batch(b)

        @block.tensor
        def _(pe):
            def bank_free(n, b):
                pe.wait_ge(pj_taken[n % 2], b * (T_PER // 2) + ST // 2 + n // 2)

            def transposes(b, first):
                pe.wait_ge(xn_ready, b + 1)
                for c in range(CC):
                    n = -4 + c if first else 12 + c
                    if not first:
                        bank_free(n, b - 1)
                    elif c >= 2:
                        pe.wait_ge(pj_taken[c % 2], 1)
                    for i in range(ST):
                        ins = pe.transpose(pj[:, c % 2, P * i:P * (i + 1)], xn[:, i, P * c:P * (c + 1)], ident[:])
                    ins.then_inc(pj_full, 1)

            def project(u, b):
                bank_free(u, b)
                kind, j = divmod(u, 4)
                for c in range(CC):
                    if kind < 2:
                        ins = pe.matmul(pj[:, u % 2, :], (w_q, w_k)[kind][:, c, P * j:P * (j + 1)], xnT[:, c, :],
                                        start=(c == 0), stop=(c == CC - 1))
                    else:
                        ins = pe.matmul(pj[:, u % 2, :], xnT[:, c, P * j:P * (j + 1)], w_v[:, c, :],
                                        start=(c == 0), stop=(c == CC - 1))
                ins.then_inc(pj_full, 1)

            def scores(s, b):
                quad, kc = divmod(s, ST)
                for r in range(4):
                    m = 4 * s + r
                    pe.wait_ge(sc_taken[m % 2], b * (N_SC // 2) + m // 2)
                    pe.matmul(sc[:, m % 2, P * kc:SEQ], kT[:, 4 * quad + r, P * kc:P * (kc + 1)],
                              qT[:, quad, P * kc:SEQ], start=True, stop=True).then_inc(sc_full, 1)

            def weighted(s, b):
                quad, kc = divmod(s, ST)
                pe.wait_ge(w_masked, b * N_STEP + s + 1)
                if kc == 0 and quad >= 2:
                    pe.wait_ge(attn_ready, b * QUADS + quad - 1)
                for r in range(4):
                    h = 4 * quad + r
                    pe.matmul(num[32 * r:32 * r + 32, quad % 2, P * kc:SEQ], v[:, kc, HD * h:HD * (h + 1)],
                              w[:, s % 2, r, P * kc:SEQ], start=(kc == 0), stop=(kc == ST - 1), skip_group_check=True)
                for r in range(4):
                    ins = pe.matmul(den[32 * r:32 * r + 32, quad % 2, P * kc:SEQ], ones[:, 0:HD],
                                    w[:, s % 2, r, P * kc:SEQ], start=(kc == 0), stop=(kc == ST - 1),
                                    skip_group_check=True)
                ins.then_inc(pv_done, 1)

            def outputs(b, u):
                pe.wait_ge(attn_ready, (b + 1) * QUADS)
                for i in range(ST):
                    bank_free(u + i, b)
                    for c in range(QUADS):
                        ins = pe.matmul(pj[:, i % 2, :], attnT[:, c, P * i:P * (i + 1)], w_o[:, c, :],
                                        start=(c == 0), stop=(c == QUADS - 1))
                    ins.then_inc(pj_full, 1)

            def batch(b, last):
                for k in range(2):
                    pe.wait_ge(pj_taken[k], b * (T_PER // 2) + 2)
                for u in range(12):
                    project(u, b)
                for k in range(2):
                    pe.wait_ge(pj_taken[k], b * (T_PER // 2) + 8)
                for s in range(N_STEP + 1):
                    if s < N_STEP:
                        scores(s, b)
                    if s >= 1:
                        weighted(s - 1, b)
                if not last:
                    transposes(b + 1, False)
                outputs(b, 12 if last else 16)

            pe.wait_ge(w_loaded, 64)
            transposes(0, True)
            batch(0, False)
            with pe.Fori(1, BATCHES - 1) as b:
                batch(b, False)
            batch(BATCHES - 1, True)

        @block.scalar
        def _(act):
            def root(b):
                act.wait_ge(var_ready, b + 1)
                nc.scalar.activation(std[:], mean_var[:, :, 1], ACT.Sqrt, bias=eps[:]).then_inc(std_ready, 1)

            def take_xnT(b, c, n):
                act.wait_ge(pj_full, n)
                nc.scalar.copy(xnT[:, c, :], pj[:, c % 2, :]).then_inc(pj_taken[c % 2], 1)

            def batch(b, last):
                for u in range(0, 12, 2):
                    kind, j = divmod(u, 4)
                    act.wait_ge(pj_full, b * T_PER + 4 + u + 1)
                    if kind == 0:
                        nc.scalar.mul(qT[:, j, :], pj[:, 0, :], ATTN_SCALE).then_inc(pj_taken[0], 1)
                    elif kind == 1:
                        for r in range(4):
                            ins = nc.scalar.copy(kT[32 * r:32 * r + 32, 4 * j + r, :], pj[32 * r:32 * r + 32, 0, :])
                        ins.then_inc(pj_taken[0], 1)
                    else:
                        nc.scalar.copy(v[:, j, :], pj[:, 0, :]).then_inc(pj_taken[0], 1)
                if not last:
                    root(b + 1)
                for s in range(N_STEP):
                    kc = s % ST
                    if s < 2:
                        pass
                    else:
                        act.wait_ge(pv_done, b * N_STEP + s - 1)
                    for r in (0, 2):
                        act.wait_ge(sc_full, b * N_SC + 4 * s + r + 1)
                        nc.scalar.activation(w[:, s % 2, r, P * kc:SEQ], sc[:, 0, P * kc:SEQ], ACT.Relu,
                                             bias=shift[:]).then_inc(sc_taken[0], 1)
                if not last:
                    for c in (0, 2):
                        take_xnT(b + 1, c, b * T_PER + 4 + 12 + c + 1)

            act.wait_ge(zeroed, 3)
            root(0)
            for c in (0, 2):
                take_xnT(0, c, c + 1)
            batch(0, False)
            with act.Fori(1, BATCHES - 1) as b:
                batch(b, False)
            batch(BATCHES - 1, True)

        @block.vector
        def _(dve):
            def normalise(b, steps):
                dve.wait_ge(x_loaded, b * 16 + 16)
                layernorm_tiles(dve, steps, lambda i: X[:, bass.ds(b * ST + i, 1), :].rearrange("p t c -> p (t c)"), stats, mean_var, ST,
                                dve_carrier[:], eps[:])\
                    .then_inc(var_ready, 1)
                dve.wait_ge(std_ready, b + 1)
                steps.mark(dve.reciprocal(rstd[:], std[:]))
                steps.wait()
                for i in range(ST):
                    ins = dve.tensor_scalar(xn[:, i, :], X[:, bass.ds(b * ST + i, 1), :].rearrange("p t c -> p (t c)"),
                                            mean_var[:, i, 0:1], rstd[:, i:i + 1], ALU.subtract, ALU.mult)
                ins.then_inc(xn_ready, 1)

            def take_xnT(c, n):
                dve.wait_ge(pj_full, n)
                dve.tensor_copy(xnT[:, c, :], pj[:, 1, :]).then_inc(pj_taken[1], 1)

            def divide(quad, b, steps):
                dve.wait_ge(pv_done, b * N_STEP + ST * (quad + 1))
                steps.mark(dve.tensor_scalar(sums[:], den[:, quad % 2, :], ATTN_EPS, None, ALU.add))
                steps.wait()
                steps.mark(dve.reciprocal(sums[:], sums[:]))
                steps.wait()
                dve.tensor_tensor(attnT[:, quad, :], num[:, quad % 2, :], sums[:], ALU.mult).then_inc(attn_ready, 1)

            PER_TURN = 2 * QUADS + 2

            def batch(b, last):
                steps = Steps(dve, dve_steps, b * PER_TURN + 2)
                for u in range(1, 12, 2):
                    kind, j = divmod(u, 4)
                    dve.wait_ge(pj_full, b * T_PER + 4 + u + 1)
                    if kind == 0:
                        dve.tensor_scalar(qT[:, j, :], pj[:, 1, :], ATTN_SCALE, None, ALU.mult).then_inc(pj_taken[1], 1)
                    elif kind == 1:
                        for r in range(4):
                            ins = dve.tensor_copy(kT[32 * r:32 * r + 32, 4 * j + r, :], pj[32 * r:32 * r + 32, 1, :])
                        ins.then_inc(pj_taken[1], 1)
                    else:
                        dve.tensor_copy(v[:, j, :], pj[:, 1, :]).then_inc(pj_taken[1], 1)
                if not last:
                    normalise(b + 1, steps)
                for s in range(N_STEP):
                    quad, kc = divmod(s, ST)
                    if s >= 2:
                        dve.wait_ge(pv_done, b * N_STEP + s - 1)
                    for r in (1, 3):
                        dve.wait_ge(sc_full, b * N_SC + 4 * s + r + 1)
                        dve.tensor_scalar(w[:, s % 2, r, P * kc:SEQ], sc[:, 1, P * kc:SEQ], ATTN_SHIFT, 0.0,
                                          ALU.add, ALU.max).then_inc(sc_taken[1], 1)
                    if kc == 1 and quad >= 1:
                        divide(quad - 1, b, steps)
                divide(QUADS - 1, b, steps)
                if not last:
                    for c in (1, 3):
                        take_xnT(c, b * T_PER + 4 + 12 + c + 1)
                for i in range(ST):
                    dve.wait_ge(pj_full, b * T_PER + 4 + (12 if last else 16) + i + 1)
                    xt = X[:, bass.ds(b * ST + i, 1), :].rearrange("p t c -> p (t c)")
                    dve.tensor_tensor(xt, xt, pj[:, i % 2, :], ALU.add).then_inc(pj_taken[i % 2], 1)

            dve.wait_ge(zeroed, 3)
            normalise(0, Steps(dve, dve_steps))
            for c in (1, 3):
                take_xnT(c, c + 1)
            batch(0, False)
            with dve.Fori(1, BATCHES - 1) as b:
                batch(b, False)
            batch(BATCHES - 1, True)


E1 = 8
TOP1 = 2
H1 = 256
HC1 = H1 // P
HS1 = 512
HSC1 = HS1 // P
GROUP = 4
GROUPS = TILES // GROUP
MAX_TILES1 = (TOKENS * TOP1 + E1 * (P - 1)) // P
PAIRS1 = (MAX_TILES1 + 1) // 2
SLOTS1 = E1 * TOKENS + P * (2 * PAIRS1 - TOKENS * TOP1 // P)
ROWS = TOKENS + P


def tile_row(X, t):
    return X[:, bass.ds(t, 1), :].rearrange("p t c -> p (t c)")


def group_rows(x, g):
    return x.rearrange("(t p) c -> p t c", p=P)[:, GROUP * g:GROUP * (g + 1), :]


def first_ffn_shared(nc, X, ident, ones, before, gate_w, sh_gate, sh_up, sh_down, w_gate, w_up, w13, xs, table,
                     weight_all, slot_all, tile_expert, tile_slot):
    with ExitStack() as ctx:
        sb = lambda name, shape, dt=F32: ctx.enter_context(nc.sbuf_tensor(name, shape, dt))
        sem = lambda name: ctx.enter_context(nc.semaphore(name))
        ps = lambda name, shape: ctx.enter_context(nc.psum_tensor(name, shape, F32))

        w_g = sb("b_wg", [P, CC, HS1])
        w_u = sb("b_wu", [P, CC, HS1])
        w_d = sb("b_wd", [P, HSC1, C])
        w_route = sb("b_wroute", [P, CC, E1 + 1])
        eps = sb("b_eps", [P, 1])
        carrier = sb("b_carrier", [P, 8])
        empty = sb("b_empty", [P, SLOTS1 // P], U32)
        zrow = sb("b_zrow", [P, C])
        expert_iota = sb("b_expert_iota", [P, E1])
        region = sb("b_region", [P, E1])
        token_id = sb("b_token_id", [P, TILES])
        stats = sb("b_stats", [P, GROUP, 6])
        mean_var = sb("b_mean_var", [P, GROUP, 2])
        std = sb("b_std", [P, GROUP])
        rstd = sb("b_rstd", [P, GROUP])
        xn = sb("b_xn", [P, GROUP, C])
        xnT = sb("b_xnT", [P, CC, GROUP * P])
        hT = sb("b_hT", [P, HSC1, GROUP * P])
        sil = sb("b_sil", [P, 2, GROUP * P])
        logits = sb("b_logits", [P, GROUP, E1 + 1])
        best = sb("b_best", [P, GROUP, 8])
        best_i = sb("b_best_i", [P, GROUP, 8], U32)
        best_f = sb("b_best_f", [P, GROUP, TOP1])
        gap = sb("b_gap", [P, GROUP, 3])
        gates = sb("b_gates", [P, GROUP, 3])
        onehot = sb("b_onehot", [P, GROUP, TOP1, E1])
        chosen = sb("b_chosen", [P, GROUP, E1])
        total = sb("b_total", [P, E1])
        base = sb("b_base", [P, E1])
        place = sb("b_place", [P, GROUP, E1])
        picked = sb("b_picked", [P, GROUP, TOP1, E1])
        slot_f = sb("b_slot_f", [P, GROUP, TOP1])
        slot_now = sb("b_slot_now", [P, GROUP, TOP1], U32)
        token_now = sb("b_token_now", [P, GROUP], U32)
        n_tiles = sb("b_n_tiles", [P, E1])
        n_tiles_i = sb("b_n_tiles_i", [P, E1], I32)
        tiles_before = sb("b_tiles_before", [P, E1])
        tile_iota = sb("b_tile_iota", [P, 2 * PAIRS1])
        past = sb("b_past", [P, 2 * PAIRS1])
        t_expert = sb("b_t_expert", [P, 2 * PAIRS1])
        t_start = sb("b_t_start", [P, 2 * PAIRS1])
        expert_all = sb("b_expert_all", [P, TILES, TOP1])
        slot_all_f = sb("b_slot_all_f", [P, TILES, TOP1])
        shift = sb("b_shift", [P, E1])
        moved = sb("b_moved", [P, TILES, TOP1])

        up = ps("b_up", [P, 4, GROUP * P])
        pj = ps("b_pj", [P, 2, C])
        lg = ps("b_lg", [P, GROUP, E1 + 1])
        cnt = ps("b_cnt", [P, GROUP + 1, E1])

        w_loaded = sem("b_w_loaded")
        set_up = sem("b_set_up")
        rows_zeroed = sem("b_rows_zeroed")
        var_ready = sem("b_var_ready")
        std_ready = sem("b_std_ready")
        xn_ready = sem("b_xn_ready")
        xn_stored = sem("b_xn_stored")
        pj_full = sem("b_pj_full")
        pj_taken = [sem("b_pj_taken0"), sem("b_pj_taken1")]
        lg_full = sem("b_lg_full")
        gap_ready = sem("b_gap_ready")
        gates_ready = sem("b_gates_ready")
        chosen_ready = sem("b_chosen_ready")
        cnt_full = sem("b_cnt_full")
        up_full = sem("b_up_full")
        sil_ready = sem("b_sil_ready")
        h_ready = sem("b_h_ready")
        slots_ready = sem("b_slots_ready")
        scattered = sem("b_scattered")
        steps_sem = sem("b_steps")
        carried = sem("b_carried")
        SET_UP = 8

        block = ctx.enter_context(nc.Block())

        @block.sync
        def _(sp):
            sp.dma_start(w_route[:], gate_w.rearrange("(c p) e -> p c e", p=P)).then_inc(w_loaded, 16)
            for dst, src in ((w_g, sh_gate), (w_u, sh_up), (w_d, sh_down)):
                sp.dma_start(dst[:], src.rearrange("(c p) o -> p c o", p=P)).then_inc(w_loaded, 16)
            sp.wait_ge(set_up, SET_UP)
            sp.dma_start(table.rearrange("(p s) one -> p (s one)", p=P), empty[:]).then_inc(rows_zeroed, 16)
            sp.dma_start(xs[TOKENS:ROWS, :], zrow[:]).then_inc(rows_zeroed, 16)
            for e in range(E1):
                for k, src in enumerate((w_gate, w_up)):
                    sp.dma_start(w13[:, CC * e:CC * (e + 1), H1 * k:H1 * (k + 1)],
                                 src[e].rearrange("(c p) f -> p c f", p=P)).then_inc(before, 16)
            for g in range(GROUPS):
                sp.wait_ge(xn_ready, g + 1)
                sp.dma_start(group_rows(xs[0:TOKENS, :], g), xn[:]).then_inc(xn_stored, 16)
            sp.wait_ge(xn_stored, 16 * GROUPS)
            sp.wait_ge(rows_zeroed, 32)

        @block.gpsimd
        def _(pool):
            nc.gpsimd.memset(eps[:], LN_EPS).then_inc(set_up, 1)
            nc.gpsimd.memset(total[:], 0.0).then_inc(set_up, 1)
            nc.gpsimd.memset(zrow[:], 0.0).then_inc(set_up, 1)
            nc.gpsimd.iota(empty[:], [[0, SLOTS1 // P]], base=TOKENS, channel_multiplier=0).then_inc(set_up, 1)
            nc.gpsimd.iota(expert_iota[:], [[1, E1]], base=0, channel_multiplier=0,
                           allow_small_or_imprecise_dtypes=True).then_inc(set_up, 1)
            nc.gpsimd.iota(region[:], [[TOKENS, E1]], base=0, channel_multiplier=0,
                           allow_small_or_imprecise_dtypes=True).then_inc(set_up, 1)
            nc.gpsimd.iota(token_id[:], [[P, TILES]], base=0, channel_multiplier=1,
                           allow_small_or_imprecise_dtypes=True).then_inc(set_up, 1)
            nc.gpsimd.iota(tile_iota[:], [[1, 2 * PAIRS1]], base=0, channel_multiplier=0,
                           allow_small_or_imprecise_dtypes=True).then_inc(set_up, 1)
            pool.wait_ge(rows_zeroed, 32)
            pool.wait_ge(set_up, SET_UP)

            def turn(g):
                pool.wait_ge(slots_ready, g + 1)
                pool.wait_ge(carried, g)
                nc.gpsimd.tensor_tensor(carrier[:, 0:1], eps[:], eps[:], ALU.add).then_inc(carried, 1)
                for i in range(GROUP):
                    for k in range(TOP1):
                        nc.gpsimd.indirect_dma_start(
                            table, bass.IndirectOffsetOnAxis(ap=slot_now[:, i, k:k + 1], axis=0),
                            token_now[:, i:i + 1], None).then_inc(scattered, 16)

            turn(0)
            with pool.Fori(1, GROUPS) as g:
                turn(g)
            pool.wait_ge(scattered, 16 * GROUPS * GROUP * TOP1)

        PJ = 8

        @block.tensor
        def _(pe):
            def bank_free(u, g):
                pe.wait_ge(pj_taken[u % 2], g * (PJ // 2) + 2 + u // 2)

            def transposes(g, first):
                pe.wait_ge(xn_ready, g + 1)
                for c in range(CC):
                    if not first:
                        bank_free(c, g - 1)
                    elif c >= 2:
                        pe.wait_ge(pj_taken[c % 2], 1)
                    for i in range(GROUP):
                        ins = pe.transpose(pj[:, c % 2, P * i:P * (i + 1)], xn[:, i, P * c:P * (c + 1)], ident[:])
                    ins.then_inc(pj_full, 1)

            def group(g, last):
                for k in range(2):
                    pe.wait_ge(pj_taken[k], g * (PJ // 2) + 2)
                pe.wait_ge(chosen_ready, g)
                for i in range(GROUP):
                    for c in range(CC):
                        ins = pe.matmul(lg[:, i, :], xnT[:, c, P * i:P * (i + 1)], w_route[:, c, :],
                                        start=(c == 0), stop=(c == CC - 1))
                ins.then_inc(lg_full, 1)
                for f in range(HSC1):
                    pe.wait_ge(h_ready, g * HSC1 + f - 1) if f >= 1 else pe.wait_ge(h_ready, g * HSC1)
                    for k, w in ((0, w_g), (1, w_u)):
                        for c in range(CC):
                            ins = pe.matmul(up[:, 2 * (f % 2) + k, :], w[:, c, P * f:P * (f + 1)], xnT[:, c, :],
                                            start=(c == 0), stop=(c == CC - 1))
                    ins.then_inc(up_full, 1)
                pe.wait_ge(chosen_ready, g + 1)
                pe.wait_ge(slots_ready, g)
                for i in range(GROUP + 1):
                    for j in range(min(i + 1, GROUP)):
                        ins = pe.matmul(cnt[:, i, :], ones[:, P:2 * P] if j == i else ones[:, 0:P], chosen[:, j, :],
                                        start=(j == 0), stop=(j == min(i, GROUP - 1)))
                ins.then_inc(cnt_full, 1)
                if not last:
                    transposes(g + 1, False)
                pe.wait_ge(h_ready, (g + 1) * HSC1)
                for i in range(GROUP):
                    bank_free((0 if last else 4) + i, g)
                    for f in range(HSC1):
                        ins = pe.matmul(pj[:, i % 2, :], hT[:, f, P * i:P * (i + 1)], w_d[:, f, :],
                                        start=(f == 0), stop=(f == HSC1 - 1))
                    ins.then_inc(pj_full, 1)

            pe.wait_ge(w_loaded, 64)
            transposes(0, True)
            group(0, False)
            with pe.Fori(1, GROUPS - 1) as g:
                group(g, False)
            group(GROUPS - 1, True)

        @block.scalar
        def _(act):
            def root(g):
                act.wait_ge(var_ready, g + 1)
                nc.scalar.activation(std[:], mean_var[:, :, 1], ACT.Sqrt, bias=eps[:]).then_inc(std_ready, 1)

            def take_xnT(c, n):
                act.wait_ge(pj_full, n)
                nc.scalar.copy(xnT[:, c, :], pj[:, c % 2, :]).then_inc(pj_taken[c % 2], 1)

            def group(g, last):
                act.wait_ge(gap_ready, g + 1)
                nc.scalar.activation(gates[:], gap[:], ACT.Sigmoid).then_inc(gates_ready, 1)
                for f in range(HSC1):
                    act.wait_ge(up_full, g * HSC1 + f + 1)
                    act.wait_ge(h_ready, g * HSC1 + f - 1) if f >= 1 else act.wait_ge(h_ready, g * HSC1)
                    nc.scalar.activation(sil[:, f % 2, :], up[:, 2 * (f % 2), :], ACT.Silu).then_inc(sil_ready, 1)
                if not last:
                    root(g + 1)
                    for c in (0, 2):
                        take_xnT(c, g * PJ + 4 + c + 1)

            act.wait_ge(set_up, SET_UP)
            root(0)
            for c in (0, 2):
                take_xnT(c, c + 1)
            group(0, False)
            with act.Fori(1, GROUPS - 1) as g:
                group(g, False)
            group(GROUPS - 1, True)

        @block.vector
        def _(dve):
            def normalise(g, steps, first):
                layernorm_tiles(dve, steps, lambda i: tile_row(X, g * GROUP + i), stats, mean_var, GROUP,
                                carrier[:, 4:5], eps[:]).then_inc(var_ready, 1)
                dve.wait_ge(std_ready, g + 1)
                steps.mark(dve.reciprocal(rstd[:], std[:]))
                steps.wait()
                if not first:
                    dve.wait_ge(xn_stored, g * 16)
                for i in range(GROUP):
                    ins = dve.tensor_scalar(xn[:, i, :], tile_row(X, g * GROUP + i),
                                            mean_var[:, i, 0:1], rstd[:, i:i + 1], ALU.subtract, ALU.mult)
                ins.then_inc(xn_ready, 1)

            def take_xnT(c, n):
                dve.wait_ge(pj_full, n)
                dve.tensor_copy(xnT[:, c, :], pj[:, 1, :]).then_inc(pj_taken[1], 1)

            def choose(g, steps):
                dve.wait_ge(lg_full, g + 1)
                steps.mark(dve.tensor_copy(logits[:], lg[:]))
                steps.wait()
                dve.tensor_copy(carrier[:, 5:6], eps[:])
                for i in range(GROUP):
                    ins = dve.max(best[:, i, :], logits[:, i, 0:E1])
                steps.mark(ins)
                steps.wait()
                dve.tensor_copy(carrier[:, 6:7], eps[:])
                for i in range(GROUP):
                    ins = dve.max_index(best_i[:, i, :], best[:, i, :], logits[:, i, 0:E1])
                steps.mark(ins)
                dve.tensor_tensor(gap[:, :, 0], best[:, :, 0], best[:, :, 1], ALU.subtract)
                dve.tensor_tensor(gap[:, :, 1], best[:, :, 1], best[:, :, 0], ALU.subtract)
                dve.tensor_copy(gap[:, :, 2], logits[:, :, E1]).then_inc(gap_ready, 1)
                steps.wait()
                steps.mark(dve.tensor_copy(best_f[:], best_i[:, :, 0:TOP1]))
                steps.wait()
                for k in range(TOP1):
                    ins = dve.tensor_tensor(onehot[:, :, k, :], expert_iota[:].unsqueeze(1).broadcast_to([P, GROUP, E1]),
                                            best_f[:, :, k:k + 1].broadcast_to([P, GROUP, E1]), ALU.is_equal)
                steps.mark(ins)
                steps.wait()
                dve.tensor_tensor(chosen[:], onehot[:, :, 0, :], onehot[:, :, 1, :], ALU.add).then_inc(chosen_ready, 1)

            def place_slots(g, steps):
                steps.mark(dve.tensor_tensor(base[:], total[:], region[:], ALU.add))
                dve.wait_ge(cnt_full, g + 1)
                steps.wait()
                steps.mark(dve.tensor_tensor(place[:], cnt[:, 0:GROUP, :],
                                             base[:].unsqueeze(1).broadcast_to([P, GROUP, E1]), ALU.add))
                steps.mark(dve.tensor_tensor(total[:], total[:], cnt[:, GROUP, :], ALU.add))
                steps.wait()
                for k in range(TOP1):
                    ins = dve.tensor_tensor(picked[:, :, k, :], onehot[:, :, k, :], place[:], ALU.mult)
                steps.mark(ins)
                steps.wait()
                steps.mark(dve.tensor_reduce(slot_f[:], picked[:], AX.X, ALU.add))
                steps.wait()
                dve.wait_ge(scattered, g * (16 * GROUP * TOP1))
                dve.tensor_copy(token_now[:], token_id[:, bass.ds(g * GROUP, GROUP)])
                dve.tensor_copy(slot_all_f[:, bass.ds(g * GROUP, GROUP), :], slot_f[:])
                dve.tensor_copy(expert_all[:, bass.ds(g * GROUP, GROUP), :], best_f[:])
                dve.tensor_copy(slot_now[:], slot_f[:]).then_inc(slots_ready, 1)
                dve.wait_ge(gates_ready, g + 1)
                steps.mark(dve.tensor_copy(weight_all[:, bass.ds(g * GROUP, GROUP), :], gates[:, :, 0:TOP1]))

            PER_TURN = 13

            def group(g, last):
                steps = Steps(dve, steps_sem, g * PER_TURN + 2)
                choose(g, steps)
                for f in range(HSC1):
                    dve.wait_ge(sil_ready, g * HSC1 + f + 1)
                    dve.tensor_tensor(hT[:, f, :], sil[:, f % 2, :], up[:, 2 * (f % 2) + 1, :], ALU.mult)\
                        .then_inc(h_ready, 1)
                if not last:
                    normalise(g + 1, steps, False)
                place_slots(g, steps)
                assert steps.n == PER_TURN - (2 if last else 0), steps.n
                if not last:
                    for c in (1, 3):
                        take_xnT(c, g * PJ + 4 + c + 1)
                for i in range(GROUP):
                    dve.wait_ge(pj_full, g * PJ + 4 + (0 if last else 4) + i + 1)
                    dve.scalar_tensor_tensor(out=tile_row(X, g * GROUP + i), in0=pj[:, i % 2, :],
                                             scalar=gates[:, i, 2:3], in1=tile_row(X, g * GROUP + i),
                                             op0=ALU.mult, op1=ALU.add).then_inc(pj_taken[i % 2], 1)
                return steps

            dve.wait_ge(set_up, SET_UP)
            normalise(0, Steps(dve, steps_sem), True)
            for c in (1, 3):
                take_xnT(c, c + 1)
            group(0, False)
            with dve.Fori(1, GROUPS - 1) as g:
                group(g, False)
            steps = group(GROUPS - 1, True)

            steps.mark(dve.tensor_scalar(n_tiles[:], total[:], float(P - 1), None, ALU.add))
            steps.wait()
            steps.mark(dve.tensor_copy(n_tiles_i[:], n_tiles[:]))
            steps.wait()
            steps.mark(dve.tensor_scalar(n_tiles_i[:], n_tiles_i[:], P.bit_length() - 1, None, ALU.arith_shift_right))
            steps.wait()
            steps.mark(dve.tensor_copy(n_tiles[:], n_tiles_i[:]))
            steps.wait()
            steps.mark(dve.tensor_copy(tiles_before[:, 0:1], n_tiles[:, 0:1]))
            for e in range(1, E1):
                steps.wait()
                steps.mark(dve.tensor_tensor(tiles_before[:, e:e + 1], tiles_before[:, e - 1:e], n_tiles[:, e:e + 1],
                                             ALU.add))
            steps.mark(dve.memset(t_expert[:], 0.0))
            steps.mark(dve.tensor_copy(t_start[:], tile_iota[:]))
            for e in range(E1):
                steps.wait()
                steps.mark(dve.tensor_scalar(past[:], tile_iota[:], tiles_before[:, e:e + 1], None, ALU.is_ge))
                steps.wait()
                steps.mark(dve.tensor_tensor(t_expert[:], t_expert[:], past[:], ALU.add))
                steps.mark(dve.tensor_scalar(past[:], past[:], n_tiles[:, e:e + 1], None, ALU.mult))
                steps.wait()
                steps.mark(dve.tensor_tensor(t_start[:], t_start[:], past[:], ALU.subtract))
            steps.wait()
            steps.mark(dve.tensor_scalar(past[:], t_expert[:], float(TOKENS // P), None, ALU.mult))
            steps.wait()
            steps.mark(dve.tensor_tensor(t_start[:], t_start[:], past[:], ALU.add))
            steps.wait()
            steps.mark(dve.tensor_scalar(t_start[:], t_start[:], float(P), None, ALU.mult))
            steps.mark(dve.tensor_scalar(t_expert[:], t_expert[:], float(E1 - 1), None, ALU.min))
            steps.wait()
            dve.tensor_copy(tile_slot[:], t_start[:])
            dve.tensor_copy(tile_expert[:], t_expert[:])

            steps.mark(dve.tensor_tensor(shift[:], tiles_before[:], n_tiles[:], ALU.subtract))
            steps.wait()
            steps.mark(dve.tensor_scalar(shift[:], shift[:], float(P), None, ALU.mult))
            steps.wait()
            steps.mark(dve.tensor_tensor(shift[:], shift[:], region[:], ALU.subtract))
            for e in range(E1):
                steps.wait()
                steps.mark(dve.tensor_scalar(moved[:], expert_all[:], float(e), shift[:, e:e + 1],
                                             ALU.is_equal, ALU.mult))
                steps.wait()
                steps.mark(dve.tensor_tensor(slot_all_f[:], slot_all_f[:], moved[:], ALU.add))
            steps.wait()
            dve.tensor_copy(slot_all[:], slot_all_f[:])


def first_ffn_experts(nc, ident, w13, w13_loaded, w2, w_down, xs, table, ys, tile_expert, tile_slot):
    with ExitStack() as ctx:
        sb = lambda name, shape, dt=F32: ctx.enter_context(nc.sbuf_tensor(name, shape, dt))
        sem = lambda name: ctx.enter_context(nc.semaphore(name))
        ps = lambda name, shape: ctx.enter_context(nc.psum_tensor(name, shape, F32))

        ids = sb("c_ids", [P, 2, 1], U32)
        xg = sb("c_xg", [P, 2, C])
        xgT = sb("c_xgT", [P, 2, CC * P])
        sil = sb("c_sil", [P, 2, H1])
        h = sb("c_h", [P, 2, H1])
        hT = sb("c_hT", [P, 2, HC1 * P])
        y = sb("c_y", [P, 2, C])
        carrier = sb("c_carrier", [P, 2])

        up = ps("c_up", [P, 2, 2 * H1])
        yp = ps("c_yp", [P, 2, C])
        xp = ps("c_xp", [P, 2, CC * P])
        hp = ps("c_hp", [P, 2, 512])

        w2_loaded = sem("c_w2_loaded")
        ids_loaded = [sem("c_ids_loaded0"), sem("c_ids_loaded1")]
        gathered = [sem("c_gathered0"), sem("c_gathered1")]
        stored = [sem("c_stored0"), sem("c_stored1")]
        x_turned = sem("c_x_turned")
        xgT_ready = sem("c_xgT_ready")
        up_full = sem("c_up_full")
        sil_ready = sem("c_sil_ready")
        h_ready = sem("c_h_ready")
        h_turned = sem("c_h_turned")
        hT_ready = sem("c_hT_ready")
        y_full = sem("c_y_full")
        y_ready = sem("c_y_ready")
        carried = sem("c_carried")
        N = 2 * PAIRS1

        def turns(eng, tile):
            for p in range(2):
                tile(0, p, "first")
            for p in range(2):
                tile(1, p, "")
            with eng.Fori(2, PAIRS1 - 1) as ii:
                for p in range(2):
                    tile(ii, p, "")
            for p in range(2):
                tile(PAIRS1 - 1, p, "last")

        block = ctx.enter_context(nc.Block())

        @block.sync
        def _(sp):
            for e in range(E1):
                sp.dma_start(w2[:, HC1 * e:HC1 * (e + 1), :],
                             w_down[e].rearrange("(c p) o -> p c o", p=P)).then_inc(w2_loaded, 16)

        @block.gpsimd
        def _(pool):
            def load_ids(ii, p, start):
                slot = pool.value_load(tile_slot[0:1, bass.ds(ii * 2 + p, 1)], min_val=0, max_val=SLOTS1 - P)
                if not start:
                    pool.wait_ge(gathered[p], ii * 16)
                pool.dma_start(ids[:, p, :], table[bass.ds(slot, P), :]).then_inc(ids_loaded[p], 16)

            def tile(ii, p, which):
                if not (which == "last" and p == 1):
                    load_ids(ii + 1 if p else ii, 1 - p, which == "first" and p == 0)
                pool.wait_ge(ids_loaded[p], ii * 16 + 16)
                if which != "first":
                    pool.wait_ge(x_turned, ii * 2 + p - 1)
                pool.wait_ge(carried, ii * 2 + p)
                nc.gpsimd.tensor_tensor(carrier[:, 0:1], ident[:, 0:1], ident[:, 0:1], ALU.add).then_inc(carried, 1)
                nc.gpsimd.indirect_dma_start(xg[:, p, :], None, xs,
                                             bass.IndirectOffsetOnAxis(ap=ids[:, p, :], axis=0)).then_inc(gathered[p], 16)

            load_ids(0, 0, True)
            turns(pool, tile)

        @block.tensor
        def _(pe):
            def turn_x(ii, p, start):
                pe.wait_ge(gathered[p], ii * 16 + 16)
                if not start:
                    pe.wait_ge(xgT_ready, ii * 2 + p - 1)
                for c in range(CC):
                    ins = pe.transpose(xp[:, p, P * c:P * (c + 1)], xg[:, p, P * c:P * (c + 1)], ident[:])
                ins.then_inc(x_turned, 1)

            def down(ii, p, start):
                e = pe.value_load(tile_expert[0:1, bass.ds(ii * 2 + p, 1)], min_val=0, max_val=E1 - 1)
                pe.wait_ge(hT_ready, ii * 2 + p + 1)
                if not start:
                    pe.wait_ge(y_ready, ii * 2 + p - 1)
                for f in range(HC1):
                    ins = pe.matmul(yp[:, p, :], hT[:, p, P * f:P * (f + 1)],
                                    w2[:, bass.ds(e * HC1 + f, 1), :].rearrange("p a c -> p (a c)"),
                                    start=(f == 0), stop=(f == HC1 - 1))
                ins.then_inc(y_full, 1)

            def tile(ii, p, which):
                e = pe.value_load(tile_expert[0:1, bass.ds(ii * 2 + p, 1)], min_val=0, max_val=E1 - 1)
                pe.wait_ge(xgT_ready, ii * 2 + p + 1)
                if which != "first":
                    pe.wait_ge(h_ready, ii * 2 + p - 1)
                for c in range(CC):
                    ins = pe.matmul(up[:, p, :], xgT[:, p, P * c:P * (c + 1)],
                                    w13[:, bass.ds(e * CC + c, 1), :].rearrange("p a f -> p (a f)"),
                                    start=(c == 0), stop=(c == CC - 1))
                ins.then_inc(up_full, 1)
                if not (which == "first" and p == 0):
                    down(ii if p else ii - 1, 1 - p, which == "first")
                if not (which == "last" and p == 1):
                    turn_x(ii + 1 if p else ii, 1 - p, which == "first" and p == 0)
                pe.wait_ge(h_ready, ii * 2 + p + 1)
                if which != "first":
                    pe.wait_ge(hT_ready, ii * 2 + p - 1)
                for f in range(HC1):
                    ins = pe.transpose(hp[:, p, P * f:P * (f + 1)], h[:, p, P * f:P * (f + 1)], ident[:])
                ins.then_inc(h_turned, 1)

            pe.wait_ge(w13_loaded, 16 * 2 * E1)
            pe.wait_ge(w2_loaded, 16 * E1)
            turn_x(0, 0, True)
            turns(pe, tile)
            down(PAIRS1 - 1, 1, False)

        @block.scalar
        def _(act):
            def take_x(ii, p, start):
                act.wait_ge(x_turned, ii * 2 + p + 1)
                if not start:
                    act.wait_ge(up_full, ii * 2 + p - 1)
                nc.scalar.copy(xgT[:, p, :], xp[:, p, :]).then_inc(xgT_ready, 1)

            def store(ii, p):
                act.wait_ge(y_ready, ii * 2 + p + 1)
                act.dma_start(ys[bass.ds(ii * (2 * P) + p * P, P), :], y[:, p, :]).then_inc(stored[p], 16)

            def tile(ii, p, which):
                act.wait_ge(up_full, ii * 2 + p + 1)
                if which != "first":
                    act.wait_ge(h_ready, ii * 2 + p - 1)
                nc.scalar.activation(sil[:, p, :], up[:, p, 0:H1], ACT.Silu).then_inc(sil_ready, 1)
                if not (which == "last" and p == 1):
                    take_x(ii + 1 if p else ii, 1 - p, which == "first" and p == 0)

                if which != "first":
                    store(ii - 1, p)

            take_x(0, 0, True)
            turns(act, tile)
            for p in range(2):
                store(PAIRS1 - 1, p)
            for p in range(2):
                act.wait_ge(stored[p], 16 * PAIRS1)

        @block.vector
        def _(dve):
            def take_y(ii, p, start):
                dve.wait_ge(y_full, ii * 2 + p + 1)
                if not start:
                    dve.wait_ge(stored[p], ii * 16)
                dve.tensor_copy(y[:, p, :], yp[:, p, :]).then_inc(y_ready, 1)

            def tile(ii, p, which):
                dve.wait_ge(sil_ready, ii * 2 + p + 1)
                if which != "first":
                    dve.wait_ge(h_turned, ii * 2 + p - 1)
                dve.tensor_tensor(h[:, p, :], sil[:, p, :], up[:, p, H1:2 * H1], ALU.mult).then_inc(h_ready, 1)
                if not (which == "first" and p == 0):
                    take_y(ii if p else ii - 1, 1 - p, which == "first")
                dve.wait_ge(h_turned, ii * 2 + p + 1)
                if which != "first":
                    dve.wait_ge(y_full, ii * 2 + p - 1)
                dve.tensor_copy(hT[:, p, :], hp[:, p, 0:HC1 * P]).then_inc(hT_ready, 1)

            turns(dve, tile)
            take_y(PAIRS1 - 1, 1, False)


POS = 8
CHUNKS = TILES // POS


def second_attention(nc, X, ident, ones, ys, slot_all, weight_all, w_qkv, w_out):
    with ExitStack() as ctx:
        sb = lambda name, shape, dt=F32: ctx.enter_context(nc.sbuf_tensor(name, shape, dt))
        sem = lambda name: ctx.enter_context(nc.semaphore(name))
        ps = lambda name, shape: ctx.enter_context(nc.psum_tensor(name, shape, F32))

        w_p = sb("d_wqkv", [P, CC, 3 * C])
        w_o = sb("d_wo", [P, CC, C])
        eps = sb("d_eps", [P, 1])
        carrier = sb("d_carrier", [P, 4])
        slot_now = sb("d_slot_now", [P, POS, TOP1], U32)
        y = sb("d_y", [P, TOP1, C])
        stats = sb("d_stats", [P, POS, 6])
        mean_var = sb("d_mean_var", [P, POS, 2])
        std = sb("d_std", [P, POS])
        rstd = sb("d_rstd", [P, POS])
        xn = sb("d_xn", [P, C])
        xnT = sb("d_xnT", [P, 2, C])
        q = sb("d_q", [P, 2, C])
        k = sb("d_k", [P, 2 * POS, C])
        v = sb("d_v", [P, 2 * POS, C])
        prod = sb("d_prod", [P, POS, C])
        s = sb("d_s", [P, POS, HEADS])
        e = sb("d_e", [P, POS, HEADS])
        most = sb("d_most", [P, HEADS])
        ao = sb("d_ao", [P, C])
        aoT = sb("d_aoT", [P, 2, C])

        qkv_p = ps("d_qkv_p", [P, 3, C])
        xp = ps("d_xp", [P, C])
        ap = ps("d_ap", [P, C])
        op = ps("d_op", [P, 2, C])

        w_loaded = sem("d_w_loaded")
        set_up = sem("d_set_up")
        slots_ready = sem("d_slots_ready")
        gathered = sem("d_gathered")
        combined = sem("d_combined")
        var_ready = sem("d_var_ready")
        std_ready = sem("d_std_ready")
        xn_ready = sem("d_xn_ready")
        x_turned = sem("d_x_turned")
        xnT_ready = sem("d_xnT_ready")
        qkv_full = sem("d_qkv_full")
        qkv_ready = sem("d_qkv_ready")
        s_ready = sem("d_s_ready")
        e_ready = sem("d_e_ready")
        ao_ready = sem("d_ao_ready")
        a_turned = sem("d_a_turned")
        aoT_ready = sem("d_aoT_ready")
        o_full = sem("d_o_full")
        o_taken = sem("d_o_taken")
        steps_sem = sem("d_steps")
        carried = sem("d_carried")

        block = ctx.enter_context(nc.Block())

        def chunks(eng, chunk):
            chunk(0, False)
            with eng.Fori(1, CHUNKS - 1) as ch:
                chunk(ch, False)
            chunk(CHUNKS - 1, True)

        @block.sync
        def _(sp):
            sp.dma_start(w_p[:], w_qkv.rearrange("(c p) o -> p c o", p=P)).then_inc(w_loaded, 16)
            sp.dma_start(w_o[:], w_out.rearrange("(c p) o -> p c o", p=P)).then_inc(w_loaded, 16)
            sp.wait_ge(w_loaded, 32)

        @block.gpsimd
        def _(pool):
            nc.gpsimd.memset(eps[:], LN_EPS).then_inc(set_up, 1)
            pool.wait_ge(set_up, 1)

            def gather(n, l, ch_slots):
                pool.wait_ge(slots_ready, ch_slots)
                pool.wait_ge(combined, n)
                pool.wait_ge(carried, n)
                nc.gpsimd.tensor_tensor(carrier[:, 0:1], eps[:], eps[:], ALU.add).then_inc(carried, 1)
                for t in range(TOP1):
                    nc.gpsimd.indirect_dma_start(y[:, t, :], None, ys, bass.IndirectOffsetOnAxis(
                        ap=slot_now[:, l, t:t + 1], axis=0)).then_inc(gathered, 16)

            def turn(ch):
                for l in range(POS):
                    gather(ch * POS + l, l, ch + 1)

            turn(0)
            with pool.Fori(1, CHUNKS) as ch:
                turn(ch)

        @block.tensor
        def _(pe):
            def turn_x(n):
                pe.wait_ge(xn_ready, n + 1)
                pe.wait_ge(xnT_ready, n)
                for c in range(CC):
                    ins = pe.transpose(xp[:, P * c:P * (c + 1)], xn[:, P * c:P * (c + 1)], ident[:])
                ins.then_inc(x_turned, 1)

            def project(n, l):
                pe.wait_ge(xnT_ready, n + 1)
                for j in range(3):
                    pe.wait_ge(qkv_ready, n * 3 - 2 + j) if l else pe.wait_ge(qkv_ready, n * 3)
                    for c in range(CC):
                        ins = pe.matmul(qkv_p[:, j, :], xnT[:, l % 2, P * c:P * (c + 1)], w_p[:, c, C * j:C * (j + 1)],
                                        start=(c == 0), stop=(c == CC - 1))
                    ins.then_inc(qkv_full, 1)

            def output(n, l):
                pe.wait_ge(ao_ready, n + 1)
                pe.wait_ge(aoT_ready, n)
                for c in range(CC):
                    ins = pe.transpose(ap[:, P * c:P * (c + 1)], ao[:, P * c:P * (c + 1)], ident[:])
                ins.then_inc(a_turned, 1)
                pe.wait_ge(aoT_ready, n + 1)
                if l >= 2:
                    pe.wait_ge(o_taken, n - 1)
                else:
                    pe.wait_ge(o_taken, n)
                for c in range(CC):
                    ins = pe.matmul(op[:, l % 2, :], aoT[:, l % 2, P * c:P * (c + 1)], w_o[:, c, :],
                                    start=(c == 0), stop=(c == CC - 1))
                ins.then_inc(o_full, 1)

            def chunk(ch, last):
                for l in range(POS):
                    n = ch * POS + l
                    project(n, l)
                    if l < POS - 1:
                        turn_x(n + 1)
                    if l >= 1:
                        output(n - 1, l - 1)
                if not last:
                    turn_x((ch + 1) * POS)
                output(ch * POS + POS - 1, POS - 1)

            pe.wait_ge(w_loaded, 32)
            turn_x(0)
            chunks(pe, chunk)

        @block.scalar
        def _(act):
            def root(ch):
                act.wait_ge(var_ready, ch + 1)
                nc.scalar.activation(std[:], mean_var[:, :, 1], ACT.Sqrt, bias=eps[:]).then_inc(std_ready, 1)

            def take_x(n, l):
                act.wait_ge(x_turned, n + 1)
                nc.scalar.copy(xnT[:, l % 2, :], xp[:]).then_inc(xnT_ready, 1)

            def take_qkv(n, l, side):
                for j in range(3):
                    act.wait_ge(qkv_full, n * 3 + j + 1)
                    if j == 0:
                        if l >= 2:
                            act.wait_ge(s_ready, n - 1)
                        else:
                            act.wait_ge(s_ready, n)
                        nc.scalar.mul(q[:, l % 2, :], qkv_p[:, 0, :], ATTN_SCALE).then_inc(qkv_ready, 1)
                    else:
                        nc.scalar.copy(tile_row((k, v)[j - 1], side * POS + l), qkv_p[:, j, :]).then_inc(qkv_ready, 1)

            def exps(n, l):
                act.wait_ge(s_ready, n + 1)
                nc.scalar.activation(e[:, 0:l + 1, :], s[:, 0:l + 1, :], ACT.Exp).then_inc(e_ready, 1)

            def take_a(n, l):
                act.wait_ge(a_turned, n + 1)
                nc.scalar.copy(aoT[:, l % 2, :], ap[:]).then_inc(aoT_ready, 1)

            def chunk(ch, last):
                side = ch % 2
                for l in range(POS):
                    n = ch * POS + l
                    take_qkv(n, l, side)
                    if l < POS - 1:
                        take_x(n + 1, l + 1)
                    if l >= 1:
                        take_a(n - 1, l - 1)
                    exps(n, l)
                if not last:
                    root(ch + 1)
                    take_x((ch + 1) * POS, 0)
                take_a(ch * POS + POS - 1, POS - 1)

            act.wait_ge(set_up, 1)
            root(0)
            take_x(0, 0)
            chunks(act, chunk)

        @block.vector
        def _(dve):
            def carry(column):
                dve.tensor_copy(carrier[:, column:column + 1], eps[:])

            def slots(ch):
                by_chunk = slot_all[:].rearrange("p (l ch) t -> p l ch t", ch=CHUNKS)
                dve.wait_ge(gathered, ch * (16 * TOP1 * POS))
                carry(1)
                dve.tensor_copy(slot_now[:], by_chunk[:, :, bass.ds(ch, 1), :].rearrange("p l c t -> p l (c t)"))\
                    .then_inc(slots_ready, 1)

            def combine(n, ch, l, steps):
                x = tile_row(X, ch + l * CHUNKS)
                dve.wait_ge(gathered, n * (16 * TOP1) + 16 * TOP1)
                for t in range(TOP1):
                    ins = dve.scalar_tensor_tensor(
                        out=x, in0=y[:, t, :],
                        scalar=weight_all[:, bass.ds(ch + l * CHUNKS, 1), t:t + 1].rearrange("p a b -> p (a b)"),
                        in1=x, op0=ALU.mult, op1=ALU.add)
                    if t == TOP1 - 1:
                        ins.then_inc(combined, 1)
                        dve.wait_ge(combined, n + 1)
                        carry(3)
                    else:
                        steps.mark(ins)
                        steps.wait()
                steps.mark(dve.bn_stats(stats[:, l, :], x))

            def aggregate(steps):
                steps.wait()
                carry(2)
                for l in range(POS):
                    ins = dve.bn_aggr(mean_var[:, l, :], stats[:, l, :])
                ins.then_inc(var_ready, 1)

            def reciprocals(ch, steps):
                dve.wait_ge(std_ready, ch + 1)
                steps.mark(dve.reciprocal(rstd[:], std[:]))
                steps.wait()

            def normalise(n, ch, l):
                dve.wait_ge(x_turned, n)
                dve.tensor_scalar(xn[:], tile_row(X, ch + l * CHUNKS), mean_var[:, l, 0:1],
                                  rstd[:, l:l + 1], ALU.subtract, ALU.mult).then_inc(xn_ready, 1)

            def take_output(n, ch, l):
                dve.wait_ge(o_full, n + 1)
                x = tile_row(X, ch + l * CHUNKS)
                dve.tensor_tensor(x, x, op[:, l % 2, :], ALU.add).then_inc(o_taken, 1)

            def scores(n, l, side, steps):
                m = l + 1
                dve.wait_ge(qkv_ready, n * 3 + 3)
                dve.wait_ge(ao_ready, n)
                steps.mark(dve.tensor_tensor(prod[:, 0:m, :], k[:, bass.ds(side * POS, m), :],
                                             q[:, l % 2:l % 2 + 1, :].broadcast_to([P, m, C]), ALU.mult))
                steps.wait()
                steps.mark(dve.tensor_reduce(s[:, 0:m, :], prod[:, 0:m, :].rearrange("p m (h d) -> p m h d", h=HEADS),
                                             AX.X, ALU.add))
                steps.wait()
                steps.mark(dve.tensor_reduce(most[:], s[:, 0:m, :].rearrange("p m h -> p h m"), AX.X, ALU.max))
                steps.wait()
                dve.tensor_tensor(s[:, 0:m, :], s[:, 0:m, :], most[:].unsqueeze(1).broadcast_to([P, m, HEADS]),
                                  ALU.subtract).then_inc(s_ready, 1)

            def average(n, l, side, steps):
                m = l + 1
                dve.wait_ge(e_ready, n + 1)
                steps.mark(dve.tensor_reduce(most[:], e[:, 0:m, :].rearrange("p m h -> p h m"), AX.X, ALU.add))
                steps.wait()
                steps.mark(dve.reciprocal(most[:], most[:]))
                steps.wait()
                steps.mark(dve.tensor_tensor(e[:, 0:m, :], e[:, 0:m, :],
                                             most[:].unsqueeze(1).broadcast_to([P, m, HEADS]), ALU.mult))
                steps.wait()
                vs = v[:, bass.ds(side * POS, m), :].rearrange("p m (h d) -> p m h d", h=HEADS)
                steps.mark(dve.tensor_tensor(prod[:, 0:m, :].rearrange("p m (h d) -> p m h d", h=HEADS), vs,
                                             e[:, 0:m, :].unsqueeze(3).broadcast_to([P, m, HEADS, HD]), ALU.mult))
                steps.wait()
                dve.wait_ge(a_turned, n)
                dve.tensor_reduce(ao[:], prod[:, 0:m, :].rearrange("p m c -> p c m"), AX.X, ALU.add)\
                    .then_inc(ao_ready, 1)

            FIRST = 2 * POS + 1
            PER_TURN = POS * 9 + 1

            def chunk(ch, last):
                side = ch % 2
                steps = Steps(dve, steps_sem, ch * PER_TURN + FIRST)
                if not last:
                    slots(ch + 1)
                for l in range(POS):
                    n = ch * POS + l
                    if l < POS - 1:
                        normalise(n + 1, ch, l + 1)
                    scores(n, l, side, steps)
                    if l >= 1:
                        take_output(n - 1, ch, l - 1)
                    if not last:
                        combine(n + POS, ch + 1, l, steps)
                        if l == POS - 1:
                            aggregate(steps)
                            reciprocals(ch + 1, steps)
                            normalise(n + 1, ch + 1, 0)
                    average(n, l, side, steps)
                take_output(ch * POS + POS - 1, ch, POS - 1)
                if not last:
                    assert steps.n == PER_TURN, steps.n

            dve.wait_ge(set_up, 1)
            slots(0)
            steps = Steps(dve, steps_sem)
            for l in range(POS):
                combine(l, 0, l, steps)
            aggregate(steps)
            reciprocals(0, steps)
            normalise(0, 0, 0)
            assert steps.n == FIRST, steps.n
            chunks(dve, chunk)


E2 = 64
TOP2 = 6
SETS = 8
TOP_SETS = 4
PER_SET = E2 // SETS
H2 = 192
HH2 = H2 // 2
ROUTE_SCALE = 2.5
CAP = 2 * (512 * TOP2 // E2)
SLOTS2 = E2 * CAP
ROWS2 = TOKENS + CAP
XC = C + E2
FAR = 3.0e38
NO_SLOT = 1.0e6
RING = 4


def second_ffn_shared(nc, X, ident, ones, gate_w, bias, ws_gate, ws_up, ws_down, w_gate, w_up, w_down,
                      wg_ring, wu_ring, wd_ring, ring_loaded, xs, table, total_rows):
    with ExitStack() as ctx:
        sb = lambda name, shape, dt=F32: ctx.enter_context(nc.sbuf_tensor(name, shape, dt))
        sem = lambda name: ctx.enter_context(nc.semaphore(name))
        ps = lambda name, shape: ctx.enter_context(nc.psum_tensor(name, shape, F32))

        w_g = sb("e_wg", [P, CC, H2])
        w_u = sb("e_wu", [P, CC, H2])
        w_d = sb("e_wd", [P, 2, C])
        w_route = sb("e_wroute", [P, CC, E2])
        bias_all = sb("e_bias", [P, E2])
        eps = sb("e_eps", [P, 1])
        carrier = sb("e_carrier", [P, 12])
        empty = sb("e_empty", [E2, CAP], U32)
        zrow = sb("e_zrow", [CAP, XC])
        set_iota = sb("e_set_iota", [P, SETS])
        expert_iota = sb("e_expert_iota", [P, E2])
        region = sb("e_region", [P, E2])
        token_id = sb("e_token_id", [P, TILES])
        stats = sb("e_stats", [P, GROUP, 6])
        mean_var = sb("e_mean_var", [P, GROUP, 2])
        std = sb("e_std", [P, GROUP])
        rstd = sb("e_rstd", [P, GROUP])
        xn = sb("e_xn", [P, GROUP, XC])
        xnT = sb("e_xnT", [P, CC, GROUP * P])
        hT = sb("e_hT", [P, 2, GROUP * P])
        sil = sb("e_sil", [P, 2, GROUP * P])
        score = sb("e_score", [P, GROUP, E2])
        biased = sb("e_biased", [P, GROUP, E2])
        set_best = sb("e_set_best", [P, GROUP, SETS, 8])
        set_score = sb("e_set_score", [P, GROUP, SETS])
        set_order = sb("e_set_order", [P, GROUP, 8])
        set_index = sb("e_set_index", [P, GROUP, 8], U32)
        set_index_f = sb("e_set_index_f", [P, GROUP, TOP_SETS])
        set_onehot = sb("e_set_onehot", [P, GROUP, TOP_SETS, SETS])
        set_kept = sb("e_set_kept", [P, GROUP, SETS])
        set_far = sb("e_set_far", [P, GROUP, SETS])
        best = sb("e_best", [P, GROUP, 8])
        best_i = sb("e_best_i", [P, GROUP, 8], U32)
        best_f = sb("e_best_f", [P, GROUP, TOP2])
        onehot = sb("e_onehot", [P, GROUP, TOP2, E2])
        chosen = sb("e_chosen", [P, GROUP, E2])
        weight = sb("e_weight", [P, GROUP, E2])
        weight_sum = sb("e_weight_sum", [P, GROUP])
        total = sb("e_total", [P, E2])
        place = sb("e_place", [P, GROUP, E2])
        fits = sb("e_fits", [P, GROUP, E2])
        slot_top = sb("e_slot_top", [P, GROUP, 8])
        slot_none = sb("e_slot_none", [P, GROUP, 8])
        slot_now = sb("e_slot_now", [P, GROUP, 8], U32)
        token_now = sb("e_token_now", [P, GROUP], U32)

        up = ps("e_up", [P, 2, 2, GROUP * P])
        pj = ps("e_pj", [P, 2, C])
        lg = ps("e_lg", [P, GROUP, E2])
        cnt = ps("e_cnt", [P, GROUP + 1, E2])

        w_loaded = sem("e_w_loaded")
        set_up = sem("e_set_up")
        rows_set = sem("e_rows_set")
        var_ready = sem("e_var_ready")
        std_ready = sem("e_std_ready")
        xn_ready = sem("e_xn_ready")
        xn_stored = sem("e_xn_stored")
        x_final = sem("e_x_final")
        x_stored = sem("e_x_stored")
        pj_full = sem("e_pj_full")
        pj_taken = [sem("e_pj_taken0"), sem("e_pj_taken1")]
        lg_full = sem("e_lg_full")
        score_ready = sem("e_score_ready")
        chosen_ready = sem("e_chosen_ready")
        weight_ready = sem("e_weight_ready")
        cnt_full = sem("e_cnt_full")
        up_full = sem("e_up_full")
        sil_ready = sem("e_sil_ready")
        h_ready = sem("e_h_ready")
        slots_ready = sem("e_slots_ready")
        scattered = sem("e_scattered")
        steps_sem = sem("e_steps")
        carried = sem("e_carried")
        SET_UP = 9
        HP = (P, H2 - P)

        block = ctx.enter_context(nc.Block())

        @block.sync
        def _(sp):
            sp.dma_start(w_route[:], gate_w.rearrange("(c p) e -> p c e", p=P)).then_inc(w_loaded, 16)
            sp.dma_start(bias_all[:], bias.unsqueeze(0).broadcast_to([P, E2])).then_inc(w_loaded, 16)
            for dst, src in ((w_g, ws_gate), (w_u, ws_up)):
                sp.dma_start(dst[:], src.rearrange("(c p) o -> p c o", p=P)).then_inc(w_loaded, 16)
            for f in range(2):
                sp.dma_start(w_d[0:HP[f], f, :], ws_down[P * f:P * f + HP[f], :]).then_inc(w_loaded, 16)
            sp.wait_ge(set_up, SET_UP)
            sp.dma_start(table.rearrange("(e s) one -> e (s one)", e=E2), empty[:]).then_inc(rows_set, 16)
            sp.dma_start(xs[TOKENS:ROWS2, :], zrow[:]).then_inc(rows_set, 16)
            sp.dma_start(total_rows[TOKENS:ROWS2, :], zrow[:, 0:C]).then_inc(rows_set, 16)
            for e in range(RING):
                for dst, src, n in ((wg_ring[:, e, :, :], w_gate, CC), (wu_ring[:, e, :, :], w_up, CC),
                                    (wd_ring[:, e, :, :], w_down, 2)):
                    sp.dma_start(dst, src[e].rearrange("(p c) f -> p c f", c=n)).then_inc(ring_loaded[e], 16)
            for g in range(GROUPS):
                sp.wait_ge(xn_ready, g + 1)
                sp.wait_ge(weight_ready, g + 1)
                sp.dma_start(group_rows(xs[0:TOKENS, :], g), xn[:]).then_inc(xn_stored, 16)
                sp.wait_ge(x_final, g + 1)
                sp.dma_start(group_rows(total_rows[0:TOKENS, :], g), X[:, GROUP * g:GROUP * (g + 1), :])\
                    .then_inc(x_stored, 16)
            sp.wait_ge(xn_stored, 16 * GROUPS)
            sp.wait_ge(x_stored, 16 * GROUPS)
            sp.wait_ge(rows_set, 48)

        @block.gpsimd
        def _(pool):
            iota = lambda out, pattern, base, m: nc.gpsimd.iota(
                out, pattern, base=base, channel_multiplier=m,
                allow_small_or_imprecise_dtypes=True).then_inc(set_up, 1)
            nc.gpsimd.memset(eps[:], LN_EPS).then_inc(set_up, 1)
            nc.gpsimd.memset(total[:], 0.0).then_inc(set_up, 1)
            nc.gpsimd.memset(zrow[:], 0.0).then_inc(set_up, 1)
            iota(empty[:], [[1, CAP]], TOKENS, 0)
            iota(set_iota[:], [[1, SETS]], 0, 0)
            iota(expert_iota[:], [[1, E2]], 0, 0)
            iota(region[:], [[CAP, E2]], 1, 0)
            iota(token_id[:], [[P, TILES]], 0, 1)
            nc.gpsimd.memset(carrier[:], 0.0).then_inc(set_up, 1)
            pool.wait_ge(rows_set, 48)
            pool.wait_ge(set_up, SET_UP)

            def turn(g):
                pool.wait_ge(slots_ready, g + 1)
                pool.wait_ge(carried, g)
                nc.gpsimd.tensor_tensor(carrier[:, 0:1], eps[:], eps[:], ALU.add).then_inc(carried, 1)
                for i in range(GROUP):
                    for k in range(TOP2):
                        nc.gpsimd.indirect_dma_start(
                            table, bass.IndirectOffsetOnAxis(ap=slot_now[:, i, k:k + 1], axis=0),
                            token_now[:, i:i + 1], None, bounds_check=SLOTS2 - 1, oob_is_err=False)\
                            .then_inc(scattered, 16)

            turn(0)
            with pool.Fori(1, GROUPS) as g:
                turn(g)
            pool.wait_ge(scattered, 16 * GROUPS * GROUP * TOP2)

        PJ = 8

        @block.tensor
        def _(pe):
            def bank_free(u, g):
                pe.wait_ge(pj_taken[u % 2], g * (PJ // 2) + 2 + u // 2)

            def transposes(g, first):
                pe.wait_ge(xn_ready, g + 1)
                for c in range(CC):
                    if not first:
                        bank_free(c, g - 1)
                    elif c >= 2:
                        pe.wait_ge(pj_taken[c % 2], 1)
                    for i in range(GROUP):
                        ins = pe.transpose(pj[:, c % 2, P * i:P * (i + 1)], xn[:, i, P * c:P * (c + 1)], ident[:])
                    ins.then_inc(pj_full, 1)

            def group(g, last):
                for k in range(2):
                    pe.wait_ge(pj_taken[k], g * (PJ // 2) + 2)
                for i in range(GROUP):
                    for c in range(CC):
                        ins = pe.matmul(lg[:, i, :], xnT[:, c, P * i:P * (i + 1)], w_route[:, c, :],
                                        start=(c == 0), stop=(c == CC - 1))
                ins.then_inc(lg_full, 1)
                for f in range(2):
                    pe.wait_ge(h_ready, g * 2)
                    for k, w in ((0, w_g), (1, w_u)):
                        for c in range(CC):
                            ins = pe.matmul(up[0:HP[f], f, k, :], w[:, c, P * f:P * f + HP[f]], xnT[:, c, :],
                                            start=(c == 0), stop=(c == CC - 1))
                    ins.then_inc(up_full, 1)
                pe.wait_ge(h_ready, g * 2 + 2)
                for i in range(GROUP):
                    bank_free(i, g)
                    for f in range(2):
                        ins = pe.matmul(pj[:, i % 2, :], hT[0:HP[f], f, P * i:P * (i + 1)], w_d[0:HP[f], f, :],
                                        start=(f == 0), stop=(f == 1))
                    ins.then_inc(pj_full, 1)
                pe.wait_ge(chosen_ready, g + 1)
                pe.wait_ge(slots_ready, g)
                for i in range(GROUP + 1):
                    for j in range(min(i + 1, GROUP)):
                        ins = pe.matmul(cnt[:, i, :], ones[:, P:2 * P] if j == i else ones[:, 0:P], chosen[:, j, :],
                                        start=(j == 0), stop=(j == min(i, GROUP - 1)))
                ins.then_inc(cnt_full, 1)
                if not last:
                    pe.wait_ge(xn_ready, g + 2)
                    for c in range(CC):
                        bank_free(4 + c, g)
                        for i in range(GROUP):
                            ins = pe.transpose(pj[:, c % 2, P * i:P * (i + 1)], xn[:, i, P * c:P * (c + 1)], ident[:])
                        ins.then_inc(pj_full, 1)

            pe.wait_ge(w_loaded, 96)
            transposes(0, True)
            group(0, False)
            with pe.Fori(1, GROUPS - 1) as g:
                group(g, False)
            group(GROUPS - 1, True)

        @block.scalar
        def _(act):
            def root(g):
                act.wait_ge(var_ready, g + 1)
                nc.scalar.activation(std[:], mean_var[:, :, 1], ACT.Sqrt, bias=eps[:]).then_inc(std_ready, 1)

            def take_xnT(c, n):
                act.wait_ge(pj_full, n)
                nc.scalar.copy(xnT[:, c, :], pj[:, c % 2, :]).then_inc(pj_taken[c % 2], 1)

            def group(g, last):
                act.wait_ge(lg_full, g + 1)
                nc.scalar.activation(score[:], lg[:], ACT.Sigmoid).then_inc(score_ready, 1)
                for f in range(2):
                    act.wait_ge(up_full, g * 2 + f + 1)
                    nc.scalar.activation(sil[0:HP[f], f, :], up[0:HP[f], f, 0, :], ACT.Silu).then_inc(sil_ready, 1)
                if not last:
                    root(g + 1)
                    for c in (0, 2):
                        take_xnT(c, g * PJ + 4 + 4 + c + 1)

            act.wait_ge(set_up, SET_UP)
            root(0)
            for c in (0, 2):
                take_xnT(c, c + 1)
            group(0, False)
            with act.Fori(1, GROUPS - 1) as g:
                group(g, False)
            group(GROUPS - 1, True)

        @block.vector
        def _(dve):
            G3 = [P, GROUP, E2]

            def carry(column):
                dve.tensor_copy(carrier[:, column:column + 1], eps[:])

            def statistics(g, steps):
                layernorm_tiles(dve, steps, lambda i: tile_row(X, g * GROUP + i), stats, mean_var, GROUP,
                                carrier[:, 4:5], eps[:]).then_inc(var_ready, 1)

            def normalise(g, steps, first):
                dve.wait_ge(std_ready, g + 1)
                steps.mark(dve.reciprocal(rstd[:], std[:]))
                steps.wait()
                if not first:
                    dve.wait_ge(xn_stored, g * 16)
                for i in range(GROUP):
                    ins = dve.tensor_scalar(xn[:, i, 0:C], tile_row(X, g * GROUP + i),
                                            mean_var[:, i, 0:1], rstd[:, i:i + 1], ALU.subtract, ALU.mult)
                ins.then_inc(xn_ready, 1)

            def take_xnT(c, n):
                dve.wait_ge(pj_full, n)
                dve.tensor_copy(xnT[:, c, :], pj[:, 1, :]).then_inc(pj_taken[1], 1)

            def hidden(g):
                for f in range(2):
                    dve.wait_ge(sil_ready, g * 2 + f + 1)
                    dve.tensor_tensor(hT[0:HP[f], f, :], sil[0:HP[f], f, :], up[0:HP[f], f, 1, :], ALU.mult)\
                        .then_inc(h_ready, 1)

            def choose_sets(g, steps):
                dve.wait_ge(score_ready, g + 1)
                steps.mark(dve.tensor_tensor(biased[:], score[:], bias_all[:].unsqueeze(1).broadcast_to(G3), ALU.add))
                steps.wait()
                carry(5)
                for i in range(GROUP):
                    for t in range(SETS):
                        ins = dve.max(set_best[:, i, t, :], biased[:, i, PER_SET * t:PER_SET * (t + 1)])
                steps.mark(ins)
                steps.wait()
                steps.mark(dve.tensor_tensor(set_score[:], set_best[:, :, :, 0], set_best[:, :, :, 1], ALU.add))
                steps.wait()
                carry(6)
                for i in range(GROUP):
                    ins = dve.max(set_order[:, i, :], set_score[:, i, :])
                steps.mark(ins)
                steps.wait()
                carry(7)
                for i in range(GROUP):
                    ins = dve.max_index(set_index[:, i, :], set_order[:, i, :], set_score[:, i, :])
                steps.mark(ins)
                steps.wait()
                steps.mark(dve.tensor_copy(set_index_f[:], set_index[:, :, 0:TOP_SETS]))
                steps.wait()
                shape = [P, GROUP, TOP_SETS, SETS]
                steps.mark(dve.tensor_tensor(set_onehot[:], set_iota[:].unsqueeze(1).unsqueeze(1).broadcast_to(shape),
                                             set_index_f[:].unsqueeze(3).broadcast_to(shape), ALU.is_equal))
                steps.wait()
                steps.mark(dve.tensor_reduce(set_kept[:], set_onehot[:].rearrange("p i k s -> p i s k"), AX.X, ALU.add))
                steps.wait()
                steps.mark(dve.tensor_scalar(set_far[:], set_kept[:], 1.0, FAR, ALU.subtract, ALU.mult))
                by_set = biased[:].rearrange("p i (s e) -> p i s e", s=SETS)
                shape = [P, GROUP, SETS, PER_SET]
                steps.mark(dve.tensor_tensor(by_set, by_set, set_kept[:].unsqueeze(3).broadcast_to(shape), ALU.mult))
                steps.wait()
                steps.mark(dve.tensor_tensor(by_set, by_set, set_far[:].unsqueeze(3).broadcast_to(shape), ALU.add))
                steps.wait()

            def choose(g, steps):
                carry(8)
                for i in range(GROUP):
                    ins = dve.max(best[:, i, :], biased[:, i, :])
                steps.mark(ins)
                steps.wait()
                carry(9)
                for i in range(GROUP):
                    ins = dve.max_index(best_i[:, i, :], best[:, i, :], biased[:, i, :])
                steps.mark(ins)
                steps.wait()
                steps.mark(dve.tensor_copy(best_f[:], best_i[:, :, 0:TOP2]))
                steps.wait()
                shape = [P, GROUP, TOP2, E2]
                steps.mark(dve.tensor_tensor(onehot[:], expert_iota[:].unsqueeze(1).unsqueeze(1).broadcast_to(shape),
                                             best_f[:].unsqueeze(3).broadcast_to(shape), ALU.is_equal))
                steps.wait()
                dve.tensor_reduce(chosen[:], onehot[:].rearrange("p i k e -> p i e k"), AX.X, ALU.add)\
                    .then_inc(chosen_ready, 1)
                dve.wait_ge(chosen_ready, g + 1)
                steps.mark(dve.tensor_tensor(weight[:], chosen[:], score[:], ALU.mult))
                steps.wait()
                steps.mark(dve.tensor_reduce(weight_sum[:], weight[:], AX.X, ALU.add))
                steps.wait()
                steps.mark(dve.reciprocal(weight_sum[:], weight_sum[:]))
                steps.wait()
                dve.wait_ge(xn_stored, g * 16)
                dve.scalar_tensor_tensor(out=xn[:, :, C:XC], in0=weight[:], scalar=ROUTE_SCALE,
                                         in1=weight_sum[:].unsqueeze(2).broadcast_to(G3), op0=ALU.mult, op1=ALU.mult)\
                    .then_inc(weight_ready, 1)

            def place_slots(g, steps):
                dve.wait_ge(cnt_full, g + 1)
                steps.mark(dve.tensor_tensor(place[:], cnt[:, 0:GROUP, :], total[:].unsqueeze(1).broadcast_to(G3),
                                             ALU.add))
                steps.wait()
                steps.mark(dve.tensor_tensor(total[:], total[:], cnt[:, GROUP, :], ALU.add))
                steps.mark(dve.scalar_tensor_tensor(out=fits[:], in0=place[:], scalar=float(CAP), in1=chosen[:],
                                                    op0=ALU.is_lt, op1=ALU.mult))
                steps.wait()
                steps.mark(dve.tensor_tensor(place[:], place[:], region[:].unsqueeze(1).broadcast_to(G3), ALU.add))
                steps.wait()
                steps.mark(dve.tensor_tensor(place[:], place[:], fits[:], ALU.mult))
                steps.wait()
                carry(10)
                for i in range(GROUP):
                    ins = dve.max(slot_top[:, i, :], place[:, i, :])
                steps.mark(ins)
                steps.wait()
                steps.mark(dve.tensor_scalar(slot_none[:], slot_top[:], 0.0, NO_SLOT, ALU.is_equal, ALU.mult))
                steps.wait()
                steps.mark(dve.scalar_tensor_tensor(out=slot_top[:], in0=slot_top[:], scalar=1.0, in1=slot_none[:],
                                                    op0=ALU.subtract, op1=ALU.add))
                steps.wait()
                dve.wait_ge(scattered, g * (16 * GROUP * TOP2))
                dve.tensor_scalar(token_now[:], token_id[:, bass.ds(g * GROUP, GROUP)], 0.0, None, ALU.add)
                dve.tensor_copy(slot_now[:], slot_top[:]).then_inc(slots_ready, 1)

            PER_TURN = 1 + 1 + 10 + 1 + 7 + 8

            def group(g, last):
                steps = Steps(dve, steps_sem, g * PER_TURN + 2)
                if not last:
                    statistics(g + 1, steps)
                choose_sets(g, steps)
                hidden(g)
                choose(g, steps)
                for i in range(GROUP):
                    dve.wait_ge(pj_full, g * PJ + 4 + i + 1)
                    x = tile_row(X, g * GROUP + i)
                    ins = dve.tensor_tensor(x, x, pj[:, i % 2, :], ALU.add)
                    ins.then_inc(pj_taken[i % 2], 1)
                dve.wait_ge(pj_taken[0], g * (PJ // 2) + 4)
                dve.wait_ge(pj_taken[1], g * (PJ // 2) + 4)
                dve.tensor_copy(carrier[:, 3:4], eps[:]).then_inc(x_final, 1)
                if not last:
                    normalise(g + 1, steps, False)
                place_slots(g, steps)
                assert steps.n == PER_TURN - (2 if last else 0), steps.n
                if not last:
                    for c in (1, 3):
                        take_xnT(c, g * PJ + 4 + 4 + c + 1)

            dve.wait_ge(set_up, SET_UP)
            dve.wait_ge(w_loaded, 96)
            steps = Steps(dve, steps_sem)
            statistics(0, steps)
            normalise(0, steps, True)
            for c in (1, 3):
                take_xnT(c, c + 1)
            group(0, False)
            with dve.Fori(1, GROUPS - 1) as g:
                group(g, False)
            group(GROUPS - 1, True)


def second_ffn_experts(nc, ident, w_gate, w_up, w_down, wg_ring, wu_ring, wd_ring, ring_loaded, xs, table, total_rows,
                       out):
    with ExitStack() as ctx:
        sb = lambda name, shape, dt=F32: ctx.enter_context(nc.sbuf_tensor(name, shape, dt))
        sem = lambda name: ctx.enter_context(nc.semaphore(name))
        ps = lambda name, shape: ctx.enter_context(nc.psum_tensor(name, shape, F32))

        ids_rows = sb("f_ids_rows", [E2, CAP], U32)
        ids_rows_f = sb("f_ids_rows_f", [E2, CAP])
        ids_f = sb("f_ids_f", [CAP, E2])
        ids = sb("f_ids", [CAP, RING, 1], U32)
        xg = sb("f_xg", [CAP, RING, XC])
        xgT = sb("f_xgT", [P, 2, CC * CAP])
        sil = sb("f_sil", [CAP, 2, H2])
        h = sb("f_h", [CAP, 2, H2])
        hT = sb("f_hT", [HH2, 2, 2 * CAP])
        y = sb("f_y", [CAP, RING, C])
        carrier = sb("f_carrier", [P, 2])

        up = ps("f_up", [CAP, 2, 512])
        yp = ps("f_yp", [CAP, 2, C])
        xp = ps("f_xp", [P, 2, 512])
        hp = ps("f_hp", [HH2, 2, 512])

        ids_loaded = sem("f_ids_loaded")
        ids_float = sem("f_ids_float")
        ids_turned = sem("f_ids_turned")
        ids_steps = sem("f_ids_steps")
        ids_ready = sem("f_ids_ready")
        gathered = [sem(f"f_gathered{r}") for r in range(RING)]
        added = sem("f_added")
        x_turned = sem("f_x_turned")
        xgT_ready = sem("f_xgT_ready")
        up_full = sem("f_up_full")
        sil_ready = sem("f_sil_ready")
        h_ready = sem("f_h_ready")
        h_turned = sem("f_h_turned")
        hT_ready = sem("f_hT_ready")
        y_full = sem("f_y_full")
        y_ready = sem("f_y_ready")
        carried = sem("f_carried")
        copied = sem("f_copied")
        TURNS = E2 // RING

        def turns(eng, expert):
            for r in range(RING):
                expert(r, r, 0, "first")
            for r in range(RING):
                expert(RING + r, r, 1, "")
            with eng.Fori(2, TURNS - 1) as t:
                for r in range(RING):
                    expert(t * RING + r, r, t, "")
            for r in range(RING):
                expert((TURNS - 1) * RING + r, r, TURNS - 1, "last")

        block = ctx.enter_context(nc.Block())

        @block.sync
        def _(sp):
            sp.dma_start(ids_rows[:], table.rearrange("(e s) one -> e (s one)", e=E2)).then_inc(ids_loaded, 16)

        @block.gpsimd
        def _(pool):
            def start(e, r):
                pool.wait_ge(ids_ready, e + 1)
                if e:
                    pool.wait_ge(carried, e)
                nc.gpsimd.tensor_tensor(carrier[:, 0:1], ident[:, 0:1], ident[:, 0:1], ALU.add).then_inc(carried, 1)
                nc.gpsimd.indirect_dma_start(xg[:, r, :], None, xs, bass.IndirectOffsetOnAxis(
                    ap=ids[:, r, :], axis=0)).then_inc(gathered[r], 16)

            AHEAD = 2

            def ahead(e, r):
                pool.wait_ge(ids_ready, e + 1)
                pool.wait_ge(carried, e * 2 - AHEAD)
                nc.gpsimd.tensor_tensor(carrier[:, 0:1], ident[:, 0:1], ident[:, 0:1], ALU.add).then_inc(carried, 1)
                nc.gpsimd.indirect_dma_start(xg[:, r, :], None, xs, bass.IndirectOffsetOnAxis(
                    ap=ids[:, r, :], axis=0)).then_inc(gathered[r], 16)

            def add_now(e, r, n):
                pool.wait_ge(y_ready, e + 1)
                pool.wait_ge(added, e * 16)
                pool.wait_ge(carried, n)
                nc.gpsimd.tensor_tensor(carrier[:, 0:1], ident[:, 0:1], ident[:, 0:1], ALU.add).then_inc(carried, 1)
                nc.gpsimd.indirect_dma_start(total_rows, bass.IndirectOffsetOnAxis(ap=ids[:, r, :], axis=0),
                                             y[:, r, :], None, compute_op=ALU.add).then_inc(added, 16)

            def expert(e, r, t, which):
                if not (which == "last" and r >= RING - AHEAD):
                    ahead(e + AHEAD, (r + AHEAD) % RING)
                    add_now(e, r, e * 2 + AHEAD + 1)
                else:
                    add_now(e, r, 2 * E2 - (E2 - e))

            for e in range(AHEAD):
                start(e, e)
            turns(pool, expert)
            pool.wait_ge(added, 16 * E2)
            rows = TOKENS // 8
            for b in range(8):
                pool.dma_start(out[rows * b:rows * (b + 1), :], total_rows[rows * b:rows * (b + 1), :])\
                    .then_inc(copied, 16)
            pool.wait_ge(copied, 16 * 8)

        @block.tensor
        def _(pe):
            def turn_x(e, r, t, start):
                pe.wait_ge(gathered[r], t * 16 + 16)
                if not start:
                    pe.wait_ge(xgT_ready, e - 1)
                rows = xg[:, r, 0:C].rearrange("s (p c) -> s c p", c=CC)
                for c in range(CC):
                    ins = pe.transpose(xp[:, r % 2, CAP * c:CAP * (c + 1)], rows[:, c, :], ident[0:CAP, 0:CAP])
                ins.then_inc(x_turned, 1)

            def down(e, r, start):
                pe.wait_ge(hT_ready, e + 1)
                if not start:
                    pe.wait_ge(y_ready, e - 1)
                for f in range(2):
                    ins = pe.matmul(yp[:, r % 2, :], hT[:, r % 2, CAP * f:CAP * (f + 1)], wd_ring[:, r, f, :],
                                    start=(f == 0), stop=(f == 1))
                ins.then_inc(y_full, 1)

            def expert(e, r, t, which):
                start = which == "first"
                pe.wait_ge(ring_loaded[r], t * 48 + 48)
                pe.wait_ge(xgT_ready, e + 1)
                if not (start and r < 2):
                    pe.wait_ge(h_ready, e - 1)
                for k, w in ((0, wg_ring), (1, wu_ring)):
                    for c in range(CC):
                        ins = pe.matmul(up[:, r % 2, H2 * k:H2 * (k + 1)], xgT[:, r % 2, CAP * c:CAP * (c + 1)],
                                        w[:, r, c, :], start=(c == 0), stop=(c == CC - 1))
                ins.then_inc(up_full, 1)
                if not (start and r == 0):
                    down(e - 1, (r - 1) % RING, start and r < 3)
                if not (which == "last" and r == RING - 1):
                    turn_x(e + 1, (r + 1) % RING, t + (r + 1) // RING, start and r < 1)
                pe.wait_ge(h_ready, e + 1)
                if not (start and r < 2):
                    pe.wait_ge(hT_ready, e - 1)
                halves = h[:, r % 2, :].rearrange("s (p c) -> s c p", c=2)
                for f in range(2):
                    ins = pe.transpose(hp[:, r % 2, CAP * f:CAP * (f + 1)], halves[:, f, :], ident[0:CAP, 0:CAP])
                ins.then_inc(h_turned, 1)

            pe.wait_ge(ids_float, 1)
            pe.transpose(hp[:, 0, 0:E2], ids_rows_f[:], ident[0:E2, 0:E2]).then_inc(ids_turned, 1)
            turn_x(0, 0, 0, True)
            turns(pe, expert)
            down(E2 - 1, RING - 1, False)

        @block.scalar
        def _(act):
            def load(e, r):
                act.wait_ge(y_full, e - (RING - 1))
                for dst, src, n in ((wg_ring[:, r, :, :], w_gate, CC), (wu_ring[:, r, :, :], w_up, CC),
                                    (wd_ring[:, r, :, :], w_down, 2)):
                    act.dma_start(dst, src[bass.ds(e, 1)].rearrange("a (p c) f -> p (a c) f", c=n))\
                        .then_inc(ring_loaded[r], 16)

            def take_x(e, r, start):
                act.wait_ge(x_turned, e + 1)
                if not start:
                    act.wait_ge(up_full, e - 1)
                nc.scalar.copy(xgT[:, r % 2, :], xp[:, r % 2, 0:CC * CAP]).then_inc(xgT_ready, 1)

            def expert(e, r, t, which):
                act.wait_ge(up_full, e + 1)
                if not (which == "first" and r < 2):
                    act.wait_ge(h_ready, e - 1)
                nc.scalar.activation(sil[:, r % 2, :], up[:, r % 2, 0:H2], ACT.Silu).then_inc(sil_ready, 1)
                if not (which == "last" and r == RING - 1):
                    take_x(e + 1, (r + 1) % RING, which == "first" and r < 1)
                if not (which == "first" and r == 0) and not (which == "last" and r >= 1):
                    load(e + RING - 1, (r - 1) % RING)

            take_x(0, 0, True)
            turns(act, expert)

        @block.vector
        def _(dve):
            def pick_ids(e, r, start):
                if not start:
                    dve.wait_ge(added, (e - RING + 1) * 16)
                dve.tensor_scalar(ids[:, r, :], ids_f[:, bass.ds(e, 1)], 0.0, None, ALU.add).then_inc(ids_ready, 1)

            def take_y(e, r, start):
                dve.wait_ge(y_full, e + 1)
                if not start:
                    dve.wait_ge(added, (e - RING + 1) * 16)
                weight = xg[:, r, bass.ds(e + C, 1)]
                dve.tensor_scalar(y[:, r, :], yp[:, r % 2, :], weight, None, ALU.mult).then_inc(y_ready, 1)

            def expert(e, r, t, which):
                dve.wait_ge(sil_ready, e + 1)
                if not (which == "first" and r < 2):
                    dve.wait_ge(h_turned, e - 1)
                dve.tensor_tensor(h[:, r % 2, :], sil[:, r % 2, :], up[:, r % 2, H2:2 * H2], ALU.mult)\
                    .then_inc(h_ready, 1)
                if not (which == "first" and r == 0):
                    take_y(e - 1, (r - 1) % RING, which == "first")
                dve.wait_ge(h_turned, e + 1)
                if not (which == "first" and r < 2):
                    dve.wait_ge(y_full, e - 1)
                dve.tensor_copy(hT[:, r % 2, :], hp[:, r % 2, 0:2 * CAP]).then_inc(hT_ready, 1)
                if not (which == "last" and r >= 1):
                    pick_ids(e + 3, (r + 3) % RING, which == "first" and r == 0)

            dve.wait_ge(ids_loaded, 16)
            dve.tensor_copy(ids_rows_f[:], ids_rows[:]).then_inc(ids_float, 1)
            dve.wait_ge(ids_turned, 1)
            dve.tensor_copy(ids_f[:], hp[:, 0, 0:E2]).then_inc(ids_steps, 1)
            dve.wait_ge(ids_steps, 1)
            for e in range(3):
                pick_ids(e, e, True)
            turns(dve, expert)
            take_y(E2 - 1, RING - 1, False)


def program(nc, x, wq, wk, wv, wo, route1, w_gate1, w_up1, w_down1, sh_gate, sh_up, sh_down, w_qkv, w_out,
            route2, bias2, w_gate2, w_up2, w_down2, ws_gate, ws_up, ws_down, out):
    rows_1 = nc.dram_tensor("rows_1", [ROWS, C], F32).ap()
    table_1 = nc.dram_tensor("table_1", [SLOTS1, 1], U32).ap()
    expert_rows = nc.dram_tensor("expert_rows", [2 * PAIRS1 * P, C], F32).ap()
    rows_2 = nc.dram_tensor("rows_2", [ROWS2, XC], F32).ap()
    table_2 = nc.dram_tensor("table_2", [SLOTS2, 1], U32).ap()
    total_rows = nc.dram_tensor("total_rows", [ROWS2, C], F32).ap()

    with ExitStack() as ctx:
        ident = ctx.enter_context(nc.sbuf_tensor("ident", [P, P], F32))
        ones = ctx.enter_context(nc.sbuf_tensor("ones", [P, 2 * P], F32))
        constants(nc, ctx, ident, ones)
        with ExitStack() as rows_ctx:
            X = rows_ctx.enter_context(nc.sbuf_tensor("X", [P, TILES, C], F32))
            first_attention(nc, x, wq, wk, wv, wo, X, ident, ones)
            with ExitStack() as routed:
                sb = lambda name, shape, dt=F32: routed.enter_context(nc.sbuf_tensor(name, shape, dt))
                weight_all = sb("weight_all", [P, TILES, TOP1])
                slot_all = sb("slot_all", [P, TILES, TOP1], U32)
                with ExitStack() as weights:
                    sb = lambda name, shape, dt=F32: weights.enter_context(nc.sbuf_tensor(name, shape, dt))
                    tile_expert = sb("tile_expert", [P, 2 * PAIRS1], I32)
                    tile_slot = sb("tile_slot", [P, 2 * PAIRS1], I32)
                    w13 = sb("w13", [P, CC * E1, 2 * H1])
                    w13_loaded = weights.enter_context(nc.semaphore("w13_loaded"))
                    first_ffn_shared(nc, X, ident, ones, w13_loaded, route1, sh_gate, sh_up, sh_down, w_gate1, w_up1,
                                     w13, rows_1, table_1, weight_all, slot_all, tile_expert, tile_slot)
                    w2 = sb("w2", [P, HC1 * E1, C])
                    first_ffn_experts(nc, ident, w13, w13_loaded, w2, w_down1, rows_1, table_1, expert_rows,
                                      tile_expert, tile_slot)
                second_attention(nc, X, ident, ones, expert_rows, slot_all, weight_all, w_qkv, w_out)
            wg_ring = rows_ctx.enter_context(nc.sbuf_tensor("wg_ring", [P, RING, CC, H2], F32))
            wu_ring = rows_ctx.enter_context(nc.sbuf_tensor("wu_ring", [P, RING, CC, H2], F32))
            wd_ring = rows_ctx.enter_context(nc.sbuf_tensor("wd_ring", [HH2, RING, 2, C], F32))
            ring_loaded = [rows_ctx.enter_context(nc.semaphore(f"ring_loaded{r}")) for r in range(RING)]
            second_ffn_shared(nc, X, ident, ones, route2, bias2, ws_gate, ws_up, ws_down, w_gate2, w_up2, w_down2,
                              wg_ring, wu_ring, wd_ring, ring_loaded, rows_2, table_2, total_rows)
            second_ffn_experts(nc, ident, w_gate2, w_up2, w_down2, wg_ring, wu_ring, wd_ring, ring_loaded, rows_2,
                               table_2, total_rows, out)


def kernel(**inputs):
    import numpy as _np
    import concourse.bacc as _bacc
    from concourse import mybir as _mybir
    from concourse.bass_utils import run_bass_kernel_spmd as _run

    a = {name: _np.asarray(value) for name, value in inputs.items()}
    turned = lambda w: _np.swapaxes(w, -1, -2)
    laid_out = {
        "x": a["L0_attn_x"].reshape(TOKENS, C),
        "wq": turned(a["L0_attn_Wq"]), "wk": turned(a["L0_attn_Wk"]), "wv": turned(a["L0_attn_Wv"]),
        "wo": turned(a["L0_attn_Wo"]),
        "route1": turned(_np.concatenate([a["L0_ffn_gate_w"], a["L0_ffn_se_gate_w"]], axis=0)),
        "w_gate1": turned(a["L0_ffn_w_gate"]), "w_up1": turned(a["L0_ffn_w_up"]), "w_down1": turned(a["L0_ffn_w_down"]),
        "sh_gate": turned(a["L0_ffn_sh_gate"]), "sh_up": turned(a["L0_ffn_sh_up"]),
        "sh_down": turned(a["L0_ffn_sh_down"]),
        "w_qkv": turned(a["L1_attn_weight_qkv"]), "w_out": turned(a["L1_attn_weight_out"]),
        "route2": a["L1_ffn_gate_w"], "bias2": a["L1_ffn_bias"],
        "w_gate2": a["L1_ffn_w_gate"], "w_up2": a["L1_ffn_w_up"], "w_down2": a["L1_ffn_w_down"],
        "ws_gate": a["L1_ffn_ws_gate"], "ws_up": a["L1_ffn_ws_up"], "ws_down": a["L1_ffn_ws_down"],
    }
    nc = _bacc.Bacc("TRN2", target_bir_lowering=False, num_devices=1)
    arrays, args = {}, []
    for name, value in laid_out.items():
        value = _np.ascontiguousarray(value)
        arrays[f"in_{name}_dram"] = value
        args.append(nc.dram_tensor(f"in_{name}_dram", value.shape, _mybir.dt.from_np(value.dtype),
                                   kind="ExternalInput").ap())
    out = nc.dram_tensor("out_dram", (TOKENS, C), F32, kind="ExternalOutput").ap()
    program(nc, *args, out)
    r = _run(nc, [arrays], core_ids=[0])
    return r.results[0]["out_dram"].reshape(BATCHES, SEQ, C)
```

```python
from contextlib import ExitStack

import concourse.bass as bass
from concourse import mybir

F32 = mybir.dt.float32
I32 = mybir.dt.int32
U32 = mybir.dt.uint32
ALU = mybir.AluOpType
ACT = mybir.ActivationFunctionType
AX = mybir.AxisListType

P = 128
C = 512
CC = C // P
TOKENS = 4096
TILES = TOKENS // P
LN_EPS = 1e-5

BATCHES = 8
SEQ = TOKENS // BATCHES
ST = SEQ // P
HEADS = 16
HD = C // HEADS
QUADS = HEADS // 4
ATTN_SCALE = float(HD) ** -0.5
ATTN_SHIFT = 0.1
ATTN_EPS = 1e-6


class Steps:

    def __init__(self, eng, sem, base=0):
        self.eng, self.sem, self.base, self.n = eng, sem, base, 0

    def mark(self, instruction):
        instruction.then_inc(self.sem, 1)
        self.n += 1

    def wait(self):
        self.eng.wait_ge(self.sem, self.base + self.n)


def constants(nc, ctx, ident, ones):
    set_up = ctx.enter_context(nc.semaphore("constants_set"))
    with nc.Block() as block:
        @block.gpsimd
        def _(pool):
            nc.gpsimd.memset(ident[:], 0.0).then_inc(set_up, 1)
            nc.gpsimd.memset(ones[:], 1.0).then_inc(set_up, 1)
            pool.wait_ge(set_up, 2)
            nc.gpsimd.affine_select(out=ident[:], in_=ident[:], compare_op=ALU.not_equal, fill=1.0, base=0,
                                    pattern=[[-1, P]], channel_multiplier=1)
            nc.gpsimd.affine_select(out=ones[:, P:2 * P], in_=ones[:, P:2 * P], compare_op=ALU.is_ge, fill=0.0,
                                    base=-1, pattern=[[1, P]], channel_multiplier=-1)


def layernorm_tiles(dve, steps, x_tile, stats, mean_var, n, carrier, one):
    for i in range(n):
        ins = dve.bn_stats(stats[:, i, :], x_tile(i))
    steps.mark(ins)
    steps.wait()
    dve.tensor_copy(carrier, one)
    for i in range(n):
        ins = dve.bn_aggr(mean_var[:, i, :], stats[:, i, :])
    return ins


def first_attention(nc, x_dram, wq, wk, wv, wo, X, ident, ones):
    with ExitStack() as ctx:
        sb = lambda name, shape: ctx.enter_context(nc.sbuf_tensor(name, shape, F32))
        sem = lambda name: ctx.enter_context(nc.semaphore(name))
        ps = lambda name, shape: ctx.enter_context(nc.psum_tensor(name, shape, F32))

        w_q, w_k, w_v, w_o = (sb(f"a_w{n}", [P, CC, C]) for n in "qkvo")
        stats = sb("a_stats", [P, ST, 6])
        mean_var = sb("a_mean_var", [P, ST, 2])
        std = sb("a_std", [P, ST])
        rstd = sb("a_rstd", [P, ST])
        eps = sb("a_eps", [P, 1])
        shift = sb("a_shift", [P, 1])
        carrier = sb("a_carrier", [P, 4])
        dve_carrier = sb("a_dve_carrier", [P, 1])
        xn = sb("a_xn", [P, ST, C])
        xnT = sb("a_xnT", [P, CC, SEQ])
        qT = sb("a_qT", [P, QUADS, SEQ])
        kT = sb("a_kT", [P, HEADS, SEQ])
        v = sb("a_v", [P, ST, C])
        w = sb("a_w", [P, 3, 4, SEQ])
        attnT = sb("a_attnT", [P, QUADS, SEQ])
        sums = sb("a_sums", [P, SEQ])

        pj = ps("a_pj", [P, 2, SEQ])
        sc = ps("a_sc", [P, 2, SEQ])
        num = ps("a_num", [P, 2, SEQ])
        den = ps("a_den", [P, 2, SEQ])

        x_loaded = sem("a_x_loaded")
        w_loaded = sem("a_w_loaded")
        zeroed = sem("a_zeroed")
        var_ready = sem("a_var_ready")
        std_ready = sem("a_std_ready")
        xn_ready = sem("a_xn_ready")
        pj_full = sem("a_pj_full")
        pj_taken = [sem("a_pj_taken0"), sem("a_pj_taken1")]
        sc_full = sem("a_sc_full")
        sc_taken = sem("a_sc_taken")
        w_masked = sem("a_w_masked")
        pv_done = sem("a_pv_done")
        attn_ready = sem("a_attn_ready")
        dve_steps = sem("a_dve_steps")

        T_PER = 20
        N_SC = QUADS * ST * 4
        N_STEP = QUADS * ST

        block = ctx.enter_context(nc.Block())

        @block.sync
        def _(sp):
            for b in range(BATCHES):
                if b >= 1:
                    sp.wait_ge(x_loaded, 16 * b)
                sp.dma_start(X[:, ST * b:ST * (b + 1), :],
                             x_dram.rearrange("(t p) c -> p t c", p=P)[:, ST * b:ST * (b + 1), :]).then_inc(x_loaded, 16)
                if b == 0:
                    for dst, src in ((w_q, wq), (w_k, wk), (w_v, wv), (w_o, wo)):
                        sp.dma_start(dst[:], src.rearrange("(c p) o -> p c o", p=P)).then_inc(w_loaded, 16)

        @block.gpsimd
        def _(pool):
            nc.gpsimd.memset(eps[:], LN_EPS).then_inc(zeroed, 1)
            nc.gpsimd.memset(shift[:], ATTN_SHIFT).then_inc(zeroed, 1)
            nc.gpsimd.memset(kT[:], 0.0).then_inc(zeroed, 1)

            def batch(b):
                for s in range(N_STEP):
                    kc = s % ST
                    pool.wait_ge(sc_taken, b * N_SC + 4 * s + 4)
                    nc.gpsimd.tensor_tensor(carrier[:, s % 4:s % 4 + 1], eps[:], eps[:], ALU.add)
                    diag = w[:, s % 3, :, P * kc:P * (kc + 1)]
                    nc.gpsimd.affine_select(out=diag, in_=diag, compare_op=ALU.is_ge, fill=0.0, base=0,
                                            pattern=[[0, 4], [1, P]], channel_multiplier=-1).then_inc(w_masked, 1)

            batch(0)
            with pool.Fori(1, BATCHES) as b:
                batch(b)

        @block.tensor
        def _(pe):
            def bank_free(n, b):
                pe.wait_ge(pj_taken[n % 2], b * (T_PER // 2) + ST // 2 + n // 2)

            def transposes(b, first):
                pe.wait_ge(xn_ready, b + 1)
                for c in range(CC):
                    n = -4 + c if first else 12 + c
                    if not first:
                        bank_free(n, b - 1)
                    elif c >= 2:
                        pe.wait_ge(pj_taken[c % 2], 1)
                    for i in range(ST):
                        ins = pe.transpose(pj[:, c % 2, P * i:P * (i + 1)], xn[:, i, P * c:P * (c + 1)], ident[:])
                    ins.then_inc(pj_full, 1)

            def project(u, b):
                bank_free(u, b)
                kind, j = divmod(u, 4)
                for c in range(CC):
                    if kind < 2:
                        ins = pe.matmul(pj[:, u % 2, :], (w_q, w_k)[kind][:, c, P * j:P * (j + 1)], xnT[:, c, :],
                                        start=(c == 0), stop=(c == CC - 1))
                    else:
                        ins = pe.matmul(pj[:, u % 2, :], xnT[:, c, P * j:P * (j + 1)], w_v[:, c, :],
                                        start=(c == 0), stop=(c == CC - 1))
                ins.then_inc(pj_full, 1)

            def scores(s, b, heads):
                quad, kc = divmod(s, ST)
                for r in heads:
                    m = 4 * s + r
                    if m >= 2:
                        pe.wait_ge(sc_taken, b * N_SC + m - 1)
                    pe.matmul(sc[:, m % 2, P * kc:SEQ], kT[:, 4 * quad + r, P * kc:P * (kc + 1)],
                              qT[:, quad, P * kc:SEQ], start=True, stop=True).then_inc(sc_full, 1)

            def numerators(s, b):
                quad, kc = divmod(s, ST)
                pe.wait_ge(w_masked, b * N_STEP + s + 1)
                if kc == 0 and quad >= 2:
                    pe.wait_ge(attn_ready, b * QUADS + quad - 1)
                for r in range(4):
                    h = 4 * quad + r
                    pe.matmul(num[32 * r:32 * r + 32, quad % 2, P * kc:SEQ], v[:, kc, HD * h:HD * (h + 1)],
                              w[:, s % 3, r, P * kc:SEQ], start=(kc == 0), stop=(kc == ST - 1), skip_group_check=True)

            def denominators(s):
                quad, kc = divmod(s, ST)
                for r in range(4):
                    ins = pe.matmul(den[32 * r:32 * r + 32, quad % 2, P * kc:SEQ], ones[:, 0:HD],
                                    w[:, s % 3, r, P * kc:SEQ], start=(kc == 0), stop=(kc == ST - 1),
                                    skip_group_check=True)
                ins.then_inc(pv_done, 1)

            def outputs(b, u):
                pe.wait_ge(attn_ready, (b + 1) * QUADS)
                for i in range(ST):
                    bank_free(u + i, b)
                    for c in range(QUADS):
                        ins = pe.matmul(pj[:, i % 2, :], attnT[:, c, P * i:P * (i + 1)], w_o[:, c, :],
                                        start=(c == 0), stop=(c == QUADS - 1))
                    ins.then_inc(pj_full, 1)

            def batch(b, last):
                for k in range(2):
                    pe.wait_ge(pj_taken[k], b * (T_PER // 2) + 2)
                for u in range(12):
                    project(u, b)
                for k in range(2):
                    pe.wait_ge(pj_taken[k], b * (T_PER // 2) + 8)
                for s in range(N_STEP + 2):
                    if s < N_STEP:
                        scores(s, b, (0, 1))
                    if s >= 2:
                        numerators(s - 2, b)
                    if s < N_STEP:
                        scores(s, b, (2, 3))
                    if s >= 2:
                        denominators(s - 2)
                if not last:
                    transposes(b + 1, False)
                outputs(b, 12 if last else 16)

            pe.wait_ge(w_loaded, 64)
            transposes(0, True)
            batch(0, False)
            with pe.Fori(1, BATCHES - 1) as b:
                batch(b, False)
            batch(BATCHES - 1, True)

        @block.scalar
        def _(act):
            def root(b):
                act.wait_ge(var_ready, b + 1)
                nc.scalar.activation(std[:], mean_var[:, :, 1], ACT.Sqrt, bias=eps[:]).then_inc(std_ready, 1)

            def take_xnT(b, c, n):
                act.wait_ge(pj_full, n)
                nc.scalar.copy(xnT[:, c, :], pj[:, c % 2, :]).then_inc(pj_taken[c % 2], 1)

            def batch(b, last):
                for u in range(0, 12, 2):
                    kind, j = divmod(u, 4)
                    act.wait_ge(pj_full, b * T_PER + 4 + u + 1)
                    if kind == 0:
                        nc.scalar.mul(qT[:, j, :], pj[:, 0, :], ATTN_SCALE).then_inc(pj_taken[0], 1)
                    elif kind == 1:
                        for r in range(4):
                            ins = nc.scalar.copy(kT[32 * r:32 * r + 32, 4 * j + r, :], pj[32 * r:32 * r + 32, 0, :])
                        ins.then_inc(pj_taken[0], 1)
                    else:
                        nc.scalar.copy(v[:, j, :], pj[:, 0, :]).then_inc(pj_taken[0], 1)
                if not last:
                    root(b + 1)
                for s in range(N_STEP):
                    kc = s % ST
                    if s >= 3:
                        act.wait_ge(pv_done, b * N_STEP + s - 2)
                    for r in range(4):
                        act.wait_ge(sc_full, b * N_SC + 4 * s + r + 1)
                        nc.scalar.activation(w[:, s % 3, r, P * kc:SEQ], sc[:, r % 2, P * kc:SEQ], ACT.Relu,
                                             bias=shift[:]).then_inc(sc_taken, 1)
                if not last:
                    for c in (0, 2):
                        take_xnT(b + 1, c, b * T_PER + 4 + 12 + c + 1)

            act.wait_ge(zeroed, 3)
            root(0)
            for c in (0, 2):
                take_xnT(0, c, c + 1)
            batch(0, False)
            with act.Fori(1, BATCHES - 1) as b:
                batch(b, False)
            batch(BATCHES - 1, True)

        @block.vector
        def _(dve):
            def normalise(b, steps):
                dve.wait_ge(x_loaded, b * 16 + 16)
                layernorm_tiles(dve, steps, lambda i: X[:, bass.ds(b * ST + i, 1), :].rearrange("p t c -> p (t c)"), stats, mean_var, ST,
                                dve_carrier[:], eps[:])\
                    .then_inc(var_ready, 1)
                dve.wait_ge(std_ready, b + 1)
                steps.mark(dve.reciprocal(rstd[:], std[:]))
                steps.wait()
                for i in range(ST):
                    ins = dve.tensor_scalar(xn[:, i, :], X[:, bass.ds(b * ST + i, 1), :].rearrange("p t c -> p (t c)"),
                                            mean_var[:, i, 0:1], rstd[:, i:i + 1], ALU.subtract, ALU.mult)
                ins.then_inc(xn_ready, 1)

            def take_xnT(c, n):
                dve.wait_ge(pj_full, n)
                dve.tensor_copy(xnT[:, c, :], pj[:, 1, :]).then_inc(pj_taken[1], 1)

            def divide(quad, b, steps):
                dve.wait_ge(pv_done, b * N_STEP + ST * (quad + 1))
                if quad >= 1:
                    dve.wait_ge(attn_ready, b * QUADS + quad)
                steps.mark(dve.tensor_scalar(sums[:], den[:, quad % 2, :], ATTN_EPS, None, ALU.add))
                steps.wait()
                steps.mark(dve.reciprocal(sums[:], sums[:]))
                steps.wait()
                dve.tensor_tensor(attnT[:, quad, :], num[:, quad % 2, :], sums[:], ALU.mult).then_inc(attn_ready, 1)

            PER_TURN = 2 * QUADS + 2

            def batch(b, last):
                steps = Steps(dve, dve_steps, b * PER_TURN + 2)
                for u in range(1, 12, 2):
                    kind, j = divmod(u, 4)
                    dve.wait_ge(pj_full, b * T_PER + 4 + u + 1)
                    if kind == 0:
                        dve.tensor_scalar(qT[:, j, :], pj[:, 1, :], ATTN_SCALE, None, ALU.mult).then_inc(pj_taken[1], 1)
                    elif kind == 1:
                        for r in range(4):
                            ins = dve.tensor_copy(kT[32 * r:32 * r + 32, 4 * j + r, :], pj[32 * r:32 * r + 32, 1, :])
                        ins.then_inc(pj_taken[1], 1)
                    else:
                        dve.tensor_copy(v[:, j, :], pj[:, 1, :]).then_inc(pj_taken[1], 1)
                if not last:
                    normalise(b + 1, steps)
                for quad in range(QUADS):
                    divide(quad, b, steps)
                if not last:
                    for c in (1, 3):
                        take_xnT(c, b * T_PER + 4 + 12 + c + 1)
                for i in range(ST):
                    dve.wait_ge(pj_full, b * T_PER + 4 + (12 if last else 16) + i + 1)
                    xt = X[:, bass.ds(b * ST + i, 1), :].rearrange("p t c -> p (t c)")
                    dve.tensor_tensor(xt, xt, pj[:, i % 2, :], ALU.add).then_inc(pj_taken[i % 2], 1)

            dve.wait_ge(zeroed, 3)
            normalise(0, Steps(dve, dve_steps))
            for c in (1, 3):
                take_xnT(c, c + 1)
            batch(0, False)
            with dve.Fori(1, BATCHES - 1) as b:
                batch(b, False)
            batch(BATCHES - 1, True)


E1 = 8
TOP1 = 2
H1 = 256
HC1 = H1 // P
HS1 = 512
HSC1 = HS1 // P
GROUP = 4
GROUPS = TILES // GROUP
MAX_TILES1 = (TOKENS * TOP1 + E1 * (P - 1)) // P
PAIRS1 = (MAX_TILES1 + 1) // 2
SLOTS1 = E1 * TOKENS + P * (2 * PAIRS1 - TOKENS * TOP1 // P)
ROWS = TOKENS + P


def tile_row(X, t):
    return X[:, bass.ds(t, 1), :].rearrange("p t c -> p (t c)")


def group_rows(x, g):
    return x.rearrange("(t p) c -> p t c", p=P)[:, GROUP * g:GROUP * (g + 1), :]


def first_ffn_shared(nc, X, ident, ones, before, gate_w, sh_gate, sh_up, sh_down, w_gate, w_up, w13, xs, table,
                     weight_all, slot_all, tile_expert, tile_slot):
    with ExitStack() as ctx:
        sb = lambda name, shape, dt=F32: ctx.enter_context(nc.sbuf_tensor(name, shape, dt))
        sem = lambda name: ctx.enter_context(nc.semaphore(name))
        ps = lambda name, shape: ctx.enter_context(nc.psum_tensor(name, shape, F32))

        w_g = sb("b_wg", [P, CC, HS1])
        w_u = sb("b_wu", [P, CC, HS1])
        w_d = sb("b_wd", [P, HSC1, C])
        w_route = sb("b_wroute", [P, CC, E1 + 1])
        eps = sb("b_eps", [P, 1])
        carrier = sb("b_carrier", [P, 8])
        empty = sb("b_empty", [P, SLOTS1 // P], U32)
        zrow = sb("b_zrow", [P, C])
        expert_iota = sb("b_expert_iota", [P, E1])
        region = sb("b_region", [P, E1])
        token_id = sb("b_token_id", [P, TILES])
        stats = sb("b_stats", [P, GROUP, 6])
        mean_var = sb("b_mean_var", [P, GROUP, 2])
        std = sb("b_std", [P, GROUP])
        rstd = sb("b_rstd", [P, GROUP])
        xn = sb("b_xn", [P, GROUP, C])
        xnT = sb("b_xnT", [P, CC, GROUP * P])
        hT = sb("b_hT", [P, HSC1, GROUP * P])
        sil = sb("b_sil", [P, 2, GROUP * P])
        logits = sb("b_logits", [P, GROUP, E1 + 1])
        best = sb("b_best", [P, GROUP, 8])
        best_i = sb("b_best_i", [P, GROUP, 8], U32)
        best_f = sb("b_best_f", [P, GROUP, TOP1])
        gap = sb("b_gap", [P, GROUP, 3])
        gates = sb("b_gates", [P, GROUP, 3])
        onehot = sb("b_onehot", [P, GROUP, TOP1, E1])
        chosen = sb("b_chosen", [P, GROUP, E1])
        total = sb("b_total", [P, E1])
        base = sb("b_base", [P, E1])
        place = sb("b_place", [P, GROUP, E1])
        picked = sb("b_picked", [P, GROUP, TOP1, E1])
        slot_f = sb("b_slot_f", [P, GROUP, TOP1])
        slot_now = sb("b_slot_now", [P, GROUP, TOP1], U32)
        token_now = sb("b_token_now", [P, GROUP], U32)
        n_tiles = sb("b_n_tiles", [P, E1])
        n_tiles_i = sb("b_n_tiles_i", [P, E1], I32)
        tiles_before = sb("b_tiles_before", [P, E1])
        tile_iota = sb("b_tile_iota", [P, 2 * PAIRS1])
        past = sb("b_past", [P, 2 * PAIRS1])
        t_expert = sb("b_t_expert", [P, 2 * PAIRS1])
        t_start = sb("b_t_start", [P, 2 * PAIRS1])
        expert_all = sb("b_expert_all", [P, TILES, TOP1])
        slot_all_f = sb("b_slot_all_f", [P, TILES, TOP1])
        shift = sb("b_shift", [P, E1])
        moved = sb("b_moved", [P, TILES, TOP1])

        up = ps("b_up", [P, 4, GROUP * P])
        pj = ps("b_pj", [P, 2, C])
        lg = ps("b_lg", [P, GROUP, E1 + 1])
        cnt = ps("b_cnt", [P, GROUP + 1, E1])

        w_loaded = sem("b_w_loaded")
        set_up = sem("b_set_up")
        rows_zeroed = sem("b_rows_zeroed")
        var_ready = sem("b_var_ready")
        std_ready = sem("b_std_ready")
        xn_ready = sem("b_xn_ready")
        xn_stored = sem("b_xn_stored")
        pj_full = sem("b_pj_full")
        pj_taken = [sem("b_pj_taken0"), sem("b_pj_taken1")]
        lg_full = sem("b_lg_full")
        gap_ready = sem("b_gap_ready")
        gates_ready = sem("b_gates_ready")
        chosen_ready = sem("b_chosen_ready")
        cnt_full = sem("b_cnt_full")
        up_full = sem("b_up_full")
        sil_ready = sem("b_sil_ready")
        h_ready = sem("b_h_ready")
        slots_ready = sem("b_slots_ready")
        scattered = sem("b_scattered")
        steps_sem = sem("b_steps")
        carried = sem("b_carried")
        SET_UP = 8

        block = ctx.enter_context(nc.Block())

        @block.sync
        def _(sp):
            sp.dma_start(w_route[:], gate_w.rearrange("(c p) e -> p c e", p=P)).then_inc(w_loaded, 16)
            for dst, src in ((w_g, sh_gate), (w_u, sh_up), (w_d, sh_down)):
                sp.dma_start(dst[:], src.rearrange("(c p) o -> p c o", p=P)).then_inc(w_loaded, 16)
            sp.wait_ge(set_up, SET_UP)
            sp.dma_start(table.rearrange("(p s) one -> p (s one)", p=P), empty[:]).then_inc(rows_zeroed, 16)
            sp.dma_start(xs[TOKENS:ROWS, :], zrow[:]).then_inc(rows_zeroed, 16)
            for e in range(E1):
                for k, src in enumerate((w_gate, w_up)):
                    sp.dma_start(w13[:, CC * e:CC * (e + 1), H1 * k:H1 * (k + 1)],
                                 src[e].rearrange("(c p) f -> p c f", p=P)).then_inc(before, 16)
            for g in range(GROUPS):
                sp.wait_ge(xn_ready, g + 1)
                sp.dma_start(group_rows(xs[0:TOKENS, :], g), xn[:]).then_inc(xn_stored, 16)
            sp.wait_ge(xn_stored, 16 * GROUPS)
            sp.wait_ge(rows_zeroed, 32)

        @block.gpsimd
        def _(pool):
            nc.gpsimd.memset(eps[:], LN_EPS).then_inc(set_up, 1)
            nc.gpsimd.memset(total[:], 0.0).then_inc(set_up, 1)
            nc.gpsimd.memset(zrow[:], 0.0).then_inc(set_up, 1)
            nc.gpsimd.iota(empty[:], [[0, SLOTS1 // P]], base=TOKENS, channel_multiplier=0).then_inc(set_up, 1)
            nc.gpsimd.iota(expert_iota[:], [[1, E1]], base=0, channel_multiplier=0,
                           allow_small_or_imprecise_dtypes=True).then_inc(set_up, 1)
            nc.gpsimd.iota(region[:], [[TOKENS, E1]], base=0, channel_multiplier=0,
                           allow_small_or_imprecise_dtypes=True).then_inc(set_up, 1)
            nc.gpsimd.iota(token_id[:], [[P, TILES]], base=0, channel_multiplier=1,
                           allow_small_or_imprecise_dtypes=True).then_inc(set_up, 1)
            nc.gpsimd.iota(tile_iota[:], [[1, 2 * PAIRS1]], base=0, channel_multiplier=0,
                           allow_small_or_imprecise_dtypes=True).then_inc(set_up, 1)
            pool.wait_ge(rows_zeroed, 32)
            pool.wait_ge(set_up, SET_UP)

            def turn(g):
                pool.wait_ge(slots_ready, g + 1)
                pool.wait_ge(carried, g)
                nc.gpsimd.tensor_tensor(carrier[:, 0:1], eps[:], eps[:], ALU.add).then_inc(carried, 1)
                for i in range(GROUP):
                    for k in range(TOP1):
                        nc.gpsimd.indirect_dma_start(
                            table, bass.IndirectOffsetOnAxis(ap=slot_now[:, i, k:k + 1], axis=0),
                            token_now[:, i:i + 1], None).then_inc(scattered, 16)

            turn(0)
            with pool.Fori(1, GROUPS) as g:
                turn(g)
            pool.wait_ge(scattered, 16 * GROUPS * GROUP * TOP1)

        PJ = 8

        @block.tensor
        def _(pe):
            def bank_free(u, g):
                pe.wait_ge(pj_taken[u % 2], g * (PJ // 2) + 2 + u // 2)

            def transposes(g, first):
                pe.wait_ge(xn_ready, g + 1)
                for c in range(CC):
                    if not first:
                        bank_free(c, g - 1)
                    elif c >= 2:
                        pe.wait_ge(pj_taken[c % 2], 1)
                    for i in range(GROUP):
                        ins = pe.transpose(pj[:, c % 2, P * i:P * (i + 1)], xn[:, i, P * c:P * (c + 1)], ident[:])
                    ins.then_inc(pj_full, 1)

            def group(g, last):
                for k in range(2):
                    pe.wait_ge(pj_taken[k], g * (PJ // 2) + 2)
                pe.wait_ge(chosen_ready, g)
                for i in range(GROUP):
                    for c in range(CC):
                        ins = pe.matmul(lg[:, i, :], xnT[:, c, P * i:P * (i + 1)], w_route[:, c, :],
                                        start=(c == 0), stop=(c == CC - 1))
                ins.then_inc(lg_full, 1)
                for f in range(HSC1):
                    pe.wait_ge(h_ready, g * HSC1 + f - 1) if f >= 1 else pe.wait_ge(h_ready, g * HSC1)
                    for k, w in ((0, w_g), (1, w_u)):
                        for c in range(CC):
                            ins = pe.matmul(up[:, 2 * (f % 2) + k, :], w[:, c, P * f:P * (f + 1)], xnT[:, c, :],
                                            start=(c == 0), stop=(c == CC - 1))
                    ins.then_inc(up_full, 1)
                pe.wait_ge(chosen_ready, g + 1)
                pe.wait_ge(slots_ready, g)
                for i in range(GROUP + 1):
                    for j in range(min(i + 1, GROUP)):
                        ins = pe.matmul(cnt[:, i, :], ones[:, P:2 * P] if j == i else ones[:, 0:P], chosen[:, j, :],
                                        start=(j == 0), stop=(j == min(i, GROUP - 1)))
                ins.then_inc(cnt_full, 1)
                if not last:
                    transposes(g + 1, False)
                pe.wait_ge(h_ready, (g + 1) * HSC1)
                for i in range(GROUP):
                    bank_free((0 if last else 4) + i, g)
                    for f in range(HSC1):
                        ins = pe.matmul(pj[:, i % 2, :], hT[:, f, P * i:P * (i + 1)], w_d[:, f, :],
                                        start=(f == 0), stop=(f == HSC1 - 1))
                    ins.then_inc(pj_full, 1)

            pe.wait_ge(w_loaded, 64)
            transposes(0, True)
            group(0, False)
            with pe.Fori(1, GROUPS - 1) as g:
                group(g, False)
            group(GROUPS - 1, True)

        @block.scalar
        def _(act):
            def root(g):
                act.wait_ge(var_ready, g + 1)
                nc.scalar.activation(std[:], mean_var[:, :, 1], ACT.Sqrt, bias=eps[:]).then_inc(std_ready, 1)

            def take_xnT(c, n):
                act.wait_ge(pj_full, n)
                nc.scalar.copy(xnT[:, c, :], pj[:, c % 2, :]).then_inc(pj_taken[c % 2], 1)

            def group(g, last):
                act.wait_ge(gap_ready, g + 1)
                nc.scalar.activation(gates[:], gap[:], ACT.Sigmoid).then_inc(gates_ready, 1)
                if not last:
                    root(g + 1)
                for f in range(HSC1):
                    act.wait_ge(up_full, g * HSC1 + f + 1)
                    act.wait_ge(h_ready, g * HSC1 + f - 1) if f >= 1 else act.wait_ge(h_ready, g * HSC1)
                    nc.scalar.activation(sil[:, f % 2, :], up[:, 2 * (f % 2), :], ACT.Silu).then_inc(sil_ready, 1)
                if not last:
                    for c in (0, 2):
                        take_xnT(c, g * PJ + 4 + c + 1)

            act.wait_ge(set_up, SET_UP)
            root(0)
            for c in (0, 2):
                take_xnT(c, c + 1)
            group(0, False)
            with act.Fori(1, GROUPS - 1) as g:
                group(g, False)
            group(GROUPS - 1, True)

        @block.vector
        def _(dve):
            def normalise(g, steps, first):
                layernorm_tiles(dve, steps, lambda i: tile_row(X, g * GROUP + i), stats, mean_var, GROUP,
                                carrier[:, 4:5], eps[:]).then_inc(var_ready, 1)
                dve.wait_ge(std_ready, g + 1)
                steps.mark(dve.reciprocal(rstd[:], std[:]))
                steps.wait()
                if not first:
                    dve.wait_ge(xn_stored, g * 16)
                for i in range(GROUP):
                    ins = dve.tensor_scalar(xn[:, i, :], tile_row(X, g * GROUP + i),
                                            mean_var[:, i, 0:1], rstd[:, i:i + 1], ALU.subtract, ALU.mult)
                ins.then_inc(xn_ready, 1)

            def take_xnT(c, n):
                dve.wait_ge(pj_full, n)
                dve.tensor_copy(xnT[:, c, :], pj[:, 1, :]).then_inc(pj_taken[1], 1)

            def choose(g, steps):
                dve.wait_ge(lg_full, g + 1)
                steps.mark(dve.tensor_copy(logits[:], lg[:]))
                steps.wait()
                dve.tensor_copy(carrier[:, 5:6], eps[:])
                for i in range(GROUP):
                    ins = dve.max(best[:, i, :], logits[:, i, 0:E1])
                steps.mark(ins)
                steps.wait()
                dve.tensor_copy(carrier[:, 6:7], eps[:])
                for i in range(GROUP):
                    ins = dve.max_index(best_i[:, i, :], best[:, i, :], logits[:, i, 0:E1])
                steps.mark(ins)
                dve.tensor_tensor(gap[:, :, 0], best[:, :, 0], best[:, :, 1], ALU.subtract)
                dve.tensor_tensor(gap[:, :, 1], best[:, :, 1], best[:, :, 0], ALU.subtract)
                dve.tensor_copy(gap[:, :, 2], logits[:, :, E1]).then_inc(gap_ready, 1)
                steps.wait()
                steps.mark(dve.tensor_copy(best_f[:], best_i[:, :, 0:TOP1]))
                steps.wait()
                for k in range(TOP1):
                    ins = dve.tensor_tensor(onehot[:, :, k, :], expert_iota[:].unsqueeze(1).broadcast_to([P, GROUP, E1]),
                                            best_f[:, :, k:k + 1].broadcast_to([P, GROUP, E1]), ALU.is_equal)
                steps.mark(ins)
                steps.wait()
                dve.tensor_tensor(chosen[:], onehot[:, :, 0, :], onehot[:, :, 1, :], ALU.add).then_inc(chosen_ready, 1)

            def place_slots(g, steps):
                steps.mark(dve.tensor_tensor(base[:], total[:], region[:], ALU.add))
                dve.wait_ge(cnt_full, g + 1)
                steps.wait()
                steps.mark(dve.tensor_tensor(place[:], cnt[:, 0:GROUP, :],
                                             base[:].unsqueeze(1).broadcast_to([P, GROUP, E1]), ALU.add))
                steps.mark(dve.tensor_tensor(total[:], total[:], cnt[:, GROUP, :], ALU.add))
                steps.wait()
                for k in range(TOP1):
                    ins = dve.tensor_tensor(picked[:, :, k, :], onehot[:, :, k, :], place[:], ALU.mult)
                steps.mark(ins)
                steps.wait()
                steps.mark(dve.tensor_reduce(slot_f[:], picked[:], AX.X, ALU.add))
                steps.wait()
                dve.wait_ge(scattered, g * (16 * GROUP * TOP1))
                dve.tensor_copy(token_now[:], token_id[:, bass.ds(g * GROUP, GROUP)])
                dve.tensor_copy(slot_all_f[:, bass.ds(g * GROUP, GROUP), :], slot_f[:])
                dve.tensor_copy(expert_all[:, bass.ds(g * GROUP, GROUP), :], best_f[:])
                dve.tensor_copy(slot_now[:], slot_f[:]).then_inc(slots_ready, 1)
                dve.wait_ge(gates_ready, g + 1)
                steps.mark(dve.tensor_copy(weight_all[:, bass.ds(g * GROUP, GROUP), :], gates[:, :, 0:TOP1]))

            PER_TURN = 13

            def group(g, last):
                steps = Steps(dve, steps_sem, g * PER_TURN + 2)
                choose(g, steps)
                if not last:
                    normalise(g + 1, steps, False)
                for f in range(HSC1):
                    dve.wait_ge(sil_ready, g * HSC1 + f + 1)
                    dve.tensor_tensor(hT[:, f, :], sil[:, f % 2, :], up[:, 2 * (f % 2) + 1, :], ALU.mult)\
                        .then_inc(h_ready, 1)
                place_slots(g, steps)
                assert steps.n == PER_TURN - (2 if last else 0), steps.n
                if not last:
                    for c in (1, 3):
                        take_xnT(c, g * PJ + 4 + c + 1)
                for i in range(GROUP):
                    dve.wait_ge(pj_full, g * PJ + 4 + (0 if last else 4) + i + 1)
                    dve.scalar_tensor_tensor(out=tile_row(X, g * GROUP + i), in0=pj[:, i % 2, :],
                                             scalar=gates[:, i, 2:3], in1=tile_row(X, g * GROUP + i),
                                             op0=ALU.mult, op1=ALU.add).then_inc(pj_taken[i % 2], 1)
                return steps

            dve.wait_ge(set_up, SET_UP)
            normalise(0, Steps(dve, steps_sem), True)
            for c in (1, 3):
                take_xnT(c, c + 1)
            group(0, False)
            with dve.Fori(1, GROUPS - 1) as g:
                group(g, False)
            steps = group(GROUPS - 1, True)

            steps.mark(dve.tensor_scalar(n_tiles[:], total[:], float(P - 1), None, ALU.add))
            steps.wait()
            steps.mark(dve.tensor_copy(n_tiles_i[:], n_tiles[:]))
            steps.wait()
            steps.mark(dve.tensor_scalar(n_tiles_i[:], n_tiles_i[:], P.bit_length() - 1, None, ALU.arith_shift_right))
            steps.wait()
            steps.mark(dve.tensor_copy(n_tiles[:], n_tiles_i[:]))
            steps.wait()
            steps.mark(dve.tensor_copy(tiles_before[:, 0:1], n_tiles[:, 0:1]))
            for e in range(1, E1):
                steps.wait()
                steps.mark(dve.tensor_tensor(tiles_before[:, e:e + 1], tiles_before[:, e - 1:e], n_tiles[:, e:e + 1],
                                             ALU.add))
            steps.mark(dve.memset(t_expert[:], 0.0))
            steps.mark(dve.tensor_copy(t_start[:], tile_iota[:]))
            for e in range(E1):
                steps.wait()
                steps.mark(dve.tensor_scalar(past[:], tile_iota[:], tiles_before[:, e:e + 1], None, ALU.is_ge))
                steps.wait()
                steps.mark(dve.tensor_tensor(t_expert[:], t_expert[:], past[:], ALU.add))
                steps.mark(dve.tensor_scalar(past[:], past[:], n_tiles[:, e:e + 1], None, ALU.mult))
                steps.wait()
                steps.mark(dve.tensor_tensor(t_start[:], t_start[:], past[:], ALU.subtract))
            steps.wait()
            steps.mark(dve.tensor_scalar(past[:], t_expert[:], float(TOKENS // P), None, ALU.mult))
            steps.wait()
            steps.mark(dve.tensor_tensor(t_start[:], t_start[:], past[:], ALU.add))
            steps.wait()
            steps.mark(dve.tensor_scalar(t_start[:], t_start[:], float(P), None, ALU.mult))
            steps.mark(dve.tensor_scalar(t_expert[:], t_expert[:], float(E1 - 1), None, ALU.min))
            steps.wait()
            dve.tensor_copy(tile_slot[:], t_start[:])
            dve.tensor_copy(tile_expert[:], t_expert[:])

            steps.mark(dve.tensor_tensor(shift[:], tiles_before[:], n_tiles[:], ALU.subtract))
            steps.wait()
            steps.mark(dve.tensor_scalar(shift[:], shift[:], float(P), None, ALU.mult))
            steps.wait()
            steps.mark(dve.tensor_tensor(shift[:], shift[:], region[:], ALU.subtract))
            for e in range(E1):
                steps.wait()
                steps.mark(dve.tensor_scalar(moved[:], expert_all[:], float(e), shift[:, e:e + 1],
                                             ALU.is_equal, ALU.mult))
                steps.wait()
                steps.mark(dve.tensor_tensor(slot_all_f[:], slot_all_f[:], moved[:], ALU.add))
            steps.wait()
            dve.tensor_copy(slot_all[:], slot_all_f[:])


def first_ffn_experts(nc, ident, w13, w13_loaded, w2, w_down, xs, table, ys, tile_expert, tile_slot):
    with ExitStack() as ctx:
        sb = lambda name, shape, dt=F32: ctx.enter_context(nc.sbuf_tensor(name, shape, dt))
        sem = lambda name: ctx.enter_context(nc.semaphore(name))
        ps = lambda name, shape: ctx.enter_context(nc.psum_tensor(name, shape, F32))

        ids = sb("c_ids", [P, 2, 1], U32)
        xg = sb("c_xg", [P, 2, C])
        xgT = sb("c_xgT", [P, 2, CC * P])
        sil = sb("c_sil", [P, 2, H1])
        h = sb("c_h", [P, 2, H1])
        hT = sb("c_hT", [P, 2, HC1 * P])
        y = sb("c_y", [P, 2, C])
        carrier = sb("c_carrier", [P, 2])

        up = ps("c_up", [P, 2, 2 * H1])
        yp = ps("c_yp", [P, 2, C])
        xp = ps("c_xp", [P, 2, CC * P])
        hp = ps("c_hp", [P, 2, 512])

        w2_loaded = sem("c_w2_loaded")
        ids_loaded = [sem("c_ids_loaded0"), sem("c_ids_loaded1")]
        gathered = [sem("c_gathered0"), sem("c_gathered1")]
        stored = [sem("c_stored0"), sem("c_stored1")]
        x_turned = sem("c_x_turned")
        xgT_ready = sem("c_xgT_ready")
        up_full = sem("c_up_full")
        sil_ready = sem("c_sil_ready")
        h_ready = sem("c_h_ready")
        h_turned = sem("c_h_turned")
        hT_ready = sem("c_hT_ready")
        y_full = sem("c_y_full")
        y_ready = sem("c_y_ready")
        carried = sem("c_carried")
        N = 2 * PAIRS1

        def turns(eng, tile):
            for p in range(2):
                tile(0, p, "first")
            for p in range(2):
                tile(1, p, "")
            with eng.Fori(2, PAIRS1 - 1) as ii:
                for p in range(2):
                    tile(ii, p, "")
            for p in range(2):
                tile(PAIRS1 - 1, p, "last")

        block = ctx.enter_context(nc.Block())

        @block.sync
        def _(sp):
            for e in range(E1):
                sp.dma_start(w2[:, HC1 * e:HC1 * (e + 1), :],
                             w_down[e].rearrange("(c p) o -> p c o", p=P)).then_inc(w2_loaded, 16)

        @block.gpsimd
        def _(pool):
            def load_ids(ii, p, start):
                slot = pool.value_load(tile_slot[0:1, bass.ds(ii * 2 + p, 1)], min_val=0, max_val=SLOTS1 - P)
                if not start:
                    pool.wait_ge(gathered[p], ii * 16)
                pool.dma_start(ids[:, p, :], table[bass.ds(slot, P), :]).then_inc(ids_loaded[p], 16)

            def tile(ii, p, which):
                if not (which == "last" and p == 1):
                    load_ids(ii + 1 if p else ii, 1 - p, which == "first" and p == 0)
                pool.wait_ge(ids_loaded[p], ii * 16 + 16)
                if which != "first":
                    pool.wait_ge(x_turned, ii * 2 + p - 1)
                pool.wait_ge(carried, ii * 2 + p)
                nc.gpsimd.tensor_tensor(carrier[:, 0:1], ident[:, 0:1], ident[:, 0:1], ALU.add).then_inc(carried, 1)
                nc.gpsimd.indirect_dma_start(xg[:, p, :], None, xs,
                                             bass.IndirectOffsetOnAxis(ap=ids[:, p, :], axis=0)).then_inc(gathered[p], 16)

            load_ids(0, 0, True)
            turns(pool, tile)

        @block.tensor
        def _(pe):
            def turn_x(ii, p, start):
                pe.wait_ge(gathered[p], ii * 16 + 16)
                if not start:
                    pe.wait_ge(xgT_ready, ii * 2 + p - 1)
                for c in range(CC):
                    ins = pe.transpose(xp[:, p, P * c:P * (c + 1)], xg[:, p, P * c:P * (c + 1)], ident[:])
                ins.then_inc(x_turned, 1)

            def load_expert(ii, p):
                return pe.value_load(tile_expert[0:1, bass.ds(ii * 2 + p, 1)], min_val=0, max_val=E1 - 1)

            def turn_h(ii, p, start):
                pe.wait_ge(h_ready, ii * 2 + p + 1)
                if not start:
                    pe.wait_ge(hT_ready, ii * 2 + p - 1)
                for f in range(HC1):
                    ins = pe.transpose(hp[:, p, P * f:P * (f + 1)], h[:, p, P * f:P * (f + 1)], ident[:])
                ins.then_inc(h_turned, 1)

            def down(ii, p, start, e):
                pe.wait_ge(hT_ready, ii * 2 + p + 1)
                if not start:
                    pe.wait_ge(y_ready, ii * 2 + p - 1)
                for f in range(HC1):
                    ins = pe.matmul(yp[:, p, :], hT[:, p, P * f:P * (f + 1)],
                                    w2[:, bass.ds(e * HC1 + f, 1), :].rearrange("p a c -> p (a c)"),
                                    start=(f == 0), stop=(f == HC1 - 1))
                ins.then_inc(y_full, 1)

            def tile(ii, p, which):
                first = which == "first" and p == 0
                before = (ii if p else ii - 1, 1 - p)
                e = load_expert(ii, p)
                if not first:
                    e_before = load_expert(*before)
                pe.wait_ge(xgT_ready, ii * 2 + p + 1)
                if which != "first":
                    pe.wait_ge(h_ready, ii * 2 + p - 1)
                for c in range(CC):
                    ins = pe.matmul(up[:, p, :], xgT[:, p, P * c:P * (c + 1)],
                                    w13[:, bass.ds(e * CC + c, 1), :].rearrange("p a f -> p (a f)"),
                                    start=(c == 0), stop=(c == CC - 1))
                    if c == 1 and not first:
                        turn_h(*before, which == "first")
                ins.then_inc(up_full, 1)
                if not (which == "last" and p == 1):
                    turn_x(ii + 1 if p else ii, 1 - p, first)
                if not first:
                    if which == "first":
                        pe.wait_ge(w2_loaded, 16 * E1)
                    down(*before, which == "first", e_before)

            turn_x(0, 0, True)
            pe.wait_ge(w13_loaded, 16 * 2 * E1)
            turns(pe, tile)
            turn_h(PAIRS1 - 1, 1, False)
            down(PAIRS1 - 1, 1, False, load_expert(PAIRS1 - 1, 1))

        @block.scalar
        def _(act):
            def take_x(ii, p, start):
                act.wait_ge(x_turned, ii * 2 + p + 1)
                if not start:
                    act.wait_ge(up_full, ii * 2 + p - 1)
                nc.scalar.copy(xgT[:, p, :], xp[:, p, :]).then_inc(xgT_ready, 1)

            def store(ii, p):
                act.wait_ge(y_ready, ii * 2 + p + 1)
                act.dma_start(ys[bass.ds(ii * (2 * P) + p * P, P), :], y[:, p, :]).then_inc(stored[p], 16)

            def tile(ii, p, which):
                act.wait_ge(up_full, ii * 2 + p + 1)
                if which != "first":
                    act.wait_ge(h_ready, ii * 2 + p - 1)
                nc.scalar.activation(sil[:, p, :], up[:, p, 0:H1], ACT.Silu).then_inc(sil_ready, 1)
                if not (which == "last" and p == 1):
                    take_x(ii + 1 if p else ii, 1 - p, which == "first" and p == 0)

                if which != "first":
                    store(ii - 1, p)

            take_x(0, 0, True)
            turns(act, tile)
            for p in range(2):
                store(PAIRS1 - 1, p)
            for p in range(2):
                act.wait_ge(stored[p], 16 * PAIRS1)

        @block.vector
        def _(dve):
            def take_y(ii, p, start):
                dve.wait_ge(y_full, ii * 2 + p + 1)
                if not start:
                    dve.wait_ge(stored[p], ii * 16)
                dve.tensor_copy(y[:, p, :], yp[:, p, :]).then_inc(y_ready, 1)

            def take_h(ii, p, start):
                dve.wait_ge(h_turned, ii * 2 + p + 1)
                if not start:
                    dve.wait_ge(y_full, ii * 2 + p - 1)
                dve.tensor_copy(hT[:, p, :], hp[:, p, 0:HC1 * P]).then_inc(hT_ready, 1)

            def tile(ii, p, which):
                before = (ii if p else ii - 1, 1 - p)
                first = which == "first" and p == 0
                if not first:
                    take_h(*before, which == "first")
                dve.wait_ge(sil_ready, ii * 2 + p + 1)
                if which != "first":
                    dve.wait_ge(h_turned, ii * 2 + p - 1)
                dve.tensor_tensor(h[:, p, :], sil[:, p, :], up[:, p, H1:2 * H1], ALU.mult).then_inc(h_ready, 1)
                if not first:
                    take_y(*before, which == "first")

            turns(dve, tile)
            take_h(PAIRS1 - 1, 1, False)
            take_y(PAIRS1 - 1, 1, False)


POS = 8
CHUNKS = TILES // POS


def second_attention(nc, X, ident, ones, ys, slot_all, weight_all, w_qkv, w_out):
    with ExitStack() as ctx:
        sb = lambda name, shape, dt=F32: ctx.enter_context(nc.sbuf_tensor(name, shape, dt))
        sem = lambda name: ctx.enter_context(nc.semaphore(name))
        ps = lambda name, shape: ctx.enter_context(nc.psum_tensor(name, shape, F32))

        w_p = sb("d_wqkv", [P, CC, 3 * C])
        w_o = sb("d_wo", [P, CC, C])
        minus_half = sb("d_minus_half", [P, 1])
        carrier = sb("d_carrier", [P, 4])
        slot_now = sb("d_slot_now", [P, POS, TOP1], U32)
        y = sb("d_y", [P, 2, TOP1, C])
        stats = sb("d_stats", [P, 6])
        mean_var = sb("d_mean_var", [P, POS, 2])
        rstd = sb("d_rstd", [P, POS])
        xn = sb("d_xn", [P, 2, C])
        xnT = sb("d_xnT", [P, 2, C])
        q = sb("d_q", [P, 2, C])
        k = sb("d_k", [P, 2 * POS, C])
        v = sb("d_v", [P, 2 * POS, C])
        prod = sb("d_prod", [P, POS, C])
        s = sb("d_s", [P, POS, HEADS])
        e = sb("d_e", [P, POS, HEADS])
        most = sb("d_most", [P, HEADS])
        ao = sb("d_ao", [P, 2, C])
        aoT = sb("d_aoT", [P, 2, C])

        qkv_p = ps("d_qkv_p", [P, 3, C])
        xp = ps("d_xp", [P, C])
        ap = ps("d_ap", [P, C])
        op = ps("d_op", [P, 2, C])

        w_loaded = sem("d_w_loaded")
        set_up = sem("d_set_up")
        slots_ready = sem("d_slots_ready")
        gathered = [sem("d_gathered0"), sem("d_gathered1")]
        combined = sem("d_combined")
        var_ready = sem("d_var_ready")
        rstd_ready = sem("d_rstd_ready")
        xn_ready = sem("d_xn_ready")
        x_turned = sem("d_x_turned")
        xnT_ready = sem("d_xnT_ready")
        qkv_full = sem("d_qkv_full")
        qkv_ready = sem("d_qkv_ready")
        s_ready = sem("d_s_ready")
        e_ready = sem("d_e_ready")
        ao_ready = sem("d_ao_ready")
        a_turned = sem("d_a_turned")
        aoT_ready = sem("d_aoT_ready")
        o_full = sem("d_o_full")
        o_taken = sem("d_o_taken")
        steps_sem = sem("d_steps")
        carried = sem("d_carried")

        block = ctx.enter_context(nc.Block())

        def chunks(eng, chunk):
            chunk(0, "first")
            with eng.Fori(1, CHUNKS - 1) as ch:
                chunk(ch, "")
            chunk(CHUNKS - 1, "last")

        @block.sync
        def _(sp):
            sp.dma_start(w_p[:], w_qkv.rearrange("(c p) o -> p c o", p=P)).then_inc(w_loaded, 16)
            sp.dma_start(w_o[:], w_out.rearrange("(c p) o -> p c o", p=P)).then_inc(w_loaded, 16)
            sp.wait_ge(w_loaded, 32)

        @block.gpsimd
        def _(pool):
            nc.gpsimd.memset(minus_half[:], -0.5).then_inc(set_up, 1)
            pool.wait_ge(set_up, 1)

            def gather(m, l, slots):
                pool.wait_ge(slots_ready, slots)
                if not (isinstance(m, int) and m < 2):
                    pool.wait_ge(combined, m - 1)
                pool.wait_ge(carried, m)
                nc.gpsimd.tensor_tensor(carrier[:, 0:1], minus_half[:], minus_half[:], ALU.add).then_inc(carried, 1)
                for t in range(TOP1):
                    nc.gpsimd.indirect_dma_start(y[:, l % 2, t, :], None, ys, bass.IndirectOffsetOnAxis(
                        ap=slot_now[:, l, t:t + 1], axis=0)).then_inc(gathered[l % 2], 16)

            def root(m, l):
                pool.wait_ge(var_ready, m + 1)
                nc.gpsimd.tensor_tensor(rstd[:, l:l + 1], mean_var[:, l, 1:2], minus_half[:], ALU.pow)\
                    .then_inc(rstd_ready, 1)

            def chunk(ch, which):
                for l in range(POS):
                    m = ch * POS + l
                    gather(m, l, ch + 1)
                    if not (which == "first" and l == 0):
                        root(m - 1, (l - 1) % POS)

            chunks(pool, chunk)
            root(TILES - 1, POS - 1)

        @block.tensor
        def _(pe):
            def turn_x(n, l):
                pe.wait_ge(xn_ready, n + 1)
                pe.wait_ge(xnT_ready, n)
                for c in range(CC):
                    ins = pe.transpose(xp[:, P * c:P * (c + 1)], xn[:, l % 2, P * c:P * (c + 1)], ident[:])
                ins.then_inc(x_turned, 1)

            def project(n, l, j, start):
                if not start:
                    pe.wait_ge(qkv_ready, n * 3 - 2 + j)
                for c in range(CC):
                    ins = pe.matmul(qkv_p[:, j, :], xnT[:, l % 2, P * c:P * (c + 1)], w_p[:, c, C * j:C * (j + 1)],
                                    start=(c == 0), stop=(c == CC - 1))
                ins.then_inc(qkv_full, 1)

            def turn_a(n, l):
                pe.wait_ge(ao_ready, n + 1)
                pe.wait_ge(aoT_ready, n)
                for c in range(CC):
                    ins = pe.transpose(ap[:, P * c:P * (c + 1)], ao[:, l % 2, P * c:P * (c + 1)], ident[:])
                ins.then_inc(a_turned, 1)

            def output(n, l, start):
                pe.wait_ge(aoT_ready, n + 1)
                if not start:
                    pe.wait_ge(o_taken, n - 1)
                for c in range(CC):
                    ins = pe.matmul(op[:, l % 2, :], aoT[:, l % 2, P * c:P * (c + 1)], w_o[:, c, :],
                                    start=(c == 0), stop=(c == CC - 1))
                ins.then_inc(o_full, 1)

            def chunk(ch, which):
                for l in range(POS):
                    n = ch * POS + l
                    early = which == "first" and l < 2
                    pe.wait_ge(xnT_ready, n + 1)
                    project(n, l, 0, which == "first" and l == 0)
                    if not (which == "last" and l == POS - 1):
                        turn_x(n + 1, l + 1)
                    project(n, l, 1, which == "first" and l == 0)
                    if not early:
                        turn_a(n - 2, l)
                    project(n, l, 2, which == "first" and l == 0)
                    if not early:
                        output(n - 2, l, which == "first" and l < 4)

            pe.wait_ge(w_loaded, 32)
            turn_x(0, 0)
            chunks(pe, chunk)
            for n in (TILES - 2, TILES - 1):
                turn_a(n, n)
                output(n, n, False)

        @block.scalar
        def _(act):
            def take_x(n, l):
                act.wait_ge(x_turned, n + 1)
                nc.scalar.copy(xnT[:, l % 2, :], xp[:]).then_inc(xnT_ready, 1)

            def take_qkv(n, l, j, side, start):
                act.wait_ge(qkv_full, n * 3 + j + 1)
                if j == 0:
                    if not start:
                        act.wait_ge(s_ready, n - 1)
                    nc.scalar.mul(q[:, l % 2, :], qkv_p[:, 0, :], ATTN_SCALE).then_inc(qkv_ready, 1)
                else:
                    nc.scalar.copy(tile_row((k, v)[j - 1], side * POS + l), qkv_p[:, j, :]).then_inc(qkv_ready, 1)

            def exps(n, l):
                act.wait_ge(s_ready, n + 1)
                nc.scalar.activation(e[:, 0:l + 1, :], s[:, 0:l + 1, :], ACT.Exp).then_inc(e_ready, 1)

            def take_a(n, l):
                act.wait_ge(a_turned, n + 1)
                nc.scalar.copy(aoT[:, l % 2, :], ap[:]).then_inc(aoT_ready, 1)

            def chunk(ch, which):
                side = ch % 2
                for l in range(POS):
                    n = ch * POS + l
                    early = which == "first" and l < 2
                    take_qkv(n, l, 0, side, early)
                    if not (which == "last" and l == POS - 1):
                        take_x(n + 1, l + 1)
                    take_qkv(n, l, 1, side, early)
                    if not (which == "first" and l == 0):
                        exps(n - 1, (l - 1) % POS)
                    if not early:
                        take_a(n - 2, l)
                    take_qkv(n, l, 2, side, early)
                exps_last = which == "last"
                if exps_last:
                    exps(TILES - 1, POS - 1)

            take_x(0, 0)
            chunks(act, chunk)
            for n in (TILES - 2, TILES - 1):
                take_a(n, n)

        @block.vector
        def _(dve):
            def tile(ch, l):
                return tile_row(X, ch + l // POS + (l % POS) * CHUNKS)

            def carry(column):
                dve.tensor_copy(carrier[:, column:column + 1], minus_half[:])

            def slots(ch, first):
                by_chunk = slot_all[:].rearrange("p (l ch) t -> p l ch t", ch=CHUNKS)
                if not first:
                    for p in range(2):
                        dve.wait_ge(gathered[p], ch * (16 * TOP1 * POS // 2))
                    carry(1)
                dve.tensor_copy(slot_now[:], by_chunk[:, :, bass.ds(ch, 1), :].rearrange("p l c t -> p l (c t)"))\
                    .then_inc(slots_ready, 1)

            def combine(ch, l, steps):
                m = ch * POS + l
                x = tile(ch, l)
                dve.wait_ge(gathered[l % 2], (ch * (POS // 2) + l // 2 + 1) * (16 * TOP1))
                for t in range(TOP1):
                    weight = weight_all[:, bass.ds(ch + l * CHUNKS, 1), t:t + 1].rearrange("p a b -> p (a b)")
                    ins = dve.scalar_tensor_tensor(out=x, in0=y[:, l % 2, t, :], scalar=weight, in1=x,
                                                   op0=ALU.mult, op1=ALU.add)
                    if t == TOP1 - 1:
                        ins.then_inc(combined, 1)
                        dve.wait_ge(combined, m + 1)
                        carry(3)
                    else:
                        steps.mark(ins)
                        steps.wait()
                steps.mark(dve.bn_stats(stats[:], x))
                steps.wait()
                carry(2)
                steps.mark(dve.bn_aggr(mean_var[:, l, :], stats[:]))
                steps.wait()
                dve.tensor_scalar(mean_var[:, l, 1:2], mean_var[:, l, 1:2], LN_EPS, None, ALU.add)\
                    .then_inc(var_ready, 1)

            def normalise(ch, l, start):
                n = ch * POS + l
                dve.wait_ge(rstd_ready, n + 1)
                if not start:
                    dve.wait_ge(x_turned, n - 1)
                at = l % POS
                dve.tensor_scalar(xn[:, l % 2, :], tile(ch, l), mean_var[:, at, 0:1],
                                  rstd[:, at:at + 1], ALU.subtract, ALU.mult).then_inc(xn_ready, 1)

            def take_output(n, x, l):
                dve.wait_ge(o_full, n + 1)
                dve.tensor_tensor(x, x, op[:, l % 2, :], ALU.add).then_inc(o_taken, 1)

            def scores(n, l, side, start, steps):
                m = l + 1
                dve.wait_ge(qkv_ready, n * 3 + 2)
                if not start:
                    dve.wait_ge(ao_ready, n)
                steps.mark(dve.tensor_tensor(prod[:, 0:m, :], k[:, bass.ds(side * POS, m), :],
                                             q[:, l % 2:l % 2 + 1, :].broadcast_to([P, m, C]), ALU.mult))
                steps.wait()
                steps.mark(dve.tensor_reduce(s[:, 0:m, :], prod[:, 0:m, :].rearrange("p m (h d) -> p m h d", h=HEADS),
                                             AX.X, ALU.add))
                steps.wait()
                steps.mark(dve.tensor_reduce(most[:], s[:, 0:m, :].rearrange("p m h -> p h m"), AX.X, ALU.max))
                steps.wait()
                dve.tensor_tensor(s[:, 0:m, :], s[:, 0:m, :], most[:].unsqueeze(1).broadcast_to([P, m, HEADS]),
                                  ALU.subtract).then_inc(s_ready, 1)

            def average(n, l, side, start, steps):
                m = l + 1
                dve.wait_ge(e_ready, n + 1)
                steps.mark(dve.tensor_reduce(most[:], e[:, 0:m, :].rearrange("p m h -> p h m"), AX.X, ALU.add))
                steps.wait()
                steps.mark(dve.reciprocal(most[:], most[:]))
                steps.wait()
                steps.mark(dve.tensor_tensor(e[:, 0:m, :], e[:, 0:m, :],
                                             most[:].unsqueeze(1).broadcast_to([P, m, HEADS]), ALU.mult))
                steps.wait()
                dve.wait_ge(qkv_ready, n * 3 + 3)
                vs = v[:, bass.ds(side * POS, m), :].rearrange("p m (h d) -> p m h d", h=HEADS)
                steps.mark(dve.tensor_tensor(prod[:, 0:m, :].rearrange("p m (h d) -> p m h d", h=HEADS), vs,
                                             e[:, 0:m, :].unsqueeze(3).broadcast_to([P, m, HEADS, HD]), ALU.mult))
                steps.wait()
                if not start:
                    dve.wait_ge(a_turned, n - 1)
                dve.tensor_reduce(ao[:, l % 2, :], prod[:, 0:m, :].rearrange("p m c -> p c m"), AX.X, ALU.add)\
                    .then_inc(ao_ready, 1)

            FIRST = 3 * POS
            PER_TURN = POS * 10

            def chunk(ch, which):
                side = ch % 2
                steps = Steps(dve, steps_sem, ch * PER_TURN + FIRST)
                if which != "last":
                    slots(ch + 1, False)
                for l in range(POS):
                    n = ch * POS + l
                    early = which == "first" and l < 2
                    scores(n, l, side, which == "first" and l == 0, steps)
                    if not (which == "last" and l >= POS - 2):
                        normalise(ch, l + 2, False)
                    if not early:
                        take_output(n - 2, tile(ch, l - 2) if l >= 2 else tile(ch - 1, l + POS - 2), l)
                    if which != "last":
                        combine(ch + 1, l, steps)
                    average(n, l, side, early, steps)
                if which != "last":
                    assert steps.n == PER_TURN, steps.n

            dve.wait_ge(set_up, 1)
            slots(0, True)
            steps = Steps(dve, steps_sem)
            for l in range(POS):
                combine(0, l, steps)
                if 1 <= l <= 2:
                    normalise(0, l - 1, True)
            assert steps.n == FIRST, steps.n
            chunks(dve, chunk)
            for l in (POS - 2, POS - 1):
                take_output((CHUNKS - 1) * POS + l, tile(CHUNKS - 1, l), l)


E2 = 64
TOP2 = 6
SETS = 8
TOP_SETS = 4
PER_SET = E2 // SETS
H2 = 192
HH2 = H2 // 2
ROUTE_SCALE = 2.5
CAP = 2 * (512 * TOP2 // E2)
SLOTS2 = E2 * CAP
ROWS2 = TOKENS + CAP
XC = C + E2
FAR = 3.0e38
NO_SLOT = 1.0e6
RING = 4
ROWS_RING = 2 * RING
AHEAD = 4


def second_ffn_shared(nc, X, ident, ones, gate_w, bias, ws_gate, ws_up, ws_down, w_gate, w_up, w_down,
                      wg_ring, wu_ring, wd_ring, ring_loaded, xs, table, total_rows):
    with ExitStack() as ctx:
        sb = lambda name, shape, dt=F32: ctx.enter_context(nc.sbuf_tensor(name, shape, dt))
        sem = lambda name: ctx.enter_context(nc.semaphore(name))
        ps = lambda name, shape: ctx.enter_context(nc.psum_tensor(name, shape, F32))

        w_g = sb("e_wg", [P, CC, H2])
        w_u = sb("e_wu", [P, CC, H2])
        w_d = sb("e_wd", [P, 2, C])
        w_route = sb("e_wroute", [P, CC, E2])
        bias_all = sb("e_bias", [P, E2])
        eps = sb("e_eps", [P, 1])
        carrier = sb("e_carrier", [P, 12])
        empty = sb("e_empty", [E2, CAP], U32)
        zrow = sb("e_zrow", [CAP, XC])
        set_iota = sb("e_set_iota", [P, SETS])
        expert_iota = sb("e_expert_iota", [P, E2])
        region = sb("e_region", [P, E2])
        token_id = sb("e_token_id", [P, TILES])
        stats = sb("e_stats", [P, GROUP, 6])
        mean_var = sb("e_mean_var", [P, GROUP, 2])
        std = sb("e_std", [P, GROUP])
        rstd = sb("e_rstd", [P, GROUP])
        xn = sb("e_xn", [P, GROUP, C])
        weight_rows = sb("e_weight_rows", [P, GROUP, E2])
        xnT = sb("e_xnT", [P, CC, GROUP * P])
        hT = sb("e_hT", [P, 2, GROUP * P])
        sil = sb("e_sil", [P, 2, GROUP * P])
        score = sb("e_score", [P, GROUP, E2])
        biased = sb("e_biased", [P, GROUP, E2])
        set_best = sb("e_set_best", [P, GROUP, SETS, 8])
        set_score = sb("e_set_score", [P, GROUP, SETS])
        set_order = sb("e_set_order", [P, GROUP, 8])
        set_index = sb("e_set_index", [P, GROUP, 8], U32)
        set_index_f = sb("e_set_index_f", [P, GROUP, TOP_SETS])
        set_onehot = sb("e_set_onehot", [P, GROUP, TOP_SETS, SETS])
        set_kept = sb("e_set_kept", [P, GROUP, SETS])
        set_far = sb("e_set_far", [P, GROUP, SETS])
        best = sb("e_best", [P, GROUP, 8])
        best_i = sb("e_best_i", [P, GROUP, 8], U32)
        best_f = sb("e_best_f", [P, GROUP, TOP2])
        onehot = sb("e_onehot", [P, GROUP, TOP2, E2])
        chosen = sb("e_chosen", [P, GROUP, E2])
        weight = sb("e_weight", [P, GROUP, E2])
        weight_sum = sb("e_weight_sum", [P, GROUP])
        total = sb("e_total", [P, E2])
        place = sb("e_place", [P, GROUP, E2])
        fits = sb("e_fits", [P, GROUP, E2])
        slot_top = sb("e_slot_top", [P, GROUP, 8])
        slot_none = sb("e_slot_none", [P, GROUP, 8])
        slot_now = sb("e_slot_now", [P, GROUP, 8], U32)
        token_now = sb("e_token_now", [P, GROUP], U32)

        up = ps("e_up", [P, 2, 2, GROUP * P])
        pj = ps("e_pj", [P, 2, C])
        lg = ps("e_lg", [P, GROUP, E2])
        cnt = ps("e_cnt", [P, GROUP + 1, E2])

        w_loaded = sem("e_w_loaded")
        set_up = sem("e_set_up")
        rows_set = sem("e_rows_set")
        var_ready = sem("e_var_ready")
        std_ready = sem("e_std_ready")
        xn_ready = sem("e_xn_ready")
        xn_stored = sem("e_xn_stored")
        weight_stored = sem("e_weight_stored")
        x_final = sem("e_x_final")
        x_stored = sem("e_x_stored")
        pj_full = sem("e_pj_full")
        pj_taken = [sem("e_pj_taken0"), sem("e_pj_taken1")]
        lg_full = sem("e_lg_full")
        score_ready = sem("e_score_ready")
        chosen_ready = sem("e_chosen_ready")
        weight_ready = sem("e_weight_ready")
        cnt_full = sem("e_cnt_full")
        up_full = sem("e_up_full")
        sil_ready = sem("e_sil_ready")
        h_ready = sem("e_h_ready")
        slots_ready = sem("e_slots_ready")
        scattered = sem("e_scattered")
        steps_sem = sem("e_steps")
        carried = sem("e_carried")
        SET_UP = 9
        HP = (P, H2 - P)

        block = ctx.enter_context(nc.Block())

        @block.sync
        def _(sp):
            sp.dma_start(w_route[:], gate_w.rearrange("(c p) e -> p c e", p=P)).then_inc(w_loaded, 16)
            sp.dma_start(bias_all[:], bias.unsqueeze(0).broadcast_to([P, E2])).then_inc(w_loaded, 16)
            for dst, src in ((w_g, ws_gate), (w_u, ws_up)):
                sp.dma_start(dst[:], src.rearrange("(c p) o -> p c o", p=P)).then_inc(w_loaded, 16)
            for f in range(2):
                sp.dma_start(w_d[0:HP[f], f, :], ws_down[P * f:P * f + HP[f], :]).then_inc(w_loaded, 16)
            sp.wait_ge(set_up, SET_UP)
            sp.dma_start(table.rearrange("(e s) one -> e (s one)", e=E2), empty[:]).then_inc(rows_set, 16)
            sp.dma_start(xs[TOKENS:ROWS2, :], zrow[:]).then_inc(rows_set, 16)
            sp.dma_start(total_rows[TOKENS:ROWS2, :], zrow[:, 0:C]).then_inc(rows_set, 16)
            for e in range(RING):
                for dst, src, n in ((wg_ring[:, e, :, :], w_gate, CC), (wu_ring[:, e, :, :], w_up, CC),
                                    (wd_ring[:, e, :, :], w_down, 2)):
                    sp.dma_start(dst, src[e].rearrange("(p c) f -> p c f", c=n)).then_inc(ring_loaded[e], 16)
            for g in range(GROUPS):
                sp.wait_ge(xn_ready, g + 1)
                sp.dma_start(group_rows(xs[0:TOKENS, 0:C], g), xn[:]).then_inc(xn_stored, 16)
                sp.wait_ge(weight_ready, g + 1)
                sp.dma_start(group_rows(xs[0:TOKENS, C:XC], g), weight_rows[:]).then_inc(weight_stored, 16)
                sp.wait_ge(x_final, g + 1)
                sp.dma_start(group_rows(total_rows[0:TOKENS, :], g), X[:, GROUP * g:GROUP * (g + 1), :])\
                    .then_inc(x_stored, 16)
            sp.wait_ge(xn_stored, 16 * GROUPS)
            sp.wait_ge(weight_stored, 16 * GROUPS)
            sp.wait_ge(x_stored, 16 * GROUPS)
            sp.wait_ge(rows_set, 48)

        @block.gpsimd
        def _(pool):
            iota = lambda out, pattern, base, m: nc.gpsimd.iota(
                out, pattern, base=base, channel_multiplier=m,
                allow_small_or_imprecise_dtypes=True).then_inc(set_up, 1)
            nc.gpsimd.memset(eps[:], LN_EPS).then_inc(set_up, 1)
            nc.gpsimd.memset(total[:], 0.0).then_inc(set_up, 1)
            nc.gpsimd.memset(zrow[:], 0.0).then_inc(set_up, 1)
            iota(empty[:], [[1, CAP]], TOKENS, 0)
            iota(set_iota[:], [[1, SETS]], 0, 0)
            iota(expert_iota[:], [[1, E2]], 0, 0)
            iota(region[:], [[CAP, E2]], 1, 0)
            iota(token_id[:], [[P, TILES]], 0, 1)
            nc.gpsimd.memset(carrier[:], 0.0).then_inc(set_up, 1)
            pool.wait_ge(rows_set, 48)
            pool.wait_ge(set_up, SET_UP)

            def turn(g):
                pool.wait_ge(slots_ready, g + 1)
                pool.wait_ge(carried, g)
                nc.gpsimd.tensor_tensor(carrier[:, 0:1], eps[:], eps[:], ALU.add).then_inc(carried, 1)
                for i in range(GROUP):
                    for k in range(TOP2):
                        nc.gpsimd.indirect_dma_start(
                            table, bass.IndirectOffsetOnAxis(ap=slot_now[:, i, k:k + 1], axis=0),
                            token_now[:, i:i + 1], None, bounds_check=SLOTS2 - 1, oob_is_err=False)\
                            .then_inc(scattered, 16)

            turn(0)
            with pool.Fori(1, GROUPS) as g:
                turn(g)
            pool.wait_ge(scattered, 16 * GROUPS * GROUP * TOP2)

        PJ = 8

        @block.tensor
        def _(pe):
            def bank_free(u, g):
                pe.wait_ge(pj_taken[u % 2], g * (PJ // 2) + 2 + u // 2)

            def transposes(g, first):
                pe.wait_ge(xn_ready, g + 1)
                for c in range(CC):
                    if not first:
                        bank_free(c, g - 1)
                    elif c >= 2:
                        pe.wait_ge(pj_taken[c % 2], 1)
                    for i in range(GROUP):
                        ins = pe.transpose(pj[:, c % 2, P * i:P * (i + 1)], xn[:, i, P * c:P * (c + 1)], ident[:])
                    ins.then_inc(pj_full, 1)

            def group(g, last):
                for k in range(2):
                    pe.wait_ge(pj_taken[k], g * (PJ // 2) + 2)
                for i in range(GROUP):
                    for c in range(CC):
                        ins = pe.matmul(lg[:, i, :], xnT[:, c, P * i:P * (i + 1)], w_route[:, c, :],
                                        start=(c == 0), stop=(c == CC - 1))
                ins.then_inc(lg_full, 1)
                for f in range(2):
                    pe.wait_ge(h_ready, g * 2)
                    for k, w in ((0, w_g), (1, w_u)):
                        for c in range(CC):
                            ins = pe.matmul(up[0:HP[f], f, k, :], w[:, c, P * f:P * f + HP[f]], xnT[:, c, :],
                                            start=(c == 0), stop=(c == CC - 1))
                    ins.then_inc(up_full, 1)
                if not last:
                    transposes(g + 1, False)
                pe.wait_ge(h_ready, g * 2 + 2)
                for i in range(GROUP):
                    bank_free((0 if last else 4) + i, g)
                    for f in range(2):
                        ins = pe.matmul(pj[:, i % 2, :], hT[0:HP[f], f, P * i:P * (i + 1)], w_d[0:HP[f], f, :],
                                        start=(f == 0), stop=(f == 1))
                    ins.then_inc(pj_full, 1)
                pe.wait_ge(chosen_ready, g + 1)
                pe.wait_ge(slots_ready, g)
                for i in range(GROUP + 1):
                    for j in range(min(i + 1, GROUP)):
                        ins = pe.matmul(cnt[:, i, :], ones[:, P:2 * P] if j == i else ones[:, 0:P], chosen[:, j, :],
                                        start=(j == 0), stop=(j == min(i, GROUP - 1)))
                ins.then_inc(cnt_full, 1)

            pe.wait_ge(w_loaded, 96)
            transposes(0, True)
            group(0, False)
            with pe.Fori(1, GROUPS - 1) as g:
                group(g, False)
            group(GROUPS - 1, True)

        @block.scalar
        def _(act):
            def root(g):
                act.wait_ge(var_ready, g + 1)
                nc.scalar.activation(std[:], mean_var[:, :, 1], ACT.Sqrt, bias=eps[:]).then_inc(std_ready, 1)

            def take_xnT(c, n):
                act.wait_ge(pj_full, n)
                nc.scalar.copy(xnT[:, c, :], pj[:, c % 2, :]).then_inc(pj_taken[c % 2], 1)

            def group(g, last):
                if not last:
                    root(g + 1)
                act.wait_ge(lg_full, g + 1)
                nc.scalar.activation(score[:], lg[:], ACT.Sigmoid).then_inc(score_ready, 1)
                for f in range(2):
                    act.wait_ge(up_full, g * 2 + f + 1)
                    nc.scalar.activation(sil[0:HP[f], f, :], up[0:HP[f], f, 0, :], ACT.Silu).then_inc(sil_ready, 1)
                if not last:
                    for c in (0, 2):
                        take_xnT(c, g * PJ + 4 + c + 1)

            act.wait_ge(set_up, SET_UP)
            root(0)
            for c in (0, 2):
                take_xnT(c, c + 1)
            group(0, False)
            with act.Fori(1, GROUPS - 1) as g:
                group(g, False)
            group(GROUPS - 1, True)

        @block.vector
        def _(dve):
            G3 = [P, GROUP, E2]

            def carry(column):
                dve.tensor_copy(carrier[:, column:column + 1], eps[:])

            def statistics(g, steps):
                layernorm_tiles(dve, steps, lambda i: tile_row(X, g * GROUP + i), stats, mean_var, GROUP,
                                carrier[:, 4:5], eps[:]).then_inc(var_ready, 1)

            def normalise(g, steps, first):
                dve.wait_ge(std_ready, g + 1)
                steps.mark(dve.reciprocal(rstd[:], std[:]))
                steps.wait()
                if not first:
                    dve.wait_ge(xn_stored, g * 16)
                for i in range(GROUP):
                    ins = dve.tensor_scalar(xn[:, i, :], tile_row(X, g * GROUP + i),
                                            mean_var[:, i, 0:1], rstd[:, i:i + 1], ALU.subtract, ALU.mult)
                ins.then_inc(xn_ready, 1)

            def take_xnT(c, n):
                dve.wait_ge(pj_full, n)
                dve.tensor_copy(xnT[:, c, :], pj[:, 1, :]).then_inc(pj_taken[1], 1)

            def hidden(g):
                for f in range(2):
                    dve.wait_ge(sil_ready, g * 2 + f + 1)
                    dve.tensor_tensor(hT[0:HP[f], f, :], sil[0:HP[f], f, :], up[0:HP[f], f, 1, :], ALU.mult)\
                        .then_inc(h_ready, 1)

            def choose_sets(g, steps):
                dve.wait_ge(score_ready, g + 1)
                steps.mark(dve.tensor_tensor(biased[:], score[:], bias_all[:].unsqueeze(1).broadcast_to(G3), ALU.add))
                steps.wait()
                carry(5)
                for i in range(GROUP):
                    for t in range(SETS):
                        ins = dve.max(set_best[:, i, t, :], biased[:, i, PER_SET * t:PER_SET * (t + 1)])
                steps.mark(ins)
                steps.wait()
                steps.mark(dve.tensor_tensor(set_score[:], set_best[:, :, :, 0], set_best[:, :, :, 1], ALU.add))
                steps.wait()
                carry(6)
                for i in range(GROUP):
                    ins = dve.max(set_order[:, i, :], set_score[:, i, :])
                steps.mark(ins)
                steps.wait()
                carry(7)
                for i in range(GROUP):
                    ins = dve.max_index(set_index[:, i, :], set_order[:, i, :], set_score[:, i, :])
                steps.mark(ins)
                steps.wait()
                steps.mark(dve.tensor_copy(set_index_f[:], set_index[:, :, 0:TOP_SETS]))
                steps.wait()
                shape = [P, GROUP, TOP_SETS, SETS]
                steps.mark(dve.tensor_tensor(set_onehot[:], set_iota[:].unsqueeze(1).unsqueeze(1).broadcast_to(shape),
                                             set_index_f[:].unsqueeze(3).broadcast_to(shape), ALU.is_equal))
                steps.wait()
                steps.mark(dve.tensor_reduce(set_kept[:], set_onehot[:].rearrange("p i k s -> p i s k"), AX.X, ALU.add))
                steps.wait()
                steps.mark(dve.tensor_scalar(set_far[:], set_kept[:], 1.0, FAR, ALU.subtract, ALU.mult))
                by_set = biased[:].rearrange("p i (s e) -> p i s e", s=SETS)
                shape = [P, GROUP, SETS, PER_SET]
                steps.mark(dve.tensor_tensor(by_set, by_set, set_kept[:].unsqueeze(3).broadcast_to(shape), ALU.mult))
                steps.wait()
                steps.mark(dve.tensor_tensor(by_set, by_set, set_far[:].unsqueeze(3).broadcast_to(shape), ALU.add))
                steps.wait()

            def choose(g, steps):
                carry(8)
                for i in range(GROUP):
                    ins = dve.max(best[:, i, :], biased[:, i, :])
                steps.mark(ins)
                steps.wait()
                carry(9)
                for i in range(GROUP):
                    ins = dve.max_index(best_i[:, i, :], best[:, i, :], biased[:, i, :])
                steps.mark(ins)
                steps.wait()
                steps.mark(dve.tensor_copy(best_f[:], best_i[:, :, 0:TOP2]))
                steps.wait()
                shape = [P, GROUP, TOP2, E2]
                steps.mark(dve.tensor_tensor(onehot[:], expert_iota[:].unsqueeze(1).unsqueeze(1).broadcast_to(shape),
                                             best_f[:].unsqueeze(3).broadcast_to(shape), ALU.is_equal))
                steps.wait()
                dve.tensor_reduce(chosen[:], onehot[:].rearrange("p i k e -> p i e k"), AX.X, ALU.add)\
                    .then_inc(chosen_ready, 1)
                dve.wait_ge(chosen_ready, g + 1)
                steps.mark(dve.tensor_tensor(weight[:], chosen[:], score[:], ALU.mult))
                steps.wait()
                steps.mark(dve.tensor_reduce(weight_sum[:], weight[:], AX.X, ALU.add))
                steps.wait()
                steps.mark(dve.reciprocal(weight_sum[:], weight_sum[:]))
                steps.wait()
                dve.wait_ge(weight_stored, g * 16)
                dve.scalar_tensor_tensor(out=weight_rows[:], in0=weight[:], scalar=ROUTE_SCALE,
                                         in1=weight_sum[:].unsqueeze(2).broadcast_to(G3), op0=ALU.mult, op1=ALU.mult)\
                    .then_inc(weight_ready, 1)

            def place_slots(g, steps):
                dve.wait_ge(cnt_full, g + 1)
                steps.mark(dve.tensor_tensor(place[:], cnt[:, 0:GROUP, :], total[:].unsqueeze(1).broadcast_to(G3),
                                             ALU.add))
                steps.wait()
                steps.mark(dve.tensor_tensor(total[:], total[:], cnt[:, GROUP, :], ALU.add))
                steps.mark(dve.scalar_tensor_tensor(out=fits[:], in0=place[:], scalar=float(CAP), in1=chosen[:],
                                                    op0=ALU.is_lt, op1=ALU.mult))
                steps.wait()
                steps.mark(dve.tensor_tensor(place[:], place[:], region[:].unsqueeze(1).broadcast_to(G3), ALU.add))
                steps.wait()
                steps.mark(dve.tensor_tensor(place[:], place[:], fits[:], ALU.mult))
                steps.wait()
                carry(10)
                for i in range(GROUP):
                    ins = dve.max(slot_top[:, i, :], place[:, i, :])
                steps.mark(ins)
                steps.wait()
                steps.mark(dve.tensor_scalar(slot_none[:], slot_top[:], 0.0, NO_SLOT, ALU.is_equal, ALU.mult))
                steps.wait()
                steps.mark(dve.scalar_tensor_tensor(out=slot_top[:], in0=slot_top[:], scalar=1.0, in1=slot_none[:],
                                                    op0=ALU.subtract, op1=ALU.add))
                steps.wait()
                dve.wait_ge(scattered, g * (16 * GROUP * TOP2))
                dve.tensor_scalar(token_now[:], token_id[:, bass.ds(g * GROUP, GROUP)], 0.0, None, ALU.add)
                dve.tensor_copy(slot_now[:], slot_top[:]).then_inc(slots_ready, 1)

            PER_TURN = 1 + 1 + 10 + 1 + 7 + 8

            def group(g, last):
                steps = Steps(dve, steps_sem, g * PER_TURN + 2)
                if not last:
                    statistics(g + 1, steps)
                    normalise(g + 1, steps, False)
                choose_sets(g, steps)
                hidden(g)
                if not last:
                    for c in (1, 3):
                        take_xnT(c, g * PJ + 4 + c + 1)
                choose(g, steps)
                for i in range(GROUP):
                    dve.wait_ge(pj_full, g * PJ + 4 + (0 if last else 4) + i + 1)
                    x = tile_row(X, g * GROUP + i)
                    dve.tensor_tensor(x, x, pj[:, i % 2, :], ALU.add).then_inc(pj_taken[i % 2], 1)
                for k in range(2):
                    dve.wait_ge(pj_taken[k], g * (PJ // 2) + (4 if last else 6))
                dve.tensor_copy(carrier[:, 3:4], eps[:]).then_inc(x_final, 1)
                place_slots(g, steps)
                assert steps.n == PER_TURN - (2 if last else 0), steps.n

            dve.wait_ge(set_up, SET_UP)
            dve.wait_ge(w_loaded, 96)
            steps = Steps(dve, steps_sem)
            statistics(0, steps)
            normalise(0, steps, True)
            for c in (1, 3):
                take_xnT(c, c + 1)
            group(0, False)
            with dve.Fori(1, GROUPS - 1) as g:
                group(g, False)
            group(GROUPS - 1, True)


def second_ffn_experts(nc, ident, w_gate, w_up, w_down, wg_ring, wu_ring, wd_ring, ring_loaded, xs, table, total_rows,
                       out):
    with ExitStack() as ctx:
        sb = lambda name, shape, dt=F32: ctx.enter_context(nc.sbuf_tensor(name, shape, dt))
        sem = lambda name: ctx.enter_context(nc.semaphore(name))
        ps = lambda name, shape: ctx.enter_context(nc.psum_tensor(name, shape, F32))

        ids_rows = sb("f_ids_rows", [E2, CAP], U32)
        ids_rows_f = sb("f_ids_rows_f", [E2, CAP])
        ids_f = sb("f_ids_f", [CAP, E2])
        ids = sb("f_ids", [CAP, ROWS_RING, 1], U32)
        xg = sb("f_xg", [CAP, ROWS_RING, XC])
        xgT = sb("f_xgT", [P, 2, CC * CAP])
        sil = sb("f_sil", [CAP, 2, H2])
        h = sb("f_h", [CAP, 2, H2])
        hT = sb("f_hT", [HH2, 2, 2 * CAP])
        y = sb("f_y", [CAP, RING, C])
        carrier = sb("f_carrier", [P, 2])

        up = ps("f_up", [CAP, 2, 512])
        yp = ps("f_yp", [CAP, 2, C])
        xp = ps("f_xp", [P, 2, 512])
        hp = ps("f_hp", [HH2, 2, 512])

        ids_loaded = sem("f_ids_loaded")
        ids_float = sem("f_ids_float")
        ids_turned = sem("f_ids_turned")
        ids_steps = sem("f_ids_steps")
        ids_ready = sem("f_ids_ready")
        gathered = [sem(f"f_gathered{r}") for r in range(ROWS_RING)]
        added = sem("f_added")
        x_turned = sem("f_x_turned")
        xgT_ready = sem("f_xgT_ready")
        up_full = sem("f_up_full")
        sil_ready = sem("f_sil_ready")
        h_ready = sem("f_h_ready")
        h_turned = sem("f_h_turned")
        hT_ready = sem("f_hT_ready")
        y_full = sem("f_y_full")
        y_ready = sem("f_y_ready")
        carried = sem("f_carried")
        copied = sem("f_copied")
        TURNS = E2 // ROWS_RING

        def turns(eng, expert):
            for r in range(ROWS_RING):
                expert(r, r, 0, "first")
            with eng.Fori(1, TURNS - 1) as t:
                for r in range(ROWS_RING):
                    expert(t * ROWS_RING + r, r, t, "")
            for r in range(ROWS_RING):
                expert((TURNS - 1) * ROWS_RING + r, r, TURNS - 1, "last")

        block = ctx.enter_context(nc.Block())

        @block.sync
        def _(sp):
            sp.dma_start(ids_rows[:], table.rearrange("(e s) one -> e (s one)", e=E2)).then_inc(ids_loaded, 16)

        @block.gpsimd
        def _(pool):
            def gather(e, r, n):
                pool.wait_ge(ids_ready, e + 1)
                pool.wait_ge(carried, n)
                nc.gpsimd.tensor_tensor(carrier[:, 0:1], ident[:, 0:1], ident[:, 0:1], ALU.add).then_inc(carried, 1)
                nc.gpsimd.indirect_dma_start(xg[:, r, :], None, xs, bass.IndirectOffsetOnAxis(
                    ap=ids[:, r, :], axis=0)).then_inc(gathered[r], 16)

            def add(e, r, n):
                pool.wait_ge(y_ready, e + 1)
                pool.wait_ge(added, e * 16)
                pool.wait_ge(carried, n)
                nc.gpsimd.tensor_tensor(carrier[:, 0:1], ident[:, 0:1], ident[:, 0:1], ALU.add).then_inc(carried, 1)
                nc.gpsimd.indirect_dma_start(total_rows, bass.IndirectOffsetOnAxis(ap=ids[:, r, :], axis=0),
                                             y[:, r % RING, :], None, compute_op=ALU.add).then_inc(added, 16)

            def expert(e, r, t, which):
                if not (which == "last" and r >= ROWS_RING - AHEAD):
                    gather(e + AHEAD, (r + AHEAD) % ROWS_RING, e * 2 + AHEAD)
                    add(e, r, e * 2 + AHEAD + 1)
                else:
                    add(e, r, E2 + e)

            for e in range(AHEAD):
                gather(e, e, e)
            turns(pool, expert)
            pool.wait_ge(added, 16 * E2)
            rows = TOKENS // 8
            for b in range(8):
                pool.dma_start(out[rows * b:rows * (b + 1), :], total_rows[rows * b:rows * (b + 1), :])\
                    .then_inc(copied, 16)
            pool.wait_ge(copied, 16 * 8)

        @block.tensor
        def _(pe):
            def turn_x(e, r, t, start):
                pe.wait_ge(gathered[r], t * 16 + 16)
                if not start:
                    pe.wait_ge(xgT_ready, e - 1)
                rows = xg[:, r, 0:C].rearrange("s (p c) -> s c p", c=CC)
                for c in range(CC):
                    ins = pe.transpose(xp[:, r % 2, CAP * c:CAP * (c + 1)], rows[:, c, :], ident[0:CAP, 0:CAP])
                ins.then_inc(x_turned, 1)

            def turn_h(e, r, start):
                pe.wait_ge(h_ready, e + 1)
                if not start:
                    pe.wait_ge(hT_ready, e - 1)
                halves = h[:, r % 2, :].rearrange("s (p c) -> s c p", c=2)
                for f in range(2):
                    ins = pe.transpose(hp[:, r % 2, CAP * f:CAP * (f + 1)], halves[:, f, :], ident[0:CAP, 0:CAP])
                ins.then_inc(h_turned, 1)

            def down(e, r, start):
                pe.wait_ge(hT_ready, e + 1)
                if not start:
                    pe.wait_ge(y_ready, e - 1)
                for f in range(2):
                    ins = pe.matmul(yp[:, r % 2, :], hT[:, r % 2, CAP * f:CAP * (f + 1)], wd_ring[:, r % RING, f, :],
                                    start=(f == 0), stop=(f == 1))
                ins.then_inc(y_full, 1)

            def expert(e, r, t, which):
                first = which == "first" and r == 0
                pe.wait_ge(ring_loaded[r % RING], (t * 2 + r // RING) * 48 + 48)
                pe.wait_ge(xgT_ready, e + 1)
                if not (which == "first" and r < 2):
                    pe.wait_ge(h_ready, e - 1)
                for k, w in ((0, wg_ring), (1, wu_ring)):
                    for c in range(CC):
                        ins = pe.matmul(up[:, r % 2, H2 * k:H2 * (k + 1)], xgT[:, r % 2, CAP * c:CAP * (c + 1)],
                                        w[:, r % RING, c, :], start=(c == 0), stop=(c == CC - 1))
                    if k == 0 and not first:
                        turn_h(e - 1, (r - 1) % ROWS_RING, which == "first" and r < 3)
                ins.then_inc(up_full, 1)
                if not (which == "last" and r == ROWS_RING - 1):
                    turn_x(e + 1, (r + 1) % ROWS_RING, t + (r + 1) // ROWS_RING, first)
                if not first:
                    down(e - 1, (r - 1) % ROWS_RING, which == "first" and r < 3)

            pe.wait_ge(ids_float, 1)
            pe.transpose(hp[:, 0, 0:E2], ids_rows_f[:], ident[0:E2, 0:E2]).then_inc(ids_turned, 1)
            turn_x(0, 0, 0, True)
            turns(pe, expert)
            turn_h(E2 - 1, ROWS_RING - 1, False)
            down(E2 - 1, ROWS_RING - 1, False)

        @block.scalar
        def _(act):
            def load(e, r):
                act.wait_ge(y_full, e - (RING - 1))
                for dst, src, n in ((wg_ring[:, r, :, :], w_gate, CC), (wu_ring[:, r, :, :], w_up, CC),
                                    (wd_ring[:, r, :, :], w_down, 2)):
                    act.dma_start(dst, src[bass.ds(e, 1)].rearrange("a (p c) f -> p (a c) f", c=n))\
                        .then_inc(ring_loaded[r], 16)

            def take_x(e, r, start):
                act.wait_ge(x_turned, e + 1)
                if not start:
                    act.wait_ge(up_full, e - 1)
                nc.scalar.copy(xgT[:, r % 2, :], xp[:, r % 2, 0:CC * CAP]).then_inc(xgT_ready, 1)

            def expert(e, r, t, which):
                act.wait_ge(up_full, e + 1)
                if not (which == "first" and r < 2):
                    act.wait_ge(h_ready, e - 1)
                nc.scalar.activation(sil[:, r % 2, :], up[:, r % 2, 0:H2], ACT.Silu).then_inc(sil_ready, 1)
                if not (which == "last" and r == ROWS_RING - 1):
                    take_x(e + 1, (r + 1) % ROWS_RING, which == "first" and r < 1)
                if not (which == "first" and r < 2) and not (which == "last" and r >= ROWS_RING - RING + 2):
                    load(e + RING - 2, (r - 2) % RING)

            take_x(0, 0, True)
            turns(act, expert)

        @block.vector
        def _(dve):
            def pick_ids(e, r, start):
                if not start:
                    dve.wait_ge(added, (e - ROWS_RING + 1) * 16)
                dve.tensor_scalar(ids[:, r, :], ids_f[:, bass.ds(e, 1)], 0.0, None, ALU.add).then_inc(ids_ready, 1)

            def take_h(e, r, start):
                dve.wait_ge(h_turned, e + 1)
                if not start:
                    dve.wait_ge(y_full, e - 1)
                dve.tensor_copy(hT[:, r % 2, :], hp[:, r % 2, 0:2 * CAP]).then_inc(hT_ready, 1)

            def take_y(e, r, start):
                dve.wait_ge(y_full, e + 1)
                if not start:
                    dve.wait_ge(added, (e - RING + 1) * 16)
                weight = xg[:, r, bass.ds(e + C, 1)]
                dve.tensor_scalar(y[:, r % RING, :], yp[:, r % 2, :], weight, None, ALU.mult).then_inc(y_ready, 1)

            def expert(e, r, t, which):
                first = which == "first" and r == 0
                if not first:
                    take_h(e - 1, (r - 1) % ROWS_RING, which == "first" and r < 3)
                dve.wait_ge(sil_ready, e + 1)
                if not (which == "first" and r < 2):
                    dve.wait_ge(h_turned, e - 1)
                dve.tensor_tensor(h[:, r % 2, :], sil[:, r % 2, :], up[:, r % 2, H2:2 * H2], ALU.mult)\
                    .then_inc(h_ready, 1)
                if not first:
                    take_y(e - 1, (r - 1) % ROWS_RING, which == "first" and r <= RING)
                if not (which == "last" and r >= ROWS_RING - AHEAD - 1):
                    pick_ids(e + AHEAD + 1, (r + AHEAD + 1) % ROWS_RING, which == "first" and r < ROWS_RING - AHEAD - 1)

            dve.wait_ge(ids_loaded, 16)
            dve.tensor_copy(ids_rows_f[:], ids_rows[:]).then_inc(ids_float, 1)
            dve.wait_ge(ids_turned, 1)
            dve.tensor_copy(ids_f[:], hp[:, 0, 0:E2]).then_inc(ids_steps, 1)
            dve.wait_ge(ids_steps, 1)
            for e in range(AHEAD + 1):
                pick_ids(e, e, True)
            turns(dve, expert)
            take_h(E2 - 1, ROWS_RING - 1, False)
            take_y(E2 - 1, ROWS_RING - 1, False)


def program(nc, x, wq, wk, wv, wo, route1, w_gate1, w_up1, w_down1, sh_gate, sh_up, sh_down, w_qkv, w_out,
            route2, bias2, w_gate2, w_up2, w_down2, ws_gate, ws_up, ws_down, out):
    rows_1 = nc.dram_tensor("rows_1", [ROWS, C], F32).ap()
    table_1 = nc.dram_tensor("table_1", [SLOTS1, 1], U32).ap()
    expert_rows = nc.dram_tensor("expert_rows", [2 * PAIRS1 * P, C], F32).ap()
    rows_2 = nc.dram_tensor("rows_2", [ROWS2, XC], F32).ap()
    table_2 = nc.dram_tensor("table_2", [SLOTS2, 1], U32).ap()
    total_rows = nc.dram_tensor("total_rows", [ROWS2, C], F32).ap()

    with ExitStack() as ctx:
        ident = ctx.enter_context(nc.sbuf_tensor("ident", [P, P], F32))
        ones = ctx.enter_context(nc.sbuf_tensor("ones", [P, 2 * P], F32))
        constants(nc, ctx, ident, ones)
        with ExitStack() as rows_ctx:
            X = rows_ctx.enter_context(nc.sbuf_tensor("X", [P, TILES, C], F32))
            first_attention(nc, x, wq, wk, wv, wo, X, ident, ones)
            with ExitStack() as routed:
                sb = lambda name, shape, dt=F32: routed.enter_context(nc.sbuf_tensor(name, shape, dt))
                weight_all = sb("weight_all", [P, TILES, TOP1])
                slot_all = sb("slot_all", [P, TILES, TOP1], U32)
                with ExitStack() as weights:
                    sb = lambda name, shape, dt=F32: weights.enter_context(nc.sbuf_tensor(name, shape, dt))
                    tile_expert = sb("tile_expert", [P, 2 * PAIRS1], I32)
                    tile_slot = sb("tile_slot", [P, 2 * PAIRS1], I32)
                    w13 = sb("w13", [P, CC * E1, 2 * H1])
                    w13_loaded = weights.enter_context(nc.semaphore("w13_loaded"))
                    first_ffn_shared(nc, X, ident, ones, w13_loaded, route1, sh_gate, sh_up, sh_down, w_gate1, w_up1,
                                     w13, rows_1, table_1, weight_all, slot_all, tile_expert, tile_slot)
                    w2 = sb("w2", [P, HC1 * E1, C])
                    first_ffn_experts(nc, ident, w13, w13_loaded, w2, w_down1, rows_1, table_1, expert_rows,
                                      tile_expert, tile_slot)
                second_attention(nc, X, ident, ones, expert_rows, slot_all, weight_all, w_qkv, w_out)
            wg_ring = rows_ctx.enter_context(nc.sbuf_tensor("wg_ring", [P, RING, CC, H2], F32))
            wu_ring = rows_ctx.enter_context(nc.sbuf_tensor("wu_ring", [P, RING, CC, H2], F32))
            wd_ring = rows_ctx.enter_context(nc.sbuf_tensor("wd_ring", [HH2, RING, 2, C], F32))
            ring_loaded = [rows_ctx.enter_context(nc.semaphore(f"ring_loaded{r}")) for r in range(RING)]
            second_ffn_shared(nc, X, ident, ones, route2, bias2, ws_gate, ws_up, ws_down, w_gate2, w_up2, w_down2,
                              wg_ring, wu_ring, wd_ring, ring_loaded, rows_2, table_2, total_rows)
            second_ffn_experts(nc, ident, w_gate2, w_up2, w_down2, wg_ring, wu_ring, wd_ring, ring_loaded, rows_2,
                               table_2, total_rows, out)


def kernel(**inputs):
    import numpy as _np
    import concourse.bacc as _bacc
    from concourse import mybir as _mybir
    from concourse.bass_utils import run_bass_kernel_spmd as _run

    a = {name: _np.asarray(value) for name, value in inputs.items()}
    turned = lambda w: _np.swapaxes(w, -1, -2)
    laid_out = {
        "x": a["L0_attn_x"].reshape(TOKENS, C),
        "wq": turned(a["L0_attn_Wq"]), "wk": turned(a["L0_attn_Wk"]), "wv": turned(a["L0_attn_Wv"]),
        "wo": turned(a["L0_attn_Wo"]),
        "route1": turned(_np.concatenate([a["L0_ffn_gate_w"], a["L0_ffn_se_gate_w"]], axis=0)),
        "w_gate1": turned(a["L0_ffn_w_gate"]), "w_up1": turned(a["L0_ffn_w_up"]), "w_down1": turned(a["L0_ffn_w_down"]),
        "sh_gate": turned(a["L0_ffn_sh_gate"]), "sh_up": turned(a["L0_ffn_sh_up"]),
        "sh_down": turned(a["L0_ffn_sh_down"]),
        "w_qkv": turned(a["L1_attn_weight_qkv"]), "w_out": turned(a["L1_attn_weight_out"]),
        "route2": a["L1_ffn_gate_w"], "bias2": a["L1_ffn_bias"],
        "w_gate2": a["L1_ffn_w_gate"], "w_up2": a["L1_ffn_w_up"], "w_down2": a["L1_ffn_w_down"],
        "ws_gate": a["L1_ffn_ws_gate"], "ws_up": a["L1_ffn_ws_up"], "ws_down": a["L1_ffn_ws_down"],
    }
    nc = _bacc.Bacc("TRN2", target_bir_lowering=False, num_devices=1)
    arrays, args = {}, []
    for name, value in laid_out.items():
        value = _np.ascontiguousarray(value)
        arrays[f"in_{name}_dram"] = value
        args.append(nc.dram_tensor(f"in_{name}_dram", value.shape, _mybir.dt.from_np(value.dtype),
                                   kind="ExternalInput").ap())
    out = nc.dram_tensor("out_dram", (TOKENS, C), F32, kind="ExternalOutput").ap()
    program(nc, *args, out)
    r = _run(nc, [arrays], core_ids=[0])
    return r.results[0]["out_dram"].reshape(BATCHES, SEQ, C)
```

```python
from contextlib import ExitStack

import concourse.bass as bass
from concourse import mybir

F32R = mybir.dt.float32r
F32 = mybir.dt.float32
I32 = mybir.dt.int32
U32 = mybir.dt.uint32
ALU = mybir.AluOpType
ACT = mybir.ActivationFunctionType
AX = mybir.AxisListType

P = 128
C = 512
CC = C // P
TOKENS = 4096
TILES = TOKENS // P
LN_EPS = 1e-5

BATCHES = 8
SEQ = TOKENS // BATCHES
ST = SEQ // P
HEADS = 16
HD = C // HEADS
QUADS = HEADS // 4
ATTN_SCALE = float(HD) ** -0.5
ATTN_SHIFT = 0.1
ATTN_EPS = 1e-6


class Steps:

    def __init__(self, eng, sem, base=0):
        self.eng, self.sem, self.base, self.n = eng, sem, base, 0

    def mark(self, instruction):
        instruction.then_inc(self.sem, 1)
        self.n += 1

    def wait(self):
        self.eng.wait_ge(self.sem, self.base + self.n)


def constants(nc, ctx, ident, ones):
    set_up = ctx.enter_context(nc.semaphore("constants_set"))
    with nc.Block() as block:
        @block.gpsimd
        def _(pool):
            nc.gpsimd.memset(ident[:], 0.0).then_inc(set_up, 1)
            nc.gpsimd.memset(ones[:], 1.0).then_inc(set_up, 1)
            pool.wait_ge(set_up, 2)
            nc.gpsimd.affine_select(out=ident[:], in_=ident[:], compare_op=ALU.not_equal, fill=1.0, base=0,
                                    pattern=[[-1, P]], channel_multiplier=1)
            nc.gpsimd.affine_select(out=ones[:, P:2 * P], in_=ones[:, P:2 * P], compare_op=ALU.is_ge, fill=0.0,
                                    base=-1, pattern=[[1, P]], channel_multiplier=-1)


def layernorm_tiles(dve, steps, x_tile, stats, mean_var, n, carrier, one):
    for i in range(n):
        ins = dve.bn_stats(stats[:, i, :], x_tile(i))
    steps.mark(ins)
    steps.wait()
    dve.tensor_copy(carrier, one)
    for i in range(n):
        ins = dve.bn_aggr(mean_var[:, i, :], stats[:, i, :])
    return ins


def first_attention(nc, x_dram, wq, wk, wv, wo, X, ident, ones):
    with ExitStack() as ctx:
        sb = lambda name, shape: ctx.enter_context(nc.sbuf_tensor(name, shape, F32))
        sem = lambda name: ctx.enter_context(nc.semaphore(name))
        ps = lambda name, shape: ctx.enter_context(nc.psum_tensor(name, shape, F32))

        RING_HEADS = 8
        at_head = lambda quad, r: (4 * quad + r) % RING_HEADS
        w_q, w_k, w_v, w_o = (sb(f"a_w{n}", [P, CC, C]) for n in "qkvo")
        stats = sb("a_stats", [P, ST, 6])
        mean_var = sb("a_mean_var", [P, ST, 2])
        std = sb("a_std", [P, ST])
        rstd = sb("a_rstd", [P, ST])
        eps = sb("a_eps", [P, 1])
        shift = sb("a_shift", [P, 1])
        carrier = sb("a_carrier", [P, 4])
        dve_carrier = sb("a_dve_carrier", [P, 1])
        xn = sb("a_xn", [P, ST, C])
        xnT = sb("a_xnT", [P, CC, SEQ])
        high = sb("a_high", [P, 2, SEQ])
        low = sb("a_low", [P, 2, SEQ])
        q3 = ctx.enter_context(nc.sbuf_tensor("a_q3", [3 * HD, RING_HEADS, SEQ], F32R))
        k3 = ctx.enter_context(nc.sbuf_tensor("a_k3", [3 * HD, RING_HEADS, SEQ], F32R))
        v = sb("a_v", [P, ST, C])
        w = sb("a_w", [P, 3, 4, SEQ])
        attnT = sb("a_attnT", [P, QUADS, SEQ])
        sums = sb("a_sums", [P, SEQ])

        pj = ps("a_pj", [P, 2, SEQ])
        sc = ps("a_sc", [P, 2, SEQ])
        num = ps("a_num", [P, 2, SEQ])
        den = ps("a_den", [P, 2, SEQ])

        x_loaded = sem("a_x_loaded")
        w_loaded = sem("a_w_loaded")
        zeroed = sem("a_zeroed")
        var_ready = sem("a_var_ready")
        std_ready = sem("a_std_ready")
        xn_ready = sem("a_xn_ready")
        pj_full = sem("a_pj_full")
        pj_taken = [sem("a_pj_taken0"), sem("a_pj_taken1")]
        high_ready = sem("a_high_ready")
        act_parts_ready = sem("a_act_parts_ready")
        dve_parts_ready = sem("a_dve_parts_ready")
        sc_full = sem("a_sc_full")
        sc_taken = sem("a_sc_taken")
        w_masked = sem("a_w_masked")
        pv_done = sem("a_pv_done")
        attn_ready = sem("a_attn_ready")
        dve_steps = sem("a_dve_steps")

        PROJECTIONS = ([("q", 0), ("k", 0)] + [("v", i) for i in range(ST)]
                       + [(kind, j) for j in range(1, QUADS) for kind in "qk"])
        USES = PROJECTIONS + [("x", c) for c in range(CC)] + [("o", i) for i in range(ST)]
        T_PER = len(USES)
        N_PROJ = len(PROJECTIONS)
        NEXT = 2 + ST
        N_QK = 2 * QUADS

        def taken(n, b):
            return b * (T_PER // 2) + ST // 2 + n // 2

        def qk_at(n):
            return 2 * USES[n][1] + "qk".index(USES[n][0])

        N_SC = QUADS * ST * 4
        N_STEP = QUADS * ST

        block = ctx.enter_context(nc.Block())

        @block.sync
        def _(sp):
            for b in range(BATCHES):
                if b >= 1:
                    sp.wait_ge(x_loaded, 16 * b)
                sp.dma_start(X[:, ST * b:ST * (b + 1), :],
                             x_dram.rearrange("(t p) c -> p t c", p=P)[:, ST * b:ST * (b + 1), :])\
                    .then_inc(x_loaded, 16)
                if b == 0:
                    for dst, src in ((w_q, wq), (w_k, wk), (w_v, wv), (w_o, wo)):
                        sp.dma_start(dst[:], src.rearrange("(c p) o -> p c o", p=P)).then_inc(w_loaded, 16)

        @block.gpsimd
        def _(pool):
            nc.gpsimd.memset(eps[:], LN_EPS).then_inc(zeroed, 1)
            nc.gpsimd.memset(shift[:], ATTN_SHIFT).then_inc(zeroed, 1)

            def batch(b):
                for s in range(N_STEP):
                    kc = s % ST
                    pool.wait_ge(sc_taken, b * N_SC + 4 * s + 4)
                    nc.gpsimd.tensor_tensor(carrier[:, s % 4:s % 4 + 1], eps[:], eps[:], ALU.add)
                    diag = w[:, s % 3, :, P * kc:P * (kc + 1)]
                    nc.gpsimd.affine_select(out=diag, in_=diag, compare_op=ALU.is_ge, fill=0.0, base=0,
                                            pattern=[[0, 4], [1, P]], channel_multiplier=-1).then_inc(w_masked, 1)

            batch(0)
            with pool.Fori(1, BATCHES) as b:
                batch(b)

        @block.tensor
        def _(pe):
            def bank_free(n, b):
                pe.wait_ge(pj_taken[n % 2], taken(n, b))

            def transposes(b, first):
                pe.wait_ge(xn_ready, b + 1)
                for c in range(CC):
                    if not first:
                        bank_free(N_PROJ + c, b - 1)
                    elif c >= 2:
                        pe.wait_ge(pj_taken[c % 2], 1)
                    for i in range(ST):
                        ins = pe.transpose(pj[:, c % 2, P * i:P * (i + 1)], xn[:, i, P * c:P * (c + 1)], ident[:])
                    ins.then_inc(pj_full, 1)

            def project(n, b, chunks=range(CC)):
                if 0 in chunks:
                    bank_free(n, b)
                kind, j = USES[n]
                for c in chunks:
                    if kind in "qk":
                        ins = pe.matmul(pj[:, n % 2, :], (w_q if kind == "q" else w_k)[:, c, P * j:P * (j + 1)],
                                        xnT[:, c, :], start=(c == 0), stop=(c == CC - 1))
                    else:
                        ins = pe.matmul(pj[:, n % 2, :], xnT[:, c, P * j:P * (j + 1)], w_v[:, c, :],
                                        start=(c == 0), stop=(c == CC - 1))
                if CC - 1 in chunks:
                    ins.then_inc(pj_full, 1)

            def scores(s, b, heads):
                quad, kc = divmod(s, ST)
                if kc == 0 and 0 in heads:
                    pe.wait_ge(act_parts_ready, b * N_QK + 2 * quad + 2)
                    pe.wait_ge(dve_parts_ready, b * N_QK + 2 * quad + 2)
                for r in heads:
                    m = 4 * s + r
                    if m >= 2:
                        pe.wait_ge(sc_taken, b * N_SC + m - 1)
                    pe.matmul(sc[:, m % 2, P * kc:SEQ], k3[:, at_head(quad, r), P * kc:P * (kc + 1)],
                              q3[:, at_head(quad, r), P * kc:SEQ], start=True, stop=True).then_inc(sc_full, 1)

            def numerators(s, b):
                quad, kc = divmod(s, ST)
                pe.wait_ge(w_masked, b * N_STEP + s + 1)
                if kc == 0 and quad >= 2:
                    pe.wait_ge(attn_ready, b * QUADS + quad - 1)
                for r in range(4):
                    h = 4 * quad + r
                    pe.matmul(num[32 * r:32 * r + 32, quad % 2, P * kc:SEQ], v[:, kc, HD * h:HD * (h + 1)],
                              w[:, s % 3, r, P * kc:SEQ], start=(kc == 0), stop=(kc == ST - 1), skip_group_check=True)

            def denominators(s):
                quad, kc = divmod(s, ST)
                for r in range(4):
                    ins = pe.matmul(den[32 * r:32 * r + 32, quad % 2, P * kc:SEQ], ones[:, 0:HD],
                                    w[:, s % 3, r, P * kc:SEQ], start=(kc == 0), stop=(kc == ST - 1),
                                    skip_group_check=True)
                ins.then_inc(pv_done, 1)

            def outputs(b, u):
                def add_quads(i, quads):
                    for c in quads:
                        ins = pe.matmul(pj[:, i % 2, :], attnT[:, c, P * i:P * (i + 1)], w_o[:, c, :],
                                        start=(c == 0), stop=(c == QUADS - 1))
                        if c == QUADS - 1:
                            ins.then_inc(pj_full, 1)

                pe.wait_ge(attn_ready, b * QUADS + QUADS - 1)
                for i in range(2):
                    bank_free(u + i, b)
                    add_quads(i, range(QUADS - 1))
                pe.wait_ge(attn_ready, (b + 1) * QUADS)
                for i in range(2):
                    add_quads(i, (QUADS - 1,))
                for i in range(2, ST):
                    bank_free(u + i, b)
                    add_quads(i, range(QUADS))

            def batch(b, last):
                for k in range(2):
                    pe.wait_ge(pj_taken[k], taken(k, b))
                for n in range(NEXT + 1):
                    project(n, b)
                for s in range(N_STEP + 2):
                    if s < N_STEP:
                        scores(s, b, (0, 1))
                    if s == 2:
                        for k in range(2):
                            pe.wait_ge(pj_taken[k], taken(NEXT + k, b))
                    projecting = s < 2 * (N_PROJ - NEXT - 1)
                    if projecting:
                        project(NEXT + 1 + s // 2, b, (s % 2 * 2,))
                    if s >= 2:
                        numerators(s - 2, b)
                    if s < N_STEP:
                        scores(s, b, (2, 3))
                    if projecting:
                        project(NEXT + 1 + s // 2, b, (s % 2 * 2 + 1,))
                    if s >= 2:
                        denominators(s - 2)
                if not last:
                    transposes(b + 1, False)
                outputs(b, N_PROJ if last else N_PROJ + CC)

            transposes(0, True)
            pe.wait_ge(w_loaded, 64)
            batch(0, False)
            with pe.Fori(1, BATCHES - 1) as b:
                batch(b, False)
            batch(BATCHES - 1, True)

        @block.scalar
        def _(act):
            def root(b):
                act.wait_ge(var_ready, b + 1)
                nc.scalar.activation(std[:], mean_var[:, :, 1], ACT.Sqrt, bias=eps[:]).then_inc(std_ready, 1)

            def take_xnT(b, c, n):
                act.wait_ge(pj_full, n)
                nc.scalar.copy(xnT[:, c, :], pj[:, c % 2, :]).then_inc(pj_taken[c % 2], 1)

            def take_part(n, b, r):
                m, (kind, j) = qk_at(n), USES[n]
                if r == 0:
                    act.wait_ge(high_ready, b * N_QK + m + 1)
                ins = nc.scalar.copy((q3 if kind == "q" else k3)[0:HD, at_head(j, r), :],
                                     high[HD * r:HD * (r + 1), m % 2, :])
                if r == 3:
                    ins.then_inc(act_parts_ready, 1)

            def batch(b, last):
                for n in range(2):
                    for r in range(4):
                        take_part(n, b, r)
                for n in (2, 4):
                    act.wait_ge(pj_full, b * T_PER + 4 + n + 1)
                    nc.scalar.copy(v[:, n - 2, :], pj[:, n % 2, :]).then_inc(pj_taken[n % 2], 1)
                for s in range(N_STEP):
                    kc = s % ST
                    if s >= 3:
                        act.wait_ge(pv_done, b * N_STEP + s - 2)
                    for r in range(4):
                        act.wait_ge(sc_full, b * N_SC + 4 * s + r + 1)
                        nc.scalar.activation(w[:, s % 3, r, P * kc:SEQ], sc[:, r % 2, P * kc:SEQ], ACT.Relu,
                                             bias=shift[:], scale=ATTN_SCALE).then_inc(sc_taken, 1)
                        if r % 2 == 1 and s < 2 * (N_PROJ - NEXT):
                            take_part(NEXT + s // 2, b, s % 2 * 2 + r // 2)
                    if s == ST - 1 and not last:
                        root(b + 1)
                if not last:
                    for c in range(CC):
                        take_xnT(b + 1, c, b * T_PER + 4 + N_PROJ + c + 1)

            act.wait_ge(zeroed, 2)
            root(0)
            for c in range(CC):
                take_xnT(0, c, c + 1)
            batch(0, False)
            with act.Fori(1, BATCHES - 1) as b:
                batch(b, False)
            batch(BATCHES - 1, True)

        @block.vector
        def _(dve):
            def normalise(b, steps):
                dve.wait_ge(x_loaded, b * 16 + 16)
                layernorm_tiles(dve, steps, lambda i: tile_row(X, b * ST + i), stats, mean_var, ST,
                                dve_carrier[:], eps[:])\
                    .then_inc(var_ready, 1)
                dve.wait_ge(std_ready, b + 1)
                steps.mark(dve.reciprocal(rstd[:], std[:]))
                steps.wait()
                for i in range(ST):
                    ins = dve.tensor_scalar(xn[:, i, :], X[:, bass.ds(b * ST + i, 1), :].rearrange("p t c -> p (t c)"),
                                            mean_var[:, i, 0:1], rstd[:, i:i + 1], ALU.subtract, ALU.mult)
                ins.then_inc(xn_ready, 1)

            def divide(quad, b, steps):
                dve.wait_ge(pv_done, b * N_STEP + ST * (quad + 1))
                if quad >= 1:
                    dve.wait_ge(attn_ready, b * QUADS + quad)
                steps.mark(dve.tensor_scalar(sums[:], den[:, quad % 2, :], ATTN_EPS, None, ALU.add))
                steps.wait()
                steps.mark(dve.reciprocal(sums[:], sums[:]))
                steps.wait()
                dve.tensor_tensor(attnT[:, quad, :], num[:, quad % 2, :], sums[:], ALU.mult).then_inc(attn_ready, 1)

            PER_TURN = 2 * QUADS + 2

            def take_parts(n, b):
                m, (kind, j) = qk_at(n), USES[n]
                dst, at_low, again = (q3, 1, 2) if kind == "q" else (k3, 2, 1)
                dve.wait_ge(pj_full, b * T_PER + 4 + n + 1)
                if not (isinstance(b, int) and b == 0 and m < 2):
                    dve.wait_ge(act_parts_ready, b * N_QK + m - 1)
                    dve.wait_ge(dve_parts_ready, b * N_QK + m - 1)
                dve.tensor_scalar(high[:, m % 2, :].bitcast(U32), pj[:, n % 2, :].bitcast(U32), 0xFFFFF000, None,
                                  ALU.bitwise_and).then_inc(high_ready, 1)
                dve.wait_ge(high_ready, b * N_QK + m + 1)
                dve.tensor_tensor(low[:, m % 2, :], pj[:, n % 2, :], high[:, m % 2, :], ALU.subtract)\
                    .then_inc(pj_taken[n % 2], 1)
                dve.wait_ge(pj_taken[n % 2], taken(n + 2, b))
                for block_at, src, heads in ((at_low, low, range(4)), (again, high, range(4))):
                    for r in heads:
                        ins = dve.tensor_copy(dst[HD * block_at:HD * (block_at + 1), at_head(j, r), :],
                                              src[HD * r:HD * (r + 1), m % 2, :])
                ins.then_inc(dve_parts_ready, 1)

            def batch(b, last):
                steps = Steps(dve, dve_steps, b * PER_TURN + 2)
                take_parts(0, b)
                take_parts(1, b)
                for n in (3, 5):
                    dve.wait_ge(pj_full, b * T_PER + 4 + n + 1)
                    dve.tensor_copy(v[:, n - 2, :], pj[:, n % 2, :]).then_inc(pj_taken[n % 2], 1)
                take_parts(NEXT, b)
                take_parts(NEXT + 1, b)
                if not last:
                    normalise(b + 1, steps)
                for quad in range(QUADS):
                    if quad < QUADS - 2:
                        take_parts(NEXT + 2 + 2 * quad, b)
                        take_parts(NEXT + 3 + 2 * quad, b)
                    divide(quad, b, steps)
                for i in range(ST):
                    dve.wait_ge(pj_full, b * T_PER + 4 + (N_PROJ if last else N_PROJ + CC) + i + 1)
                    xt = X[:, bass.ds(b * ST + i, 1), :].rearrange("p t c -> p (t c)")
                    dve.tensor_tensor(xt, xt, pj[:, i % 2, :], ALU.add).then_inc(pj_taken[i % 2], 1)

            dve.wait_ge(zeroed, 2)
            normalise(0, Steps(dve, dve_steps))
            batch(0, False)
            with dve.Fori(1, BATCHES - 1) as b:
                batch(b, False)
            batch(BATCHES - 1, True)


E1 = 8
TOP1 = 2
H1 = 256
HC1 = H1 // P
HS1 = 512
HSC1 = HS1 // P
GROUP = 4
GROUPS = TILES // GROUP
MAX_TILES1 = (TOKENS * TOP1 + E1 * (P - 1)) // P
PAIRS1 = (MAX_TILES1 + 1) // 2
SLOTS1 = E1 * TOKENS + P * (2 * PAIRS1 - TOKENS * TOP1 // P)
ROWS = TOKENS + P


def tile_row(X, t):
    return X[:, bass.ds(t, 1), :].rearrange("p t c -> p (t c)")


def group_rows(x, g):
    return x.rearrange("(t p) c -> p t c", p=P)[:, GROUP * g:GROUP * (g + 1), :]


def first_ffn_shared(nc, X, ident, ones, before, gate_w, sh_gate, sh_up, sh_down, w_gate, w_up, w13, xs, table,
                     weight_all, slot_all, tile_expert, tile_slot, w_p):
    with ExitStack() as ctx:
        sb = lambda name, shape, dt=F32: ctx.enter_context(nc.sbuf_tensor(name, shape, dt))
        sem = lambda name: ctx.enter_context(nc.semaphore(name))
        ps = lambda name, shape: ctx.enter_context(nc.psum_tensor(name, shape, F32))

        w_g, w_u, w_d = (w_p[:, :, C * j:C * (j + 1)] for j in range(3))
        w_route = sb("b_wroute", [P, CC, E1 + 1])
        eps = sb("b_eps", [P, 1])
        carrier = sb("b_carrier", [P, 8])
        empty = sb("b_empty", [P, SLOTS1 // P], U32)
        zrow = sb("b_zrow", [P, C])
        expert_iota = sb("b_expert_iota", [P, E1])
        region = sb("b_region", [P, E1])
        token_id = sb("b_token_id", [P, TILES])
        stats = sb("b_stats", [P, GROUP, 6])
        mean_var = sb("b_mean_var", [P, GROUP, 2])
        std = sb("b_std", [P, GROUP])
        rstd = sb("b_rstd", [P, GROUP])
        xn = sb("b_xn", [P, GROUP, C])
        xnT = sb("b_xnT", [P, CC, GROUP * P])
        hT = sb("b_hT", [P, HSC1, GROUP * P])
        sil = sb("b_sil", [P, 2, GROUP * P])
        logits = sb("b_logits", [P, GROUP, E1 + 1])
        best = sb("b_best", [P, GROUP, 8])
        best_i = sb("b_best_i", [P, GROUP, 8], U32)
        best_f = sb("b_best_f", [P, GROUP, TOP1])
        gap = sb("b_gap", [P, GROUP, 3])
        gates = sb("b_gates", [P, GROUP, 3])
        onehot = sb("b_onehot", [P, GROUP, TOP1, E1])
        chosen = sb("b_chosen", [P, GROUP, E1])
        total = sb("b_total", [P, E1])
        base = sb("b_base", [P, E1])
        place = sb("b_place", [P, GROUP, E1])
        picked = sb("b_picked", [P, GROUP, TOP1, E1])
        slot_f = sb("b_slot_f", [P, GROUP, TOP1])
        slot_now = sb("b_slot_now", [P, GROUP, TOP1], U32)
        token_now = sb("b_token_now", [P, GROUP], U32)
        n_tiles = sb("b_n_tiles", [P, E1])
        n_tiles_i = sb("b_n_tiles_i", [P, E1], I32)
        tiles_before = sb("b_tiles_before", [P, E1])
        tile_iota = sb("b_tile_iota", [P, 2 * PAIRS1])
        compared = sb("b_compared", [P, 2 * PAIRS1, E1])
        t_expert = sb("b_t_expert", [P, 2 * PAIRS1])
        t_start = sb("b_t_start", [P, 2 * PAIRS1])
        expert_all = sb("b_expert_all", [P, TILES, TOP1])
        slot_all_f = sb("b_slot_all_f", [P, TILES, TOP1])
        shift = sb("b_shift", [P, E1])
        moved = sb("b_moved", [P, TILES, TOP1])

        up = ps("b_up", [P, 4, GROUP * P])
        pj = ps("b_pj", [P, 2, C])
        lg = ps("b_lg", [P, GROUP, E1 + 1])
        cnt = ps("b_cnt", [P, GROUP + 1, E1])

        w_loaded = sem("b_w_loaded")
        set_up = sem("b_set_up")
        rows_zeroed = sem("b_rows_zeroed")
        var_ready = sem("b_var_ready")
        std_ready = sem("b_std_ready")
        xn_ready = sem("b_xn_ready")
        xn_stored = sem("b_xn_stored")
        pj_full = sem("b_pj_full")
        pj_taken = [sem("b_pj_taken0"), sem("b_pj_taken1")]
        lg_full = sem("b_lg_full")
        gap_ready = sem("b_gap_ready")
        gates_ready = sem("b_gates_ready")
        chosen_ready = sem("b_chosen_ready")
        cnt_full = sem("b_cnt_full")
        up_full = sem("b_up_full")
        sil_ready = sem("b_sil_ready")
        h_ready = sem("b_h_ready")
        slots_ready = sem("b_slots_ready")
        scattered = sem("b_scattered")
        steps_sem = sem("b_steps")
        carried = sem("b_carried")
        SET_UP = 8

        block = ctx.enter_context(nc.Block())

        @block.sync
        def _(sp):
            sp.dma_start(w_route[:], gate_w.rearrange("(c p) e -> p c e", p=P)).then_inc(w_loaded, 16)
            for dst, src in ((w_g, sh_gate), (w_u, sh_up), (w_d, sh_down)):
                sp.dma_start(dst[:], src.rearrange("(c p) o -> p c o", p=P)).then_inc(w_loaded, 16)
            sp.wait_ge(set_up, SET_UP)
            sp.dma_start(table.rearrange("(p s) one -> p (s one)", p=P), empty[:]).then_inc(rows_zeroed, 16)
            sp.dma_start(xs[TOKENS:ROWS, :], zrow[:]).then_inc(rows_zeroed, 16)
            for e in range(E1):
                for k, src in enumerate((w_gate, w_up)):
                    sp.dma_start(w13[:, CC * e:CC * (e + 1), H1 * k:H1 * (k + 1)],
                                 src[e].rearrange("(c p) f -> p c f", p=P)).then_inc(before, 16)
            for g in range(GROUPS):
                sp.wait_ge(xn_ready, g + 1)
                sp.dma_start(group_rows(xs[0:TOKENS, :], g), xn[:]).then_inc(xn_stored, 16)
            sp.wait_ge(xn_stored, 16 * GROUPS)
            sp.wait_ge(rows_zeroed, 32)

        @block.gpsimd
        def _(pool):
            nc.gpsimd.memset(eps[:], LN_EPS).then_inc(set_up, 1)
            nc.gpsimd.memset(total[:], 0.0).then_inc(set_up, 1)
            nc.gpsimd.memset(zrow[:], 0.0).then_inc(set_up, 1)
            nc.gpsimd.iota(empty[:], [[0, SLOTS1 // P]], base=TOKENS, channel_multiplier=0).then_inc(set_up, 1)
            nc.gpsimd.iota(expert_iota[:], [[1, E1]], base=0, channel_multiplier=0,
                           allow_small_or_imprecise_dtypes=True).then_inc(set_up, 1)
            nc.gpsimd.iota(region[:], [[TOKENS, E1]], base=0, channel_multiplier=0,
                           allow_small_or_imprecise_dtypes=True).then_inc(set_up, 1)
            nc.gpsimd.iota(token_id[:], [[P, TILES]], base=0, channel_multiplier=1,
                           allow_small_or_imprecise_dtypes=True).then_inc(set_up, 1)
            nc.gpsimd.iota(tile_iota[:], [[1, 2 * PAIRS1]], base=0, channel_multiplier=0,
                           allow_small_or_imprecise_dtypes=True).then_inc(set_up, 1)
            pool.wait_ge(rows_zeroed, 32)
            pool.wait_ge(set_up, SET_UP)

            def turn(g):
                pool.wait_ge(slots_ready, g + 1)
                pool.wait_ge(carried, g)
                nc.gpsimd.tensor_tensor(carrier[:, 0:1], eps[:], eps[:], ALU.add).then_inc(carried, 1)
                for i in range(GROUP):
                    for k in range(TOP1):
                        nc.gpsimd.indirect_dma_start(
                            table, bass.IndirectOffsetOnAxis(ap=slot_now[:, i, k:k + 1], axis=0),
                            token_now[:, i:i + 1], None).then_inc(scattered, 16)

            turn(0)
            with pool.Fori(1, GROUPS) as g:
                turn(g)
            pool.wait_ge(scattered, 16 * GROUPS * GROUP * TOP1)

        PJ = 8

        @block.tensor
        def _(pe):
            def bank_free(u, g):
                pe.wait_ge(pj_taken[u % 2], g * (PJ // 2) + 2 + u // 2)

            def transposes(g, first):
                pe.wait_ge(xn_ready, g + 1)
                for c in range(CC):
                    if not first:
                        bank_free(c, g - 1)
                    elif c >= 2:
                        pe.wait_ge(pj_taken[c % 2], 1)
                    for i in range(GROUP):
                        ins = pe.transpose(pj[:, c % 2, P * i:P * (i + 1)], xn[:, i, P * c:P * (c + 1)], ident[:])
                    ins.then_inc(pj_full, 1)

            def group(g, last):
                for k in range(2):
                    pe.wait_ge(pj_taken[k], g * (PJ // 2) + 2)
                pe.wait_ge(chosen_ready, g)
                for i in range(GROUP):
                    for c in range(CC):
                        ins = pe.matmul(lg[:, i, :], xnT[:, c, P * i:P * (i + 1)], w_route[:, c, :],
                                        start=(c == 0), stop=(c == CC - 1))
                ins.then_inc(lg_full, 1)
                for f in range(HSC1):
                    pe.wait_ge(h_ready, g * HSC1 + max(f - 1, 0))
                    for k, w in ((0, w_g), (1, w_u)):
                        for c in range(CC):
                            ins = pe.matmul(up[:, 2 * (f % 2) + k, :], w[:, c, P * f:P * (f + 1)], xnT[:, c, :],
                                            start=(c == 0), stop=(c == CC - 1))
                    ins.then_inc(up_full, 1)
                pe.wait_ge(chosen_ready, g + 1)
                pe.wait_ge(slots_ready, g)
                for j in range(GROUP):
                    pe.matmul(cnt[:, j, :], ones[:, P:2 * P], chosen[:, j, :], start=(j == 0), stop=True,
                              skip_group_check=True)
                    ins = pe.matmul(cnt[:, j + 1:, :], ones[:, 0:P],
                                    chosen[:, j:j + 1, :].broadcast_to([P, GROUP - j, E1]),
                                    start=(j == 0), stop=(j == GROUP - 1), skip_group_check=True)
                ins.then_inc(cnt_full, 1)
                if not last:
                    transposes(g + 1, False)
                pe.wait_ge(h_ready, (g + 1) * HSC1)
                for i in range(GROUP):
                    bank_free((0 if last else 4) + i, g)
                    for f in range(HSC1):
                        ins = pe.matmul(pj[:, i % 2, :], hT[:, f, P * i:P * (i + 1)], w_d[:, f, :],
                                        start=(f == 0), stop=(f == HSC1 - 1))
                    ins.then_inc(pj_full, 1)

            transposes(0, True)
            pe.wait_ge(w_loaded, 64)
            group(0, False)
            with pe.Fori(1, GROUPS - 1) as g:
                group(g, False)
            group(GROUPS - 1, True)

        @block.scalar
        def _(act):
            def root(g):
                act.wait_ge(var_ready, g + 1)
                nc.scalar.activation(std[:], mean_var[:, :, 1], ACT.Sqrt, bias=eps[:]).then_inc(std_ready, 1)

            def take_xnT(c, n):
                act.wait_ge(pj_full, n)
                nc.scalar.copy(xnT[:, c, :], pj[:, c % 2, :]).then_inc(pj_taken[c % 2], 1)

            def group(g, last):
                act.wait_ge(gap_ready, g + 1)
                nc.scalar.activation(gates[:], gap[:], ACT.Sigmoid).then_inc(gates_ready, 1)
                if not last:
                    root(g + 1)
                for f in range(HSC1):
                    act.wait_ge(up_full, g * HSC1 + f + 1)
                    act.wait_ge(h_ready, g * HSC1 + max(f - 1, 0))
                    nc.scalar.activation(sil[:, f % 2, :], up[:, 2 * (f % 2), :], ACT.Silu).then_inc(sil_ready, 1)
                if not last:
                    for c in range(CC):
                        take_xnT(c, g * PJ + 4 + c + 1)

            act.wait_ge(set_up, SET_UP)
            root(0)
            for c in range(CC):
                take_xnT(c, c + 1)
            group(0, False)
            with act.Fori(1, GROUPS - 1) as g:
                group(g, False)
            group(GROUPS - 1, True)

        @block.vector
        def _(dve):
            def normalise(g, steps, first):
                layernorm_tiles(dve, steps, lambda i: tile_row(X, g * GROUP + i), stats, mean_var, GROUP,
                                carrier[:, 4:5], eps[:]).then_inc(var_ready, 1)
                dve.wait_ge(std_ready, g + 1)
                steps.mark(dve.reciprocal(rstd[:], std[:]))
                steps.wait()
                if not first:
                    dve.wait_ge(xn_stored, g * 16)
                for i in range(GROUP):
                    ins = dve.tensor_scalar(xn[:, i, :], tile_row(X, g * GROUP + i),
                                            mean_var[:, i, 0:1], rstd[:, i:i + 1], ALU.subtract, ALU.mult)
                ins.then_inc(xn_ready, 1)

            def choose(g, steps):
                dve.wait_ge(lg_full, g + 1)
                steps.mark(dve.tensor_copy(logits[:], lg[:]))
                steps.wait()
                dve.tensor_copy(carrier[:, 5:6], eps[:])
                for i in range(GROUP):
                    ins = dve.max(best[:, i, :], logits[:, i, 0:E1])
                steps.mark(ins)
                steps.wait()
                dve.tensor_copy(carrier[:, 6:7], eps[:])
                for i in range(GROUP):
                    ins = dve.max_index(best_i[:, i, :], best[:, i, :], logits[:, i, 0:E1])
                steps.mark(ins)
                dve.tensor_tensor(gap[:, :, 0], best[:, :, 0], best[:, :, 1], ALU.subtract)
                dve.tensor_tensor(gap[:, :, 1], best[:, :, 1], best[:, :, 0], ALU.subtract)
                dve.tensor_copy(gap[:, :, 2], logits[:, :, E1]).then_inc(gap_ready, 1)
                steps.wait()
                steps.mark(dve.tensor_copy(best_f[:], best_i[:, :, 0:TOP1]))
                steps.wait()
                for k in range(TOP1):
                    ins = dve.tensor_tensor(onehot[:, :, k, :],
                                            expert_iota[:].unsqueeze(1).broadcast_to([P, GROUP, E1]),
                                            best_f[:, :, k:k + 1].broadcast_to([P, GROUP, E1]), ALU.is_equal)
                steps.mark(ins)
                steps.wait()
                dve.tensor_tensor(chosen[:], onehot[:, :, 0, :], onehot[:, :, 1, :], ALU.add).then_inc(chosen_ready, 1)

            def place_slots(g, steps):
                steps.mark(dve.tensor_tensor(base[:], total[:], region[:], ALU.add))
                dve.wait_ge(cnt_full, g + 1)
                steps.wait()
                steps.mark(dve.tensor_tensor(place[:], cnt[:, 0:GROUP, :],
                                             base[:].unsqueeze(1).broadcast_to([P, GROUP, E1]), ALU.add))
                steps.mark(dve.tensor_tensor(total[:], total[:], cnt[:, GROUP, :], ALU.add))
                steps.wait()
                for k in range(TOP1):
                    ins = dve.tensor_tensor(picked[:, :, k, :], onehot[:, :, k, :], place[:], ALU.mult)
                steps.mark(ins)
                steps.wait()
                steps.mark(dve.tensor_reduce(slot_f[:], picked[:], AX.X, ALU.add))
                steps.wait()
                dve.wait_ge(scattered, g * (16 * GROUP * TOP1))
                dve.tensor_copy(token_now[:], token_id[:, bass.ds(g * GROUP, GROUP)])
                dve.tensor_copy(slot_all_f[:, bass.ds(g * GROUP, GROUP), :], slot_f[:])
                dve.tensor_copy(expert_all[:, bass.ds(g * GROUP, GROUP), :], best_f[:])
                dve.tensor_copy(slot_now[:], slot_f[:]).then_inc(slots_ready, 1)
                dve.wait_ge(gates_ready, g + 1)
                steps.mark(dve.tensor_copy(weight_all[:, bass.ds(g * GROUP, GROUP), :], gates[:, :, 0:TOP1]))

            def count_tiles(steps):
                steps.mark(dve.tensor_scalar(n_tiles[:], total[:], float(P - 1), None, ALU.add))
                steps.wait()
                steps.mark(dve.tensor_copy(n_tiles_i[:], n_tiles[:]))
                steps.wait()
                steps.mark(dve.tensor_scalar(n_tiles_i[:], n_tiles_i[:], P.bit_length() - 1, None,
                                             ALU.arith_shift_right))
                steps.wait()
                steps.mark(dve.tensor_copy(n_tiles[:], n_tiles_i[:]))
                steps.wait()
                steps.mark(dve.tensor_copy(tiles_before[:, 0:1], n_tiles[:, 0:1]))
                for e in range(1, E1):
                    steps.wait()
                    steps.mark(dve.tensor_tensor(tiles_before[:, e:e + 1], tiles_before[:, e - 1:e],
                                                 n_tiles[:, e:e + 1], ALU.add))

            N_TILES = 2 * PAIRS1
            by_expert = lambda x, n: x[:].unsqueeze(1).broadcast_to([P, n, E1])
            past = compared[:, 0:N_TILES, :]

            def tile_experts(steps):
                steps.wait()
                steps.mark(dve.tensor_tensor(past, tile_iota[:].unsqueeze(2).broadcast_to([P, N_TILES, E1]),
                                             by_expert(tiles_before, N_TILES), ALU.is_ge))
                steps.wait()
                steps.mark(dve.tensor_reduce(t_expert[:], past, AX.X, ALU.add))
                steps.wait()
                steps.mark(dve.tensor_tensor(past, past, by_expert(n_tiles, N_TILES), ALU.mult))

            def tile_slots(steps):
                steps.wait()
                steps.mark(dve.tensor_reduce(t_start[:], past, AX.X, ALU.add))
                steps.wait()
                steps.mark(dve.tensor_tensor(t_start[:], tile_iota[:], t_start[:], ALU.subtract))
                steps.wait()
                steps.mark(dve.scalar_tensor_tensor(out=t_start[:], in0=t_expert[:], scalar=float(TOKENS // P),
                                                    in1=t_start[:], op0=ALU.mult, op1=ALU.add))
                steps.wait()
                steps.mark(dve.tensor_scalar(t_start[:], t_start[:], float(P), None, ALU.mult))
                steps.mark(dve.tensor_scalar(t_expert[:], t_expert[:], float(E1 - 1), None, ALU.min))
                steps.wait()
                dve.tensor_copy(tile_slot[:], t_start[:])
                dve.tensor_copy(tile_expert[:], t_expert[:])

            def output_rows(steps):
                steps.mark(dve.tensor_tensor(shift[:], tiles_before[:], n_tiles[:], ALU.subtract))
                steps.wait()
                steps.mark(dve.tensor_scalar(shift[:], shift[:], float(P), None, ALU.mult))
                steps.wait()
                steps.mark(dve.tensor_tensor(shift[:], shift[:], region[:], ALU.subtract))
                steps.wait()
                n = TILES * TOP1
                moves = compared[:, 0:n, :]
                experts = expert_all[:].rearrange("p t k -> p (t k)").unsqueeze(2).broadcast_to([P, n, E1])
                steps.mark(dve.tensor_tensor(moves, by_expert(expert_iota, n), experts, ALU.is_equal))
                steps.wait()
                steps.mark(dve.tensor_tensor(moves, moves, by_expert(shift, n), ALU.mult))
                steps.wait()
                steps.mark(dve.tensor_reduce(moved[:].rearrange("p t k -> p (t k)"), moves, AX.X, ALU.add))
                steps.wait()
                dve.tensor_tensor(slot_all[:], slot_all_f[:], moved[:], ALU.add)

            PER_TURN = 13

            def group(g, last):
                steps = Steps(dve, steps_sem, g * PER_TURN + 2)
                choose(g, steps)
                if not last:
                    normalise(g + 1, steps, False)
                for f in range(HSC1):
                    dve.wait_ge(sil_ready, g * HSC1 + f + 1)
                    dve.tensor_tensor(hT[:, f, :], sil[:, f % 2, :], up[:, 2 * (f % 2) + 1, :], ALU.mult)\
                        .then_inc(h_ready, 1)
                place_slots(g, steps)
                assert steps.n == PER_TURN - (2 if last else 0), steps.n
                for i in range(GROUP):
                    dve.wait_ge(pj_full, g * PJ + 4 + (0 if last else 4) + i + 1)
                    dve.scalar_tensor_tensor(out=tile_row(X, g * GROUP + i), in0=pj[:, i % 2, :],
                                             scalar=gates[:, i, 2:3], in1=tile_row(X, g * GROUP + i),
                                             op0=ALU.mult, op1=ALU.add).then_inc(pj_taken[i % 2], 1)
                    if last:
                        (count_tiles, tile_experts, tile_slots, output_rows)[i](steps)

            dve.wait_ge(set_up, SET_UP)
            normalise(0, Steps(dve, steps_sem), True)
            group(0, False)
            with dve.Fori(1, GROUPS - 1) as g:
                group(g, False)
            group(GROUPS - 1, True)
def first_ffn_experts(nc, ident, w13, w13_loaded, w2, w_down, xs, table, ys, tile_expert, tile_slot, w_qkv, w_p,
                      qkv_loaded):
    with ExitStack() as ctx:
        sb = lambda name, shape, dt=F32: ctx.enter_context(nc.sbuf_tensor(name, shape, dt))
        sem = lambda name: ctx.enter_context(nc.semaphore(name))
        ps = lambda name, shape: ctx.enter_context(nc.psum_tensor(name, shape, F32))

        ids = sb("c_ids", [P, 2, 1], U32)
        xg = sb("c_xg", [P, 2, C])
        xgT = sb("c_xgT", [P, 2, CC * P])
        sil = sb("c_sil", [P, 2, H1])
        h = sb("c_h", [P, 2, H1])
        hT = sb("c_hT", [P, 2, HC1 * P])
        y = sb("c_y", [P, 2, C])
        carrier = sb("c_carrier", [P, 2])

        up = ps("c_up", [P, 2, 2 * H1])
        yp = ps("c_yp", [P, 2, C])
        xp = ps("c_xp", [P, 2, CC * P])
        hp = ps("c_hp", [P, 2, 512])

        w2_loaded = sem("c_w2_loaded")
        ids_loaded = [sem("c_ids_loaded0"), sem("c_ids_loaded1")]
        gathered = [sem("c_gathered0"), sem("c_gathered1")]
        stored = [sem("c_stored0"), sem("c_stored1")]
        x_turned = sem("c_x_turned")
        xgT_ready = sem("c_xgT_ready")
        up_full = sem("c_up_full")
        sil_ready = sem("c_sil_ready")
        h_ready = sem("c_h_ready")
        h_turned = sem("c_h_turned")
        hT_ready = sem("c_hT_ready")
        y_full = sem("c_y_full")
        y_ready = sem("c_y_ready")
        carried = sem("c_carried")
        N = 2 * PAIRS1

        def turns(eng, tile):
            for p in range(2):
                tile(0, p, "first")
            for p in range(2):
                tile(1, p, "")
            with eng.Fori(2, PAIRS1 - 1) as ii:
                for p in range(2):
                    tile(ii, p, "")
            for p in range(2):
                tile(PAIRS1 - 1, p, "last")

        block = ctx.enter_context(nc.Block())

        @block.sync
        def _(sp):
            for p in range(2):
                sp.wait_ge(gathered[p], 16)
            for e in range(E1):
                sp.dma_start(w2[:, HC1 * e:HC1 * (e + 1), :],
                             w_down[e].rearrange("(c p) o -> p c o", p=P)).then_inc(w2_loaded, 16)
            sp.dma_start(w_p[:], w_qkv.rearrange("(c p) o -> p c o", p=P)).then_inc(qkv_loaded, 16)

        @block.gpsimd
        def _(pool):
            def load_ids(ii, p, start):
                slot = pool.value_load(tile_slot[0:1, bass.ds(ii * 2 + p, 1)], min_val=0, max_val=SLOTS1 - P)
                if not start:
                    pool.wait_ge(gathered[p], ii * 16)
                pool.dma_start(ids[:, p, :], table[bass.ds(slot, P), :]).then_inc(ids_loaded[p], 16)

            def tile(ii, p, which):
                if not (which == "last" and p == 1):
                    load_ids(ii + 1 if p else ii, 1 - p, which == "first" and p == 0)
                pool.wait_ge(ids_loaded[p], ii * 16 + 16)
                if which != "first":
                    pool.wait_ge(x_turned, ii * 2 + p - 1)
                pool.wait_ge(carried, ii * 2 + p)
                nc.gpsimd.tensor_tensor(carrier[:, 0:1], ident[:, 0:1], ident[:, 0:1], ALU.add).then_inc(carried, 1)
                nc.gpsimd.indirect_dma_start(xg[:, p, :], None, xs,
                                             bass.IndirectOffsetOnAxis(ap=ids[:, p, :], axis=0))\
                    .then_inc(gathered[p], 16)

            load_ids(0, 0, True)
            turns(pool, tile)

        @block.tensor
        def _(pe):
            def turn_x(ii, p, start):
                pe.wait_ge(gathered[p], ii * 16 + 16)
                if not start:
                    pe.wait_ge(xgT_ready, ii * 2 + p - 1)
                for c in range(CC):
                    ins = pe.transpose(xp[:, p, P * c:P * (c + 1)], xg[:, p, P * c:P * (c + 1)], ident[:])
                ins.then_inc(x_turned, 1)

            def load_expert(ii, p):
                return pe.value_load(tile_expert[0:1, bass.ds(ii * 2 + p, 1)], min_val=0, max_val=E1 - 1)

            def turn_h(ii, p, start):
                pe.wait_ge(h_ready, ii * 2 + p + 1)
                if not start:
                    pe.wait_ge(hT_ready, ii * 2 + p - 1)
                for f in range(HC1):
                    ins = pe.transpose(hp[:, p, P * f:P * (f + 1)], h[:, p, P * f:P * (f + 1)], ident[:])
                ins.then_inc(h_turned, 1)

            def down(ii, p, start, e):
                pe.wait_ge(hT_ready, ii * 2 + p + 1)
                if not start:
                    pe.wait_ge(y_ready, ii * 2 + p - 1)
                for f in range(HC1):
                    ins = pe.matmul(yp[:, p, :], hT[:, p, P * f:P * (f + 1)],
                                    w2[:, bass.ds(e * HC1 + f, 1), :].rearrange("p a c -> p (a c)"),
                                    start=(f == 0), stop=(f == HC1 - 1))
                ins.then_inc(y_full, 1)

            def tile(ii, p, which):
                first = which == "first" and p == 0
                before = (ii if p else ii - 1, 1 - p)
                e = load_expert(ii, p)
                if not first:
                    e_before = load_expert(*before)
                pe.wait_ge(xgT_ready, ii * 2 + p + 1)
                if which != "first":
                    pe.wait_ge(h_ready, ii * 2 + p - 1)
                for c in range(CC):
                    ins = pe.matmul(up[:, p, :], xgT[:, p, P * c:P * (c + 1)],
                                    w13[:, bass.ds(e * CC + c, 1), :].rearrange("p a f -> p (a f)"),
                                    start=(c == 0), stop=(c == CC - 1))
                    if c == 1 and not first:
                        turn_h(*before, which == "first")
                ins.then_inc(up_full, 1)
                if not (which == "last" and p == 1):
                    turn_x(ii + 1 if p else ii, 1 - p, first)
                if not first:
                    if which == "first":
                        pe.wait_ge(w2_loaded, 16 * E1)
                    down(*before, which == "first", e_before)

            turn_x(0, 0, True)
            pe.wait_ge(w13_loaded, 16 * 2 * E1)
            turns(pe, tile)
            turn_h(PAIRS1 - 1, 1, False)
            down(PAIRS1 - 1, 1, False, load_expert(PAIRS1 - 1, 1))

        @block.scalar
        def _(act):
            def take_x(ii, p, start):
                act.wait_ge(x_turned, ii * 2 + p + 1)
                if not start:
                    act.wait_ge(up_full, ii * 2 + p - 1)
                nc.scalar.copy(xgT[:, p, :], xp[:, p, :]).then_inc(xgT_ready, 1)

            def store(ii, p):
                act.wait_ge(y_ready, ii * 2 + p + 1)
                act.dma_start(ys[bass.ds(ii * (2 * P) + p * P, P), :], y[:, p, :]).then_inc(stored[p], 16)

            def tile(ii, p, which):
                act.wait_ge(up_full, ii * 2 + p + 1)
                if which != "first":
                    act.wait_ge(h_ready, ii * 2 + p - 1)
                nc.scalar.activation(sil[:, p, :], up[:, p, 0:H1], ACT.Silu).then_inc(sil_ready, 1)
                if not (which == "last" and p == 1):
                    take_x(ii + 1 if p else ii, 1 - p, which == "first" and p == 0)

                if which != "first":
                    store(ii - 1, p)

            take_x(0, 0, True)
            turns(act, tile)
            for p in range(2):
                store(PAIRS1 - 1, p)
            for p in range(2):
                act.wait_ge(stored[p], 16 * PAIRS1)

        @block.vector
        def _(dve):
            def take_y(ii, p, start):
                dve.wait_ge(y_full, ii * 2 + p + 1)
                if not start:
                    dve.wait_ge(stored[p], ii * 16)
                dve.tensor_copy(y[:, p, :], yp[:, p, :]).then_inc(y_ready, 1)

            def take_h(ii, p, start):
                dve.wait_ge(h_turned, ii * 2 + p + 1)
                if not start:
                    dve.wait_ge(y_full, ii * 2 + p - 1)
                dve.tensor_copy(hT[:, p, :], hp[:, p, 0:HC1 * P]).then_inc(hT_ready, 1)

            def tile(ii, p, which):
                before = (ii if p else ii - 1, 1 - p)
                first = which == "first" and p == 0
                if not first:
                    take_h(*before, which == "first")
                dve.wait_ge(sil_ready, ii * 2 + p + 1)
                if which != "first":
                    dve.wait_ge(h_turned, ii * 2 + p - 1)
                dve.tensor_tensor(h[:, p, :], sil[:, p, :], up[:, p, H1:2 * H1], ALU.mult).then_inc(h_ready, 1)
                if not first:
                    take_y(*before, which == "first")

            turns(dve, tile)
            take_h(PAIRS1 - 1, 1, False)
            take_y(PAIRS1 - 1, 1, False)


POS = 8
CHUNKS = TILES // POS
HEAD_START = 5
LAG = 3
XN_RING = 2
Q_RING = 4


def second_attention(nc, X, ident, ones, ys, slot_all, weight_all, w_out, w_p, qkv_loaded):
    with ExitStack() as ctx:
        sb = lambda name, shape, dt=F32: ctx.enter_context(nc.sbuf_tensor(name, shape, dt))
        sem = lambda name: ctx.enter_context(nc.semaphore(name))
        ps = lambda name, shape: ctx.enter_context(nc.psum_tensor(name, shape, F32))

        w_o = sb("d_wo", [P, CC, C])
        minus_half = sb("d_minus_half", [P, 1])
        zero = sb("d_zero", [P, 1])
        scaled = sb("d_scaled", [P, POS])
        offset = sb("d_offset", [P, POS])
        carrier = sb("d_carrier", [P, 4])
        slot_now = sb("d_slot_now", [P, POS, TOP1], U32)
        y = sb("d_y", [P, 2, TOP1, C])
        stats = sb("d_stats", [P, 6])
        mean_var = sb("d_mean_var", [P, POS, 2])
        rstd = sb("d_rstd", [P, POS])
        xn = sb("d_xn", [P, XN_RING, C])
        xnT = sb("d_xnT", [P, 2, C])
        q = sb("d_q", [P, Q_RING, C])
        k = sb("d_k", [P, 2 * POS, C])
        v = sb("d_v", [P, 2 * POS, C])
        prod = sb("d_prod", [P, POS, C])
        s = sb("d_s", [P, POS, HEADS])
        e = sb("d_e", [P, POS, HEADS])
        most = sb("d_most", [P, HEADS])
        ao = q
        aoT = sb("d_aoT", [P, 2, C])

        qkv_p = ps("d_qkv_p", [P, 3, C])
        xp = ps("d_xp", [P, C])
        ap = ps("d_ap", [P, C])
        op = ps("d_op", [P, 2, C])

        w_o_loaded = sem("d_w_o_loaded")
        set_up = sem("d_set_up")
        slots_ready = sem("d_slots_ready")
        gathered = [sem("d_gathered0"), sem("d_gathered1")]
        combined = sem("d_combined")
        var_ready = sem("d_var_ready")
        root_steps = sem("d_root_steps")
        rstd_ready = sem("d_rstd_ready")
        xn_ready = sem("d_xn_ready")
        x_turned = sem("d_x_turned")
        xnT_ready = sem("d_xnT_ready")
        qkv_full = sem("d_qkv_full")
        qkv_ready = sem("d_qkv_ready")
        s_ready = sem("d_s_ready")
        e_ready = sem("d_e_ready")
        ao_ready = sem("d_ao_ready")
        a_turned = sem("d_a_turned")
        aoT_ready = sem("d_aoT_ready")
        o_full = sem("d_o_full")
        o_taken = sem("d_o_taken")
        steps_sem = sem("d_steps")
        carried = sem("d_carried")

        block = ctx.enter_context(nc.Block())

        def tile(ch, l):
            return tile_row(X, ch + l // POS + (l % POS) * CHUNKS)

        def chunks(eng, chunk):
            chunk(0, "first")
            with eng.Fori(1, CHUNKS - 1) as ch:
                chunk(ch, "")
            chunk(CHUNKS - 1, "last")

        @block.sync
        def _(sp):
            sp.dma_start(w_o[:], w_out.rearrange("(c p) o -> p c o", p=P)).then_inc(w_o_loaded, 16)

        @block.gpsimd
        def _(pool):
            nc.gpsimd.memset(minus_half[:], -0.5).then_inc(set_up, 1)
            nc.gpsimd.memset(zero[:], 0.0).then_inc(set_up, 1)
            pool.wait_ge(set_up, 2)

            def gather(m, l, slots):
                pool.wait_ge(slots_ready, slots)
                if not (isinstance(m, int) and m < 2):
                    pool.wait_ge(combined, m - 1)
                pool.wait_ge(carried, m)
                nc.gpsimd.tensor_tensor(carrier[:, 0:1], minus_half[:], minus_half[:], ALU.add).then_inc(carried, 1)
                for t in range(TOP1):
                    nc.gpsimd.indirect_dma_start(y[:, l % 2, t, :], None, ys, bass.IndirectOffsetOnAxis(
                        ap=slot_now[:, l, t:t + 1], axis=0)).then_inc(gathered[l % 2], 16)

            def root(m, l):
                pool.wait_ge(var_ready, m + 1)
                nc.gpsimd.tensor_tensor(rstd[:, l:l + 1], mean_var[:, l, 1:2], minus_half[:], ALU.pow)\
                    .then_inc(root_steps, 1)
                pool.wait_ge(root_steps, 2 * m + 1)
                nc.gpsimd.tensor_tensor(scaled[:, l:l + 1], mean_var[:, l, 0:1], rstd[:, l:l + 1], ALU.mult)\
                    .then_inc(root_steps, 1)
                pool.wait_ge(root_steps, 2 * m + 2)
                nc.gpsimd.tensor_tensor(offset[:, l:l + 1], zero[:], scaled[:, l:l + 1], ALU.subtract)\
                    .then_inc(rstd_ready, 1)

            def chunk(ch, which):
                for l in range(POS):
                    m = ch * POS + l
                    gather(m, l, ch + 1)
                    if not (which == "first" and l == 0):
                        root(m - 1, (l - 1) % POS)

            chunks(pool, chunk)
            root(TILES - 1, POS - 1)

        @block.tensor
        def _(pe):
            def turn_x(n, l):
                pe.wait_ge(xn_ready, n + 1)
                pe.wait_ge(xnT_ready, n)
                for c in range(CC):
                    ins = pe.transpose(xp[:, P * c:P * (c + 1)], xn[:, l % XN_RING, P * c:P * (c + 1)], ident[:])
                ins.then_inc(x_turned, 1)

            def project(n, l, j, start):
                if not start:
                    pe.wait_ge(qkv_ready, n * 3 - 2 + j)
                for c in range(CC):
                    ins = pe.matmul(qkv_p[:, j, :], xnT[:, l % 2, P * c:P * (c + 1)], w_p[:, c, C * j:C * (j + 1)],
                                    start=(c == 0), stop=(c == CC - 1))
                ins.then_inc(qkv_full, 1)

            def turn_a(n, l):
                pe.wait_ge(ao_ready, n + 1)
                pe.wait_ge(aoT_ready, n)
                for c in range(CC):
                    ins = pe.transpose(ap[:, P * c:P * (c + 1)], ao[:, l % Q_RING, P * c:P * (c + 1)], ident[:])
                ins.then_inc(a_turned, 1)

            def output(n, l, start):
                pe.wait_ge(aoT_ready, n + 1)
                if not start:
                    pe.wait_ge(o_taken, n - 1)
                for c in range(CC):
                    ins = pe.matmul(op[:, l % 2, :], aoT[:, l % 2, P * c:P * (c + 1)], w_o[:, c, :],
                                    start=(c == 0), stop=(c == CC - 1))
                ins.then_inc(o_full, 1)

            def chunk(ch, which):
                for l in range(POS):
                    n = ch * POS + l
                    early = which == "first" and l < LAG
                    pe.wait_ge(xnT_ready, n + 1)
                    project(n, l, 0, which == "first" and l == 0)
                    if not (which == "last" and l == POS - 1):
                        turn_x(n + 1, l + 1)
                    project(n, l, 1, which == "first" and l == 0)
                    if not early:
                        turn_a(n - LAG, l - LAG)
                    project(n, l, 2, which == "first" and l == 0)
                    if not early:
                        output(n - LAG, l - LAG, which == "first" and l < LAG + 2)

            pe.wait_ge(qkv_loaded, 16)
            pe.wait_ge(w_o_loaded, 16)
            turn_x(0, 0)
            chunks(pe, chunk)
            for n in range(TILES - LAG, TILES):
                turn_a(n, n)
                output(n, n, False)

        @block.scalar
        def _(act):
            def normalise(ch, l):
                n = ch * POS + l
                act.wait_ge(rstd_ready, n + 1)
                if not (isinstance(ch, int) and n < XN_RING):
                    act.wait_ge(x_turned, n - XN_RING + 1)
                at = l % POS
                nc.scalar.activation(xn[:, l % XN_RING, :], tile(ch, l), ACT.Identity, bias=offset[:, at:at + 1],
                                     scale=rstd[:, at:at + 1]).then_inc(xn_ready, 1)

            def take_x(n, l):
                act.wait_ge(x_turned, n + 1)
                nc.scalar.copy(xnT[:, l % 2, :], xp[:]).then_inc(xnT_ready, 1)

            def take_qkv(n, l, j, side, start):
                act.wait_ge(qkv_full, n * 3 + j + 1)
                if j == 0:
                    if not start:
                        act.wait_ge(a_turned, n - Q_RING + 1)
                    nc.scalar.mul(q[:, l % Q_RING, :], qkv_p[:, 0, :], ATTN_SCALE).then_inc(qkv_ready, 1)
                else:
                    nc.scalar.copy(tile_row((k, v)[j - 1], side * POS + l), qkv_p[:, j, :]).then_inc(qkv_ready, 1)

            def exps(n, l):
                act.wait_ge(s_ready, n + 1)
                nc.scalar.activation(e[:, 0:l + 1, :], s[:, 0:l + 1, :], ACT.Exp).then_inc(e_ready, 1)

            def take_a(n, l):
                act.wait_ge(a_turned, n + 1)
                nc.scalar.copy(aoT[:, l % 2, :], ap[:]).then_inc(aoT_ready, 1)

            def chunk(ch, which):
                side = ch % 2
                for l in range(POS):
                    n = ch * POS + l
                    early = which == "first" and l < LAG
                    take_qkv(n, l, 0, side, which == "first" and l < Q_RING)
                    if not (which == "last" and l == POS - 1):
                        take_x(n + 1, l + 1)
                    if not (which == "last" and l >= POS - 2):
                        normalise(ch, l + 2)
                    take_qkv(n, l, 1, side, False)
                    if not early:
                        take_a(n - LAG, l - LAG)
                    take_qkv(n, l, 2, side, False)
                    if not (which == "first" and l == 0):
                        exps(n - 1, (l - 1) % POS)
                if which == "last":
                    exps(TILES - 1, POS - 1)

            normalise(0, 0)
            normalise(0, 1)
            take_x(0, 0)
            chunks(act, chunk)
            for n in range(TILES - LAG, TILES):
                take_a(n, n)

        @block.vector
        def _(dve):
            def carry(column):
                dve.tensor_copy(carrier[:, column:column + 1], minus_half[:])

            def slots(ch, first):
                by_chunk = slot_all[:].rearrange("p (l ch) t -> p l ch t", ch=CHUNKS)
                if not first:
                    for p in range(2):
                        dve.wait_ge(gathered[p], ch * (16 * TOP1 * POS // 2))
                    carry(1)
                dve.tensor_copy(slot_now[:], by_chunk[:, :, bass.ds(ch, 1), :].rearrange("p l c t -> p l (c t)"))\
                    .then_inc(slots_ready, 1)

            def combine(ch, l, steps):
                m = ch * POS + l
                x = tile(ch, l)
                dve.wait_ge(gathered[l % 2], (ch * (POS // 2) + l // 2 + 1) * (16 * TOP1))
                for t in range(TOP1):
                    weight = weight_all[:, bass.ds(ch + l * CHUNKS, 1), t:t + 1].rearrange("p a b -> p (a b)")
                    ins = dve.scalar_tensor_tensor(out=x, in0=y[:, l % 2, t, :], scalar=weight, in1=x,
                                                   op0=ALU.mult, op1=ALU.add)
                    if t == TOP1 - 1:
                        ins.then_inc(combined, 1)
                        dve.wait_ge(combined, m + 1)
                        carry(3)
                    else:
                        steps.mark(ins)
                        steps.wait()
                steps.mark(dve.bn_stats(stats[:], x))
                steps.wait()
                carry(2)
                steps.mark(dve.bn_aggr(mean_var[:, l, :], stats[:]))
                steps.wait()
                dve.tensor_scalar(mean_var[:, l, 1:2], mean_var[:, l, 1:2], LN_EPS, None, ALU.add)\
                    .then_inc(var_ready, 1)

            def take_output(n, x, l):
                dve.wait_ge(o_full, n + 1)
                dve.tensor_tensor(x, x, op[:, l % 2, :], ALU.add).then_inc(o_taken, 1)

            def scores(n, l, side, start, steps):
                m = l + 1
                dve.wait_ge(qkv_ready, n * 3 + 2)
                if not start:
                    dve.wait_ge(ao_ready, n)
                steps.mark(dve.tensor_tensor(prod[:, 0:m, :], k[:, bass.ds(side * POS, m), :],
                                             q[:, l % Q_RING:l % Q_RING + 1, :].broadcast_to([P, m, C]), ALU.mult))
                steps.wait()
                steps.mark(dve.tensor_reduce(s[:, 0:m, :], prod[:, 0:m, :].rearrange("p m (h d) -> p m h d", h=HEADS),
                                             AX.X, ALU.add))
                steps.wait()
                steps.mark(dve.tensor_reduce(most[:], s[:, 0:m, :].rearrange("p m h -> p h m"), AX.X, ALU.max))
                steps.wait()
                dve.tensor_tensor(s[:, 0:m, :], s[:, 0:m, :], most[:].unsqueeze(1).broadcast_to([P, m, HEADS]),
                                  ALU.subtract).then_inc(s_ready, 1)

            def average(n, l, side, steps):
                m = l + 1
                dve.wait_ge(e_ready, n + 1)
                steps.mark(dve.tensor_reduce(most[:], e[:, 0:m, :].rearrange("p m h -> p h m"), AX.X, ALU.add))
                steps.wait()
                steps.mark(dve.reciprocal(most[:], most[:]))
                steps.wait()
                steps.mark(dve.tensor_tensor(e[:, 0:m, :], e[:, 0:m, :],
                                             most[:].unsqueeze(1).broadcast_to([P, m, HEADS]), ALU.mult))
                steps.wait()
                dve.wait_ge(qkv_ready, n * 3 + 3)
                vs = v[:, bass.ds(side * POS, m), :].rearrange("p m (h d) -> p m h d", h=HEADS)
                steps.mark(dve.tensor_tensor(prod[:, 0:m, :].rearrange("p m (h d) -> p m h d", h=HEADS), vs,
                                             e[:, 0:m, :].unsqueeze(3).broadcast_to([P, m, HEADS, HD]), ALU.mult))
                steps.wait()
                dve.tensor_reduce(ao[:, l % Q_RING, :], prod[:, 0:m, :].rearrange("p m c -> p c m"), AX.X, ALU.add)\
                    .then_inc(ao_ready, 1)

            PER_COMBINE = 3
            PER_TURN = POS * 10
            first_combined = [HEAD_START + more for more in (0, 1, 2, 3, 5, 7, 9, 10)] + [2 * POS]

            def chunk(ch, which):
                side = ch % 2
                ahead = PER_COMBINE * (HEAD_START if which == "first" else POS)
                steps = Steps(dve, steps_sem, ch * PER_TURN + ahead)
                if which == "":
                    slots(ch + 1, False)
                for l in range(POS):
                    n = ch * POS + l
                    scores(n, l, side, which == "first" and l == 0, steps)
                    if not (which == "first" and l < LAG):
                        take_output(n - LAG, tile(ch, l - LAG) if l >= LAG else tile(ch - 1, l + POS - LAG), l - LAG)
                    if which == "first":
                        for m in range(first_combined[l], first_combined[l + 1]):
                            combine(m // POS, m % POS, steps)
                            if m == POS - 1:
                                slots(1, False)
                    elif which == "":
                        combine(ch + 1, l, steps)
                    average(n, l, side, steps)
                if which != "last":
                    assert steps.n == PER_TURN + PER_COMBINE * POS - ahead, steps.n

            dve.wait_ge(set_up, 2)
            slots(0, True)
            steps = Steps(dve, steps_sem)
            for l in range(HEAD_START):
                combine(0, l, steps)
            chunks(dve, chunk)
            for l in range(POS - LAG, POS):
                take_output((CHUNKS - 1) * POS + l, tile(CHUNKS - 1, l), l)


E2 = 64
TOP2 = 6
SETS = 8
TOP_SETS = 4
PER_SET = E2 // SETS
H2 = 192
HH2 = H2 // 2
ROUTE_SCALE = 2.5
CAP = 2 * (512 * TOP2 // E2)
SLOTS2 = E2 * CAP
ROWS2 = TOKENS + CAP
XC = C + E2
FAR = 3.0e38
NO_SLOT = 1.0e6
RING = 4
ROWS_RING = 2 * RING
AHEAD = 4


def second_ffn_shared(nc, X, ident, ones, gate_w, bias, ws_gate, ws_up, ws_down, w_gate, w_up, w_down,
                      wg_ring, wu_ring, wd_ring, ring_loaded, xs, table, out):
    with ExitStack() as ctx:
        sb = lambda name, shape, dt=F32: ctx.enter_context(nc.sbuf_tensor(name, shape, dt))
        sem = lambda name: ctx.enter_context(nc.semaphore(name))
        ps = lambda name, shape: ctx.enter_context(nc.psum_tensor(name, shape, F32))

        w_g = sb("e_wg", [P, CC, H2])
        w_u = sb("e_wu", [P, CC, H2])
        w_d = sb("e_wd", [P, 2, C])
        w_route = sb("e_wroute", [P, CC, E2])
        bias_all = sb("e_bias", [P, E2])
        eps = sb("e_eps", [P, 1])
        carrier = sb("e_carrier", [P, 12])
        empty = sb("e_empty", [E2, CAP], U32)
        zrow = sb("e_zrow", [CAP, XC])
        set_iota = sb("e_set_iota", [P, SETS])
        expert_iota = sb("e_expert_iota", [P, E2])
        region = sb("e_region", [P, E2])
        token_id = sb("e_token_id", [P, TILES])
        stats = sb("e_stats", [P, GROUP, 6])
        mean_var = sb("e_mean_var", [P, GROUP, 2])
        std = sb("e_std", [P, GROUP])
        rstd = sb("e_rstd", [P, GROUP])
        y = sb("e_y", [P, GROUP, C])
        xn = sb("e_xn", [P, GROUP, C])
        weight_rows = sb("e_weight_rows", [P, GROUP, E2])
        xnT = sb("e_xnT", [P, CC, GROUP * P])
        hT = sb("e_hT", [P, 2, GROUP * P])
        sil = sb("e_sil", [P, 2, GROUP * P])
        score = sb("e_score", [P, GROUP, E2])
        biased = sb("e_biased", [P, GROUP, E2])
        set_best = sb("e_set_best", [P, GROUP, SETS, 8])
        set_score = sb("e_set_score", [P, GROUP, SETS])
        set_order = sb("e_set_order", [P, GROUP, 8])
        set_index = sb("e_set_index", [P, GROUP, 8], U32)
        set_index_f = sb("e_set_index_f", [P, GROUP, TOP_SETS])
        set_onehot = sb("e_set_onehot", [P, GROUP, TOP_SETS, SETS])
        set_kept = sb("e_set_kept", [P, GROUP, SETS])
        set_far = sb("e_set_far", [P, GROUP, SETS])
        best = sb("e_best", [P, GROUP, 8])
        best_i = sb("e_best_i", [P, GROUP, 8], U32)
        best_f = sb("e_best_f", [P, GROUP, TOP2])
        onehot = sb("e_onehot", [P, GROUP, TOP2, E2])
        chosen = sb("e_chosen", [P, GROUP, E2])
        weight = sb("e_weight", [P, GROUP, E2])
        weight_sum = sb("e_weight_sum", [P, GROUP])
        total = sb("e_total", [P, E2])
        place = sb("e_place", [P, GROUP, E2])
        fits = sb("e_fits", [P, GROUP, E2])
        slot_top = sb("e_slot_top", [P, GROUP, 8])
        slot_none = sb("e_slot_none", [P, GROUP, 8])
        slot_now = sb("e_slot_now", [P, GROUP, 8], U32)
        token_now = sb("e_token_now", [P, GROUP], U32)

        up = ps("e_up", [P, 2, 2, GROUP * P])
        pj = ps("e_pj", [P, 2, C])
        lg = ps("e_lg", [P, GROUP, E2])
        cnt = ps("e_cnt", [P, GROUP + 1, E2])

        w_loaded = sem("e_w_loaded")
        set_up = sem("e_set_up")
        rows_set = sem("e_rows_set")
        var_ready = sem("e_var_ready")
        std_ready = sem("e_std_ready")
        xn_ready = sem("e_xn_ready")
        xn_stored = sem("e_xn_stored")
        weight_stored = sem("e_weight_stored")
        x_final = sem("e_x_final")
        x_stored = sem("e_x_stored")
        pj_full = sem("e_pj_full")
        pj_taken = [sem("e_pj_taken0"), sem("e_pj_taken1")]
        lg_full = sem("e_lg_full")
        score_ready = sem("e_score_ready")
        chosen_ready = sem("e_chosen_ready")
        weight_ready = sem("e_weight_ready")
        cnt_full = sem("e_cnt_full")
        up_full = sem("e_up_full")
        sil_ready = sem("e_sil_ready")
        h_ready = sem("e_h_ready")
        slots_ready = sem("e_slots_ready")
        scattered = sem("e_scattered")
        steps_sem = sem("e_steps")
        carried = sem("e_carried")
        SET_UP = 9
        HP = (P, H2 - P)

        block = ctx.enter_context(nc.Block())

        @block.sync
        def _(sp):
            sp.dma_start(w_route[:], gate_w.rearrange("(c p) e -> p c e", p=P)).then_inc(w_loaded, 16)
            sp.dma_start(bias_all[:], bias.unsqueeze(0).broadcast_to([P, E2])).then_inc(w_loaded, 16)
            for dst, src in ((w_g, ws_gate), (w_u, ws_up)):
                sp.dma_start(dst[:], src.rearrange("(c p) o -> p c o", p=P)).then_inc(w_loaded, 16)
            for f in range(2):
                sp.dma_start(w_d[0:HP[f], f, :], ws_down[P * f:P * f + HP[f], :]).then_inc(w_loaded, 16)
            sp.wait_ge(set_up, SET_UP)
            sp.dma_start(table.rearrange("(e s) one -> e (s one)", e=E2), empty[:]).then_inc(rows_set, 16)
            sp.dma_start(xs[TOKENS:ROWS2, :], zrow[:]).then_inc(rows_set, 16)
            sp.dma_start(out[TOKENS:ROWS2, :], zrow[:, 0:C]).then_inc(rows_set, 16)
            for e in range(RING):
                for dst, src, n in ((wg_ring[:, e, :, :], w_gate, CC), (wu_ring[:, e, :, :], w_up, CC),
                                    (wd_ring[:, e, :, :], w_down, 2)):
                    sp.dma_start(dst, src[e].rearrange("(p c) f -> p c f", c=n)).then_inc(ring_loaded[e], 16)
            def store_xn(g):
                sp.wait_ge(xn_ready, g + 1)
                sp.dma_start(group_rows(xs[0:TOKENS, 0:C], g), xn[:]).then_inc(xn_stored, 16)

            store_xn(0)
            for g in range(GROUPS):
                if g + 1 < GROUPS:
                    store_xn(g + 1)
                sp.wait_ge(weight_ready, g + 1)
                sp.dma_start(group_rows(xs[0:TOKENS, C:XC], g), weight_rows[:]).then_inc(weight_stored, 16)
                sp.wait_ge(x_final, g + 1)
                sp.dma_start(group_rows(out[0:TOKENS, :], g), X[:, GROUP * g:GROUP * (g + 1), :])\
                    .then_inc(x_stored, 16)
            sp.wait_ge(xn_stored, 16 * GROUPS)
            sp.wait_ge(weight_stored, 16 * GROUPS)
            sp.wait_ge(x_stored, 16 * GROUPS)
            sp.wait_ge(rows_set, 48)

        @block.gpsimd
        def _(pool):
            iota = lambda out, pattern, base, m: nc.gpsimd.iota(
                out, pattern, base=base, channel_multiplier=m,
                allow_small_or_imprecise_dtypes=True).then_inc(set_up, 1)
            nc.gpsimd.memset(eps[:], LN_EPS).then_inc(set_up, 1)
            nc.gpsimd.memset(total[:], 0.0).then_inc(set_up, 1)
            nc.gpsimd.memset(zrow[:], 0.0).then_inc(set_up, 1)
            iota(empty[:], [[1, CAP]], TOKENS, 0)
            iota(set_iota[:], [[1, SETS]], 0, 0)
            iota(expert_iota[:], [[1, E2]], 0, 0)
            iota(region[:], [[CAP, E2]], 1, 0)
            iota(token_id[:], [[P, TILES]], 0, 1)
            nc.gpsimd.memset(carrier[:], 0.0).then_inc(set_up, 1)
            pool.wait_ge(rows_set, 48)
            pool.wait_ge(set_up, SET_UP)

            def turn(g):
                pool.wait_ge(slots_ready, g + 1)
                pool.wait_ge(carried, g)
                nc.gpsimd.tensor_tensor(carrier[:, 0:1], eps[:], eps[:], ALU.add).then_inc(carried, 1)
                for i in range(GROUP):
                    for k in range(TOP2):
                        nc.gpsimd.indirect_dma_start(
                            table, bass.IndirectOffsetOnAxis(ap=slot_now[:, i, k:k + 1], axis=0),
                            token_now[:, i:i + 1], None, bounds_check=SLOTS2 - 1, oob_is_err=False)\
                            .then_inc(scattered, 16)

            turn(0)
            with pool.Fori(1, GROUPS) as g:
                turn(g)
            pool.wait_ge(scattered, 16 * GROUPS * GROUP * TOP2)

        PJ = 8

        @block.tensor
        def _(pe):
            def bank_free(u, g):
                pe.wait_ge(pj_taken[u % 2], g * (PJ // 2) + 2 + u // 2)

            def transposes(g, first):
                pe.wait_ge(xn_ready, g + 1)
                for c in range(CC):
                    if not first:
                        bank_free(c, g - 1)
                    elif c >= 2:
                        pe.wait_ge(pj_taken[c % 2], 1)
                    for i in range(GROUP):
                        ins = pe.transpose(pj[:, c % 2, P * i:P * (i + 1)], xn[:, i, P * c:P * (c + 1)], ident[:])
                    ins.then_inc(pj_full, 1)

            def counts(g):
                pe.wait_ge(chosen_ready, g + 1)
                pe.wait_ge(slots_ready, g)
                for j in range(GROUP):
                    pe.matmul(cnt[:, j, :], ones[:, P:2 * P], chosen[:, j, :], start=(j == 0), stop=True,
                              skip_group_check=True)
                    ins = pe.matmul(cnt[:, j + 1:, :], ones[:, 0:P],
                                    chosen[:, j:j + 1, :].broadcast_to([P, GROUP - j, E2]),
                                    start=(j == 0), stop=(j == GROUP - 1), skip_group_check=True)
                ins.then_inc(cnt_full, 1)

            def group(g, last):
                for k in range(2):
                    pe.wait_ge(pj_taken[k], g * (PJ // 2) + 2)
                for i in range(GROUP):
                    for c in range(CC):
                        ins = pe.matmul(lg[:, i, :], xnT[:, c, P * i:P * (i + 1)], w_route[:, c, :],
                                        start=(c == 0), stop=(c == CC - 1))
                ins.then_inc(lg_full, 1)
                for f in range(2):
                    pe.wait_ge(h_ready, g * 2)
                    for k, w in ((0, w_g), (1, w_u)):
                        for c in range(CC):
                            ins = pe.matmul(up[0:HP[f], f, k, :], w[:, c, P * f:P * f + HP[f]], xnT[:, c, :],
                                            start=(c == 0), stop=(c == CC - 1))
                    ins.then_inc(up_full, 1)
                if last:
                    counts(g)
                else:
                    transposes(g + 1, False)
                pe.wait_ge(h_ready, g * 2 + 2)
                for i in range(GROUP):
                    bank_free((0 if last else 4) + i, g)
                    for f in range(2):
                        ins = pe.matmul(pj[:, i % 2, :], hT[0:HP[f], f, P * i:P * (i + 1)], w_d[0:HP[f], f, :],
                                        start=(f == 0), stop=(f == 1))
                    ins.then_inc(pj_full, 1)
                if not last:
                    counts(g)

            transposes(0, True)
            pe.wait_ge(w_loaded, 96)
            group(0, False)
            with pe.Fori(1, GROUPS - 1) as g:
                group(g, False)
            group(GROUPS - 1, True)

        @block.scalar
        def _(act):
            def root(g):
                act.wait_ge(var_ready, g + 1)
                nc.scalar.activation(std[:], mean_var[:, :, 1], ACT.Sqrt, bias=eps[:]).then_inc(std_ready, 1)

            def take_xnT(c, n):
                act.wait_ge(pj_full, n)
                nc.scalar.copy(xnT[:, c, :], pj[:, c % 2, :]).then_inc(pj_taken[c % 2], 1)

            def group(g, start, last):
                if not last:
                    root(g + 1)
                act.wait_ge(lg_full, g + 1)
                if not start:
                    act.wait_ge(weight_ready, g)
                nc.scalar.activation(score[:], lg[:], ACT.Sigmoid).then_inc(score_ready, 1)
                for f in range(2):
                    act.wait_ge(up_full, g * 2 + f + 1)
                    nc.scalar.activation(sil[0:HP[f], f, :], up[0:HP[f], f, 0, :], ACT.Silu).then_inc(sil_ready, 1)
                if not last:
                    for c in range(CC):
                        take_xnT(c, g * PJ + 4 + c + 1)
                if not start:
                    act.wait_ge(x_final, g)
                for i in range(GROUP):
                    act.wait_ge(pj_full, g * PJ + 4 + (0 if last else 4) + i + 1)
                    nc.scalar.copy(y[:, i, :], pj[:, i % 2, :]).then_inc(pj_taken[i % 2], 1)

            act.wait_ge(set_up, SET_UP)
            root(0)
            for c in range(CC):
                take_xnT(c, c + 1)
            group(0, True, False)
            with act.Fori(1, GROUPS - 1) as g:
                group(g, False, False)
            group(GROUPS - 1, False, True)

        @block.vector
        def _(dve):
            G3 = [P, GROUP, E2]

            def carry(column):
                dve.tensor_copy(carrier[:, column:column + 1], eps[:])

            def statistics(g, steps):
                layernorm_tiles(dve, steps, lambda i: tile_row(X, g * GROUP + i), stats, mean_var, GROUP,
                                carrier[:, 4:5], eps[:]).then_inc(var_ready, 1)

            def normalise(g, steps, first):
                dve.wait_ge(std_ready, g + 1)
                steps.mark(dve.reciprocal(rstd[:], std[:]))
                steps.wait()
                if not first:
                    dve.wait_ge(xn_stored, g * 16)
                for i in range(GROUP):
                    ins = dve.tensor_scalar(xn[:, i, :], tile_row(X, g * GROUP + i),
                                            mean_var[:, i, 0:1], rstd[:, i:i + 1], ALU.subtract, ALU.mult)
                ins.then_inc(xn_ready, 1)

            def hidden(g):
                for f in range(2):
                    dve.wait_ge(sil_ready, g * 2 + f + 1)
                    dve.tensor_tensor(hT[0:HP[f], f, :], sil[0:HP[f], f, :], up[0:HP[f], f, 1, :], ALU.mult)\
                        .then_inc(h_ready, 1)

            def choose_sets(g, steps):
                dve.wait_ge(score_ready, g + 1)
                steps.mark(dve.tensor_tensor(biased[:], score[:], bias_all[:].unsqueeze(1).broadcast_to(G3), ALU.add))
                steps.wait()
                carry(5)
                for i in range(GROUP):
                    for t in range(SETS):
                        ins = dve.max(set_best[:, i, t, :], biased[:, i, PER_SET * t:PER_SET * (t + 1)])
                steps.mark(ins)
                steps.wait()
                steps.mark(dve.tensor_tensor(set_score[:], set_best[:, :, :, 0], set_best[:, :, :, 1], ALU.add))
                steps.wait()
                carry(6)
                for i in range(GROUP):
                    ins = dve.max(set_order[:, i, :], set_score[:, i, :])
                steps.mark(ins)
                steps.wait()
                carry(7)
                for i in range(GROUP):
                    ins = dve.max_index(set_index[:, i, :], set_order[:, i, :], set_score[:, i, :])
                steps.mark(ins)
                steps.wait()
                steps.mark(dve.tensor_copy(set_index_f[:], set_index[:, :, 0:TOP_SETS]))
                steps.wait()
                shape = [P, GROUP, TOP_SETS, SETS]
                steps.mark(dve.tensor_tensor(set_onehot[:], set_iota[:].unsqueeze(1).unsqueeze(1).broadcast_to(shape),
                                             set_index_f[:].unsqueeze(3).broadcast_to(shape), ALU.is_equal))
                steps.wait()
                steps.mark(dve.tensor_reduce(set_kept[:], set_onehot[:].rearrange("p i k s -> p i s k"), AX.X, ALU.add))
                steps.wait()
                steps.mark(dve.tensor_scalar(set_far[:], set_kept[:], 1.0, FAR, ALU.subtract, ALU.mult))
                by_set = biased[:].rearrange("p i (s e) -> p i s e", s=SETS)
                shape = [P, GROUP, SETS, PER_SET]
                steps.mark(dve.tensor_tensor(by_set, by_set, set_kept[:].unsqueeze(3).broadcast_to(shape), ALU.mult))
                steps.wait()
                steps.mark(dve.tensor_tensor(by_set, by_set, set_far[:].unsqueeze(3).broadcast_to(shape), ALU.add))
                steps.wait()

            def choose(g, steps):
                carry(8)
                for i in range(GROUP):
                    ins = dve.max(best[:, i, :], biased[:, i, :])
                steps.mark(ins)
                steps.wait()
                carry(9)
                for i in range(GROUP):
                    ins = dve.max_index(best_i[:, i, :], best[:, i, :], biased[:, i, :])
                steps.mark(ins)
                steps.wait()
                steps.mark(dve.tensor_copy(best_f[:], best_i[:, :, 0:TOP2]))
                steps.wait()
                shape = [P, GROUP, TOP2, E2]
                steps.mark(dve.tensor_tensor(onehot[:], expert_iota[:].unsqueeze(1).unsqueeze(1).broadcast_to(shape),
                                             best_f[:].unsqueeze(3).broadcast_to(shape), ALU.is_equal))
                steps.wait()
                dve.tensor_reduce(chosen[:], onehot[:].rearrange("p i k e -> p i e k"), AX.X, ALU.add)\
                    .then_inc(chosen_ready, 1)
                dve.wait_ge(chosen_ready, g + 1)
                steps.mark(dve.tensor_tensor(weight[:], chosen[:], score[:], ALU.mult))
                steps.wait()
                steps.mark(dve.tensor_reduce(weight_sum[:], weight[:], AX.X, ALU.add))
                steps.wait()
                steps.mark(dve.reciprocal(weight_sum[:], weight_sum[:]))
                steps.wait()
                dve.wait_ge(weight_stored, g * 16)
                dve.scalar_tensor_tensor(out=weight_rows[:], in0=weight[:], scalar=ROUTE_SCALE,
                                         in1=weight_sum[:].unsqueeze(2).broadcast_to(G3), op0=ALU.mult, op1=ALU.mult)\
                    .then_inc(weight_ready, 1)

            def place_slots(g, steps):
                dve.wait_ge(cnt_full, g + 1)
                steps.mark(dve.tensor_tensor(place[:], cnt[:, 0:GROUP, :], total[:].unsqueeze(1).broadcast_to(G3),
                                             ALU.add))
                steps.wait()
                steps.mark(dve.tensor_tensor(total[:], total[:], cnt[:, GROUP, :], ALU.add))
                steps.mark(dve.scalar_tensor_tensor(out=fits[:], in0=place[:], scalar=float(CAP), in1=chosen[:],
                                                    op0=ALU.is_lt, op1=ALU.mult))
                steps.wait()
                steps.mark(dve.tensor_tensor(place[:], place[:], region[:].unsqueeze(1).broadcast_to(G3), ALU.add))
                steps.wait()
                steps.mark(dve.tensor_tensor(place[:], place[:], fits[:], ALU.mult))
                steps.wait()
                carry(10)
                for i in range(GROUP):
                    ins = dve.max(slot_top[:, i, :], place[:, i, :])
                steps.mark(ins)
                steps.wait()
                steps.mark(dve.tensor_scalar(slot_none[:], slot_top[:], 0.0, NO_SLOT, ALU.is_equal, ALU.mult))
                steps.wait()
                steps.mark(dve.scalar_tensor_tensor(out=slot_top[:], in0=slot_top[:], scalar=1.0, in1=slot_none[:],
                                                    op0=ALU.subtract, op1=ALU.add))
                steps.wait()
                dve.wait_ge(scattered, g * (16 * GROUP * TOP2))
                dve.tensor_scalar(token_now[:], token_id[:, bass.ds(g * GROUP, GROUP)], 0.0, None, ALU.add)
                dve.tensor_copy(slot_now[:], slot_top[:]).then_inc(slots_ready, 1)

            PER_TURN = 1 + 1 + 10 + 1 + 7 + 8

            def group(g, last):
                steps = Steps(dve, steps_sem, g * PER_TURN + 2)
                if not last:
                    statistics(g + 1, steps)
                    normalise(g + 1, steps, False)
                choose_sets(g, steps)
                hidden(g)
                choose(g, steps)
                place_slots(g, steps)
                for k in range(2):
                    dve.wait_ge(pj_taken[k], g * (PJ // 2) + (4 if last else 6))
                x = X[:, bass.ds(g * GROUP, GROUP), :]
                dve.tensor_tensor(x, x, y[:], ALU.add).then_inc(x_final, 1)
                assert steps.n == PER_TURN - (2 if last else 0), steps.n

            dve.wait_ge(set_up, SET_UP)
            dve.wait_ge(w_loaded, 96)
            steps = Steps(dve, steps_sem)
            statistics(0, steps)
            normalise(0, steps, True)
            group(0, False)
            with dve.Fori(1, GROUPS - 1) as g:
                group(g, False)
            group(GROUPS - 1, True)


def second_ffn_experts(nc, ident, w_gate, w_up, w_down, wg_ring, wu_ring, wd_ring, ring_loaded, xs, table, out):
    with ExitStack() as ctx:
        sb = lambda name, shape, dt=F32: ctx.enter_context(nc.sbuf_tensor(name, shape, dt))
        sem = lambda name: ctx.enter_context(nc.semaphore(name))
        ps = lambda name, shape: ctx.enter_context(nc.psum_tensor(name, shape, F32))

        ids_rows = sb("f_ids_rows", [E2, CAP], U32)
        ids_rows_f = sb("f_ids_rows_f", [E2, CAP])
        ids_f = sb("f_ids_f", [CAP, E2])
        ids = sb("f_ids", [CAP, ROWS_RING, 1], U32)
        xg = sb("f_xg", [CAP, ROWS_RING, XC])
        xgT = sb("f_xgT", [P, 2, CC * CAP])
        sil = sb("f_sil", [CAP, 2, H2])
        h = sb("f_h", [CAP, 2, H2])
        hT = sb("f_hT", [HH2, 2, 2 * CAP])
        y = sb("f_y", [CAP, RING, C])
        carrier = sb("f_carrier", [P, 2])

        up = ps("f_up", [CAP, 2, 512])
        yp = ps("f_yp", [CAP, 2, C])
        xp = ps("f_xp", [P, 2, 512])
        hp = ps("f_hp", [HH2, 2, 512])

        ids_loaded = sem("f_ids_loaded")
        ids_float = sem("f_ids_float")
        ids_turned = sem("f_ids_turned")
        ids_steps = sem("f_ids_steps")
        ids_ready = sem("f_ids_ready")
        gathered = [sem(f"f_gathered{r}") for r in range(ROWS_RING)]
        added = sem("f_added")
        x_turned = sem("f_x_turned")
        xgT_ready = sem("f_xgT_ready")
        up_full = sem("f_up_full")
        sil_ready = sem("f_sil_ready")
        h_ready = sem("f_h_ready")
        h_turned = sem("f_h_turned")
        hT_ready = sem("f_hT_ready")
        y_full = sem("f_y_full")
        y_ready = sem("f_y_ready")
        carried = sem("f_carried")
        TURNS = E2 // ROWS_RING

        def turns(eng, expert):
            for r in range(ROWS_RING):
                expert(r, r, 0, "first")
            with eng.Fori(1, TURNS - 1) as t:
                for r in range(ROWS_RING):
                    expert(t * ROWS_RING + r, r, t, "")
            for r in range(ROWS_RING):
                expert((TURNS - 1) * ROWS_RING + r, r, TURNS - 1, "last")

        block = ctx.enter_context(nc.Block())

        @block.sync
        def _(sp):
            sp.dma_start(ids_rows[:], table.rearrange("(e s) one -> e (s one)", e=E2)).then_inc(ids_loaded, 16)

        @block.gpsimd
        def _(pool):
            def gather(e, r, n):
                pool.wait_ge(ids_ready, e + 1)
                pool.wait_ge(carried, n)
                nc.gpsimd.tensor_tensor(carrier[:, 0:1], ident[:, 0:1], ident[:, 0:1], ALU.add).then_inc(carried, 1)
                nc.gpsimd.indirect_dma_start(xg[:, r, :], None, xs, bass.IndirectOffsetOnAxis(
                    ap=ids[:, r, :], axis=0)).then_inc(gathered[r], 16)

            def add(e, r, n):
                pool.wait_ge(y_ready, e + 1)
                pool.wait_ge(added, e * 16)
                pool.wait_ge(carried, n)
                nc.gpsimd.tensor_tensor(carrier[:, 0:1], ident[:, 0:1], ident[:, 0:1], ALU.add).then_inc(carried, 1)
                nc.gpsimd.indirect_dma_start(out, bass.IndirectOffsetOnAxis(ap=ids[:, r, :], axis=0),
                                             y[:, r % RING, :], None, compute_op=ALU.add).then_inc(added, 16)

            def expert(e, r, t, which):
                if not (which == "last" and r >= ROWS_RING - AHEAD):
                    gather(e + AHEAD, (r + AHEAD) % ROWS_RING, e * 2 + AHEAD)
                    add(e, r, e * 2 + AHEAD + 1)
                else:
                    add(e, r, E2 + e)

            for e in range(AHEAD):
                gather(e, e, e)
            turns(pool, expert)
            pool.wait_ge(added, 16 * E2)

        @block.tensor
        def _(pe):
            def turn_x(e, r, t, start):
                pe.wait_ge(gathered[r], t * 16 + 16)
                if not start:
                    pe.wait_ge(xgT_ready, e - 1)
                rows = xg[:, r, 0:C].rearrange("s (p c) -> s c p", c=CC)
                for c in range(CC):
                    ins = pe.transpose(xp[:, r % 2, CAP * c:CAP * (c + 1)], rows[:, c, :], ident[0:CAP, 0:CAP])
                ins.then_inc(x_turned, 1)

            def turn_h(e, r, start):
                pe.wait_ge(h_ready, e + 1)
                if not start:
                    pe.wait_ge(hT_ready, e - 1)
                halves = h[:, r % 2, :].rearrange("s (p c) -> s c p", c=2)
                for f in range(2):
                    ins = pe.transpose(hp[:, r % 2, CAP * f:CAP * (f + 1)], halves[:, f, :], ident[0:CAP, 0:CAP])
                ins.then_inc(h_turned, 1)

            def down(e, r, start):
                pe.wait_ge(hT_ready, e + 1)
                if not start:
                    pe.wait_ge(y_ready, e - 1)
                for f in range(2):
                    ins = pe.matmul(yp[:, r % 2, :], hT[:, r % 2, CAP * f:CAP * (f + 1)], wd_ring[:, r % RING, f, :],
                                    start=(f == 0), stop=(f == 1))
                ins.then_inc(y_full, 1)

            def expert(e, r, t, which):
                first = which == "first" and r == 0
                pe.wait_ge(ring_loaded[r % RING], (t * 2 + r // RING) * 48 + 48)
                pe.wait_ge(xgT_ready, e + 1)
                if not (which == "first" and r < 2):
                    pe.wait_ge(h_ready, e - 1)
                for k, w in ((0, wg_ring), (1, wu_ring)):
                    for c in range(CC):
                        ins = pe.matmul(up[:, r % 2, H2 * k:H2 * (k + 1)], xgT[:, r % 2, CAP * c:CAP * (c + 1)],
                                        w[:, r % RING, c, :], start=(c == 0), stop=(c == CC - 1))
                    if k == 0 and not first:
                        turn_h(e - 1, (r - 1) % ROWS_RING, which == "first" and r < 3)
                ins.then_inc(up_full, 1)
                if not (which == "last" and r == ROWS_RING - 1):
                    turn_x(e + 1, (r + 1) % ROWS_RING, t + (r + 1) // ROWS_RING, first)
                if not first:
                    down(e - 1, (r - 1) % ROWS_RING, which == "first" and r < 3)

            pe.wait_ge(ids_float, 1)
            pe.transpose(hp[:, 0, 0:E2], ids_rows_f[:], ident[0:E2, 0:E2]).then_inc(ids_turned, 1)
            turn_x(0, 0, 0, True)
            turns(pe, expert)
            turn_h(E2 - 1, ROWS_RING - 1, False)
            down(E2 - 1, ROWS_RING - 1, False)

        @block.scalar
        def _(act):
            def load(e, r):
                act.wait_ge(y_full, e - (RING - 1))
                for dst, src, n in ((wg_ring[:, r, :, :], w_gate, CC), (wu_ring[:, r, :, :], w_up, CC),
                                    (wd_ring[:, r, :, :], w_down, 2)):
                    act.dma_start(dst, src[bass.ds(e, 1)].rearrange("a (p c) f -> p (a c) f", c=n))\
                        .then_inc(ring_loaded[r], 16)

            def take_x(e, r, start):
                act.wait_ge(x_turned, e + 1)
                if not start:
                    act.wait_ge(up_full, e - 1)
                nc.scalar.copy(xgT[:, r % 2, :], xp[:, r % 2, 0:CC * CAP]).then_inc(xgT_ready, 1)

            def expert(e, r, t, which):
                act.wait_ge(up_full, e + 1)
                if not (which == "first" and r < 2):
                    act.wait_ge(h_ready, e - 1)
                nc.scalar.activation(sil[:, r % 2, :], up[:, r % 2, 0:H2], ACT.Silu).then_inc(sil_ready, 1)
                if not (which == "last" and r == ROWS_RING - 1):
                    take_x(e + 1, (r + 1) % ROWS_RING, which == "first" and r < 1)
                if not (which == "first" and r < 2) and not (which == "last" and r >= ROWS_RING - RING + 2):
                    load(e + RING - 2, (r - 2) % RING)

            take_x(0, 0, True)
            turns(act, expert)

        @block.vector
        def _(dve):
            def pick_ids(e, r, start):
                if not start:
                    dve.wait_ge(added, (e - ROWS_RING + 1) * 16)
                dve.tensor_scalar(ids[:, r, :], ids_f[:, bass.ds(e, 1)], 0.0, None, ALU.add).then_inc(ids_ready, 1)

            def take_h(e, r, start):
                dve.wait_ge(h_turned, e + 1)
                if not start:
                    dve.wait_ge(y_full, e - 1)
                dve.tensor_copy(hT[:, r % 2, :], hp[:, r % 2, 0:2 * CAP]).then_inc(hT_ready, 1)

            def take_y(e, r, start):
                dve.wait_ge(y_full, e + 1)
                if not start:
                    dve.wait_ge(added, (e - RING + 1) * 16)
                weight = xg[:, r, bass.ds(e + C, 1)]
                dve.tensor_scalar(y[:, r % RING, :], yp[:, r % 2, :], weight, None, ALU.mult).then_inc(y_ready, 1)

            def expert(e, r, t, which):
                first = which == "first" and r == 0
                if not first:
                    take_h(e - 1, (r - 1) % ROWS_RING, which == "first" and r < 3)
                dve.wait_ge(sil_ready, e + 1)
                if not (which == "first" and r < 2):
                    dve.wait_ge(h_turned, e - 1)
                dve.tensor_tensor(h[:, r % 2, :], sil[:, r % 2, :], up[:, r % 2, H2:2 * H2], ALU.mult)\
                    .then_inc(h_ready, 1)
                if not first:
                    take_y(e - 1, (r - 1) % ROWS_RING, which == "first" and r <= RING)
                if not (which == "last" and r >= ROWS_RING - AHEAD - 1):
                    pick_ids(e + AHEAD + 1, (r + AHEAD + 1) % ROWS_RING, which == "first" and r < ROWS_RING - AHEAD - 1)

            dve.wait_ge(ids_loaded, 16)
            dve.tensor_copy(ids_rows_f[:], ids_rows[:]).then_inc(ids_float, 1)
            dve.wait_ge(ids_turned, 1)
            dve.tensor_copy(ids_f[:], hp[:, 0, 0:E2]).then_inc(ids_steps, 1)
            dve.wait_ge(ids_steps, 1)
            for e in range(AHEAD + 1):
                pick_ids(e, e, True)
            turns(dve, expert)
            take_h(E2 - 1, ROWS_RING - 1, False)
            take_y(E2 - 1, ROWS_RING - 1, False)


def program(nc, x, wq, wk, wv, wo, route1, w_gate1, w_up1, w_down1, sh_gate, sh_up, sh_down, w_qkv, w_out,
            route2, bias2, w_gate2, w_up2, w_down2, ws_gate, ws_up, ws_down, out):
    rows_1 = nc.dram_tensor("rows_1", [ROWS, C], F32).ap()
    table_1 = nc.dram_tensor("table_1", [SLOTS1, 1], U32).ap()
    expert_rows = nc.dram_tensor("expert_rows", [2 * PAIRS1 * P, C], F32).ap()
    rows_2 = nc.dram_tensor("rows_2", [ROWS2, XC], F32).ap()
    table_2 = nc.dram_tensor("table_2", [SLOTS2, 1], U32).ap()

    with ExitStack() as ctx:
        ident = ctx.enter_context(nc.sbuf_tensor("ident", [P, P], F32))
        ones = ctx.enter_context(nc.sbuf_tensor("ones", [P, 2 * P], F32))
        constants(nc, ctx, ident, ones)
        with ExitStack() as rows_ctx:
            X = rows_ctx.enter_context(nc.sbuf_tensor("X", [P, TILES, C], F32))
            first_attention(nc, x, wq, wk, wv, wo, X, ident, ones)
            with ExitStack() as routed:
                sb = lambda name, shape, dt=F32: routed.enter_context(nc.sbuf_tensor(name, shape, dt))
                weight_all = sb("weight_all", [P, TILES, TOP1])
                slot_all = sb("slot_all", [P, TILES, TOP1], U32)
                w_p = sb("w_p", [P, CC, 3 * C])
                qkv_loaded = routed.enter_context(nc.semaphore("qkv_loaded"))
                with ExitStack() as weights:
                    sb = lambda name, shape, dt=F32: weights.enter_context(nc.sbuf_tensor(name, shape, dt))
                    tile_expert = sb("tile_expert", [P, 2 * PAIRS1], I32)
                    tile_slot = sb("tile_slot", [P, 2 * PAIRS1], I32)
                    w13 = sb("w13", [P, CC * E1, 2 * H1])
                    w13_loaded = weights.enter_context(nc.semaphore("w13_loaded"))
                    first_ffn_shared(nc, X, ident, ones, w13_loaded, route1, sh_gate, sh_up, sh_down, w_gate1, w_up1,
                                     w13, rows_1, table_1, weight_all, slot_all, tile_expert, tile_slot, w_p)
                    w2 = sb("w2", [P, HC1 * E1, C])
                    first_ffn_experts(nc, ident, w13, w13_loaded, w2, w_down1, rows_1, table_1, expert_rows,
                                      tile_expert, tile_slot, w_qkv, w_p, qkv_loaded)
                second_attention(nc, X, ident, ones, expert_rows, slot_all, weight_all, w_out, w_p, qkv_loaded)
            wg_ring = rows_ctx.enter_context(nc.sbuf_tensor("wg_ring", [P, RING, CC, H2], F32))
            wu_ring = rows_ctx.enter_context(nc.sbuf_tensor("wu_ring", [P, RING, CC, H2], F32))
            wd_ring = rows_ctx.enter_context(nc.sbuf_tensor("wd_ring", [HH2, RING, 2, C], F32))
            ring_loaded = [rows_ctx.enter_context(nc.semaphore(f"ring_loaded{r}")) for r in range(RING)]
            second_ffn_shared(nc, X, ident, ones, route2, bias2, ws_gate, ws_up, ws_down, w_gate2, w_up2, w_down2,
                              wg_ring, wu_ring, wd_ring, ring_loaded, rows_2, table_2, out)
            second_ffn_experts(nc, ident, w_gate2, w_up2, w_down2, wg_ring, wu_ring, wd_ring, ring_loaded, rows_2,
                               table_2, out)


def kernel(**inputs):
    import numpy as _np
    import concourse.bacc as _bacc
    from concourse import mybir as _mybir
    from concourse.bass_utils import run_bass_kernel_spmd as _run

    a = {name: _np.asarray(value) for name, value in inputs.items()}
    turned = lambda w: _np.swapaxes(w, -1, -2)
    laid_out = {
        "x": a["L0_attn_x"].reshape(TOKENS, C),
        "wq": turned(a["L0_attn_Wq"]), "wk": turned(a["L0_attn_Wk"]), "wv": turned(a["L0_attn_Wv"]),
        "wo": turned(a["L0_attn_Wo"]),
        "route1": turned(_np.concatenate([a["L0_ffn_gate_w"], a["L0_ffn_se_gate_w"]], axis=0)),
        "w_gate1": turned(a["L0_ffn_w_gate"]), "w_up1": turned(a["L0_ffn_w_up"]), "w_down1": turned(a["L0_ffn_w_down"]),
        "sh_gate": turned(a["L0_ffn_sh_gate"]), "sh_up": turned(a["L0_ffn_sh_up"]),
        "sh_down": turned(a["L0_ffn_sh_down"]),
        "w_qkv": turned(a["L1_attn_weight_qkv"]), "w_out": turned(a["L1_attn_weight_out"]),
        "route2": a["L1_ffn_gate_w"], "bias2": a["L1_ffn_bias"],
        "w_gate2": a["L1_ffn_w_gate"], "w_up2": a["L1_ffn_w_up"], "w_down2": a["L1_ffn_w_down"],
        "ws_gate": a["L1_ffn_ws_gate"], "ws_up": a["L1_ffn_ws_up"], "ws_down": a["L1_ffn_ws_down"],
    }
    nc = _bacc.Bacc("TRN2", target_bir_lowering=False, num_devices=1)
    arrays, args = {}, []
    for name, value in laid_out.items():
        value = _np.ascontiguousarray(value)
        arrays[f"in_{name}_dram"] = value
        args.append(nc.dram_tensor(f"in_{name}_dram", value.shape, _mybir.dt.from_np(value.dtype),
                                   kind="ExternalInput").ap())
    out = nc.dram_tensor("out_dram", (ROWS2, C), F32, kind="ExternalOutput").ap()
    program(nc, *args, out)
    r = _run(nc, [arrays], core_ids=[0])
    return r.results[0]["out_dram"][:TOKENS].reshape(BATCHES, SEQ, C)
```
